# Optimizing a Trainium2 kernel written in Bass

```python
import numpy as np
import jax
import jax.numpy as jnp

def _softmax(x, axis=-1):
    return jax.nn.softmax(x, axis=axis)

def _gelu(x):
    return jax.nn.gelu(x, approximate=True)

def _silu(x):
    return jax.nn.silu(x)

def _sigmoid(x):
    return jax.nn.sigmoid(x)

def _layernorm(x, axis=-1, eps=1e-05):
    m = jnp.mean(x, axis=axis, keepdims=True)
    v = jnp.var(x, axis=axis, keepdims=True)
    return (x - m) / jnp.sqrt(v + eps)

def _scatter_add(tgt, idx, src, axis=0):
    return tgt.at[idx].add(src)

def _segment_sum(src, seg, n):
    return jax.ops.segment_sum(src, seg, n)
kernel_name = 'mk_lm_tower_d2_tok_ids1024_r4_94fd42'

def setup_inputs(seed: int=0):
    np.random.seed(seed)
    _w = jnp.asarray

    def _rec_inputs():
        import jax
        import jax.numpy as jnp
        _rk = jax.random.key(seed)
        x = jax.random.randint(jax.random.fold_in(_rk, 1), (8, 512), 0, 12564, jnp.int32)
        return x
    x = _rec_inputs()

    def _L0_tok_setup():
        import jax, jax.numpy as jnp
        import numpy as np
        VOCAB, HID, RANK, MAX_LEN = (50257, 256, 32, 512)
        B, S = (32, 512)
        key = jax.random.key(seed)
        k1, k2, k3, k4, k5 = jax.random.split(key, 5)
        input_ids = jax.random.randint(k1, (B, S), 0, VOCAB)
        E1 = jax.random.normal(k2, (VOCAB, RANK), dtype=jnp.float32)
        W2 = jax.random.normal(k3, (HID, RANK), dtype=jnp.float32) / np.sqrt(RANK)
        b2 = jax.random.normal(k4, (HID,), dtype=jnp.float32) * 0.01
        pos_emb = jax.random.normal(k5, (1, MAX_LEN, HID), dtype=jnp.float32)
        return {'input_ids': input_ids, 'E1': E1, 'W2': W2, 'b2': b2, 'pos_emb': pos_emb}
    _L0_tok_all = _L0_tok_setup()
    _L0_tok_in = {k: v for k, v in _L0_tok_all.items() if k in ('E1', 'W2', 'b2', 'pos_emb')}
    del _L0_tok_all

    def _L0_attn_setup():
        import jax, jax.numpy as jnp
        import numpy as np
        NUM_HEADS = 16
        D_MODEL = 256
        D_K = D_MODEL // NUM_HEADS
        MAX_SEQ_LEN = 1024
        ROPE_BASE = 10000.0
        BATCH = 2
        SEQ_LEN = 512

        def _rope_tables(seq_len, d_k, base=ROPE_BASE):
            theta = 1.0 / base ** (jnp.arange(0, d_k, 2, dtype=jnp.float32) / d_k)
            m = jnp.arange(seq_len, dtype=jnp.float32)
            m_theta = jnp.outer(m, theta)
            ang = jnp.concatenate([m_theta, m_theta], axis=-1)
            return (jnp.cos(ang), jnp.sin(ang))

        def _apply_rope(x, cos, sin):
            d2 = x.shape[-1] // 2
            x1, x2 = (x[..., :d2], x[..., d2:])
            x_flip = jnp.concatenate([-x2, x1], axis=-1)
            return x * cos + x_flip * sin
        key = jax.random.key(seed)
        kx, kq, kk, kv, ko = jax.random.split(key, 5)
        s = 1.0 / np.sqrt(D_MODEL)
        x = jax.random.normal(kx, (BATCH, SEQ_LEN, D_MODEL), dtype=jnp.float32)
        W_Q = jax.random.uniform(kq, (D_MODEL, D_MODEL), jnp.float32, -s, s)
        W_K = jax.random.uniform(kk, (D_MODEL, D_MODEL), jnp.float32, -s, s)
        W_V = jax.random.uniform(kv, (D_MODEL, D_MODEL), jnp.float32, -s, s)
        W_O = jax.random.uniform(ko, (D_MODEL, D_MODEL), jnp.float32, -s, s)
        return {'x': x, 'W_Q': W_Q, 'W_K': W_K, 'W_V': W_V, 'W_O': W_O}
    _L0_attn_all = _L0_attn_setup()
    _L0_attn_in = {k: v for k, v in _L0_attn_all.items() if k in ('W_Q', 'W_K', 'W_V', 'W_O')}
    del _L0_attn_all

    def _L0_ffn_setup():
        import jax, jax.numpy as jnp
        import numpy as np
        D_MODEL = 256
        EXPERT_DIM = 128
        N_EXPERTS = 8
        TOP_K = 2

        def _sq_relu(h):
            return jnp.square(jax.nn.relu(h))
        key = jax.random.key(seed)
        ks = jax.random.split(key, 6)
        s = 0.02
        x = jax.random.normal(ks[0], (2, 512, D_MODEL), dtype=jnp.float32)
        Ws1 = jax.random.normal(ks[1], (D_MODEL, EXPERT_DIM), dtype=jnp.float32) * s
        Ws2 = jax.random.normal(ks[2], (EXPERT_DIM, D_MODEL), dtype=jnp.float32) * s
        W1 = jax.random.normal(ks[3], (N_EXPERTS, D_MODEL, EXPERT_DIM), dtype=jnp.float32) * s
        W2 = jax.random.normal(ks[4], (N_EXPERTS, EXPERT_DIM, D_MODEL), dtype=jnp.float32) * s
        Wr = jax.random.normal(ks[5], (D_MODEL, N_EXPERTS), dtype=jnp.float32) * s
        return {'x': x, 'Ws1': Ws1, 'Ws2': Ws2, 'W1': W1, 'W2': W2, 'Wr': Wr}
    _L0_ffn_all = _L0_ffn_setup()
    _L0_ffn_in = {k: v for k, v in _L0_ffn_all.items() if k in ('Ws1', 'Ws2', 'W1', 'W2', 'Wr')}
    del _L0_ffn_all

    def _L1_attn_setup():
        import jax, jax.numpy as jnp
        import numpy as np
        import math
        N_EMBD = 256
        N_HEAD = 16
        BLOCK_SIZE = 256
        B, T = (4, 256)
        key = jax.random.key(seed)
        ks = jax.random.split(key, 7)
        C = N_EMBD
        return {'x': jax.random.normal(ks[0], (B, T, C), dtype=jnp.float32), 'Wqk': jax.random.normal(ks[1], (C, 2 * C), dtype=jnp.float32) * 0.02, 'bqk': jnp.zeros((2 * C,), dtype=jnp.float32), 'Wgate': jax.random.normal(ks[2], (C, N_HEAD), dtype=jnp.float32) * 0.02, 'bgate': jnp.zeros((N_HEAD,), dtype=jnp.float32), 'Wproj': jax.random.normal(ks[3], (C, C), dtype=jnp.float32) * 0.02, 'bproj': jnp.zeros((C,), dtype=jnp.float32)}
    _L1_attn_all = _L1_attn_setup()
    _L1_attn_in = {k: v for k, v in _L1_attn_all.items() if k in ('Wqk', 'bqk', 'Wgate', 'bgate', 'Wproj', 'bproj')}
    del _L1_attn_all

    def _L1_ffn_setup():
        import jax, jax.numpy as jnp
        import numpy as np
        D, H, E, K, S = (256, 512, 8, 2, 1)
        B, L = (4, 512)
        key = jax.random.key(seed)
        ks = jax.random.split(key, 9)
        std = 0.02
        return {'x': jax.random.normal(ks[0], (B, L, D), dtype=jnp.float32), 'router_w': jax.random.normal(ks[1], (E, D), dtype=jnp.float32) * std, 'experts_bias': jnp.zeros((E,), dtype=jnp.float32), 'w1': jax.random.normal(ks[2], (E, D, H), dtype=jnp.float32) * std, 'w3': jax.random.normal(ks[3], (E, D, H), dtype=jnp.float32) * std, 'w2': jax.random.normal(ks[4], (E, H, D), dtype=jnp.float32) * std, 'sw1': jax.random.normal(ks[5], (S, D, H), dtype=jnp.float32) * std, 'sw3': jax.random.normal(ks[6], (S, D, H), dtype=jnp.float32) * std, 'sw2': jax.random.normal(ks[7], (S, H, D), dtype=jnp.float32) * std}
    _L1_ffn_all = _L1_ffn_setup()
    _L1_ffn_in = {k: v for k, v in _L1_ffn_all.items() if k in ('router_w', 'experts_bias', 'w1', 'w3', 'w2', 'sw1', 'sw3', 'sw2')}
    del _L1_ffn_all
    return {'x': x, 'L0_tok_E1': _L0_tok_in['E1'], 'L0_tok_W2': _L0_tok_in['W2'], 'L0_tok_b2': _L0_tok_in['b2'], 'L0_tok_pos_emb': _L0_tok_in['pos_emb'], 'L0_attn_W_Q': _L0_attn_in['W_Q'], 'L0_attn_W_K': _L0_attn_in['W_K'], 'L0_attn_W_V': _L0_attn_in['W_V'], 'L0_attn_W_O': _L0_attn_in['W_O'], 'L0_ffn_Ws1': _L0_ffn_in['Ws1'], 'L0_ffn_Ws2': _L0_ffn_in['Ws2'], 'L0_ffn_W1': _L0_ffn_in['W1'], 'L0_ffn_W2': _L0_ffn_in['W2'], 'L0_ffn_Wr': _L0_ffn_in['Wr'], 'L1_attn_Wqk': _L1_attn_in['Wqk'], 'L1_attn_bqk': _L1_attn_in['bqk'], 'L1_attn_Wgate': _L1_attn_in['Wgate'], 'L1_attn_bgate': _L1_attn_in['bgate'], 'L1_attn_Wproj': _L1_attn_in['Wproj'], 'L1_attn_bproj': _L1_attn_in['bproj'], 'L1_ffn_router_w': _L1_ffn_in['router_w'], 'L1_ffn_experts_bias': _L1_ffn_in['experts_bias'], 'L1_ffn_w1': _L1_ffn_in['w1'], 'L1_ffn_w3': _L1_ffn_in['w3'], 'L1_ffn_w2': _L1_ffn_in['w2'], 'L1_ffn_sw1': _L1_ffn_in['sw1'], 'L1_ffn_sw3': _L1_ffn_in['sw3'], 'L1_ffn_sw2': _L1_ffn_in['sw2']}

def reference(x, L0_tok_E1, L0_tok_W2, L0_tok_b2, L0_tok_pos_emb, L0_attn_W_Q, L0_attn_W_K, L0_attn_W_V, L0_attn_W_O, L0_ffn_Ws1, L0_ffn_Ws2, L0_ffn_W1, L0_ffn_W2, L0_ffn_Wr, L1_attn_Wqk, L1_attn_bqk, L1_attn_Wgate, L1_attn_bgate, L1_attn_Wproj, L1_attn_bproj, L1_ffn_router_w, L1_ffn_experts_bias, L1_ffn_w1, L1_ffn_w3, L1_ffn_w2, L1_ffn_sw1, L1_ffn_sw3, L1_ffn_sw2):
    import jax
    import jax.numpy as jnp

    def _L0_tok_ref(input_ids, E1, W2, b2, pos_emb):
        import jax, jax.numpy as jnp
        import numpy as np
        VOCAB, HID, RANK, MAX_LEN = (50257, 256, 32, 512)
        B, S = (32, 512)
        x = E1[input_ids]
        x = jnp.einsum('bsr,hr->bsh', x, W2) + b2
        S_ = input_ids.shape[1]
        return x + pos_emb[:, :S_]

    def _L0_attn_ref(x, W_Q, W_K, W_V, W_O):
        import jax, jax.numpy as jnp
        import numpy as np
        NUM_HEADS = 16
        D_MODEL = 256
        D_K = D_MODEL // NUM_HEADS
        MAX_SEQ_LEN = 1024
        ROPE_BASE = 10000.0
        BATCH = 2
        SEQ_LEN = 512

        def _rope_tables(seq_len, d_k, base=ROPE_BASE):
            theta = 1.0 / base ** (jnp.arange(0, d_k, 2, dtype=jnp.float32) / d_k)
            m = jnp.arange(seq_len, dtype=jnp.float32)
            m_theta = jnp.outer(m, theta)
            ang = jnp.concatenate([m_theta, m_theta], axis=-1)
            return (jnp.cos(ang), jnp.sin(ang))

        def _apply_rope(x, cos, sin):
            d2 = x.shape[-1] // 2
            x1, x2 = (x[..., :d2], x[..., d2:])
            x_flip = jnp.concatenate([-x2, x1], axis=-1)
            return x * cos + x_flip * sin
        B, S, _ = x.shape

        def proj(W):
            y = jnp.einsum('bsd,ed->bse', x, W)
            return y.reshape(B, S, NUM_HEADS, D_K).transpose(0, 2, 1, 3)
        Q, K, V = (proj(W_Q), proj(W_K), proj(W_V))
        cos, sin = _rope_tables(S, D_K)
        Q = _apply_rope(Q, cos, sin)
        K = _apply_rope(K, cos, sin)
        scores = jnp.einsum('bhsd,bhtd->bhst', Q, K) / jnp.sqrt(jnp.float32(D_K))
        causal = jnp.tril(jnp.ones((S, S), dtype=bool))
        scores = jnp.where(causal[None, None], scores, -jnp.inf)
        attn = jax.nn.softmax(scores, axis=-1)
        out = jnp.einsum('bhst,bhtd->bhsd', attn, V)
        out = out.transpose(0, 2, 1, 3).reshape(B, S, D_MODEL)
        return jnp.einsum('bsd,ed->bse', out, W_O)

    def _L0_ffn_ref(x, Ws1, Ws2, W1, W2, Wr):
        import jax, jax.numpy as jnp
        import numpy as np
        D_MODEL = 256
        EXPERT_DIM = 128
        N_EXPERTS = 8
        TOP_K = 2

        def _sq_relu(h):
            return jnp.square(jax.nn.relu(h))
        shape = x.shape
        xf = x.reshape(-1, D_MODEL)
        out_shared = _sq_relu(xf @ Ws1) @ Ws2
        logits = xf @ Wr
        top_vals, top_idx = jax.lax.top_k(logits, TOP_K)
        rw = jax.nn.softmax(top_vals.astype(jnp.float32), axis=-1).astype(x.dtype)
        onehot = jax.nn.one_hot(top_idx, N_EXPERTS, dtype=x.dtype)
        prob = jnp.einsum('tk,tke->te', rw, onehot)
        prob = jnp.trunc(prob)
        h = _sq_relu(jnp.einsum('td,edf->tef', xf, W1))
        y = jnp.einsum('tef,efd->ted', h, W2)
        out_routed = jnp.einsum('ted,te->td', y, prob)
        return (out_shared + out_routed).reshape(shape)

    def _L1_attn_ref(x, Wqk, bqk, Wgate, bgate, Wproj, bproj):
        import jax, jax.numpy as jnp
        import numpy as np
        import math
        N_EMBD = 256
        N_HEAD = 16
        BLOCK_SIZE = 256
        B, T = (4, 256)
        Bx, Tx, C = x.shape
        H = N_HEAD
        D = C // H
        windows = jnp.array([max(4, BLOCK_SIZE // 2 ** h) for h in range(H)], dtype=jnp.int32)
        qk = x @ Wqk + bqk
        q, k = jnp.split(qk, 2, axis=-1)
        v = k
        q = q.reshape(Bx, Tx, H, D).transpose(0, 2, 1, 3)
        k = k.reshape(Bx, Tx, H, D).transpose(0, 2, 1, 3)
        v = v.reshape(Bx, Tx, H, D).transpose(0, 2, 1, 3)
        i = jnp.arange(Tx)[:, None]
        j = jnp.arange(Tx)[None, :]
        mask = (j <= i)[None] & (j > i - windows[:, None, None])
        att = jnp.einsum('bhtd,bhsd->bhts', q, k) * (1.0 / math.sqrt(D))
        att = jnp.where(mask[None], att, -jnp.inf)
        att = jax.nn.softmax(att, axis=-1)
        out = jnp.einsum('bhts,bhsd->bhtd', att, v)
        combined = out.transpose(0, 2, 1, 3)
        gates = jax.nn.softmax(x @ Wgate + bgate, axis=-1)
        gated = (combined * gates[..., None]).reshape(Bx, Tx, C)
        return gated @ Wproj + bproj

    def _L1_ffn_ref(x, router_w, experts_bias, w1, w3, w2, sw1, sw3, sw2):
        import jax, jax.numpy as jnp
        import numpy as np
        D, H, E, K, S = (256, 512, 8, 2, 1)
        B, L = (4, 512)
        b, l, d = x.shape
        xf = x.reshape(-1, d)
        sg = jnp.einsum('td,sdh->tsh', xf, sw1)
        su = jnp.einsum('td,sdh->tsh', xf, sw3)
        shared_out = jnp.einsum('tsh,shd->td', jax.nn.silu(sg) * su, sw2)
        logits = xf @ router_w.T + experts_bias
        rw, sel = jax.lax.top_k(logits, K)
        rw = jax.nn.softmax(rw.astype(jnp.float32), axis=-1).astype(x.dtype)
        cw = (jax.nn.one_hot(sel, E, dtype=x.dtype) * rw[..., None]).sum(axis=1)
        g = jnp.einsum('td,edh->teh', xf, w1)
        u = jnp.einsum('td,edh->teh', xf, w3)
        eo = jax.nn.silu(g) * u
        moe_out = jnp.einsum('te,teh,ehd->td', cw, eo, w2)
        return (moe_out + shared_out).reshape(b, l, d)
    h = _L0_tok_ref(x, L0_tok_E1, L0_tok_W2, L0_tok_b2, L0_tok_pos_emb)
    h = h + _L0_attn_ref(_layernorm(h, axis=-1), L0_attn_W_Q, L0_attn_W_K, L0_attn_W_V, L0_attn_W_O)
    h = h + _L0_ffn_ref(_layernorm(h, axis=-1), L0_ffn_Ws1, L0_ffn_Ws2, L0_ffn_W1, L0_ffn_W2, L0_ffn_Wr)
    h = h + _L1_attn_ref(_layernorm(h, axis=-1), L1_attn_Wqk, L1_attn_bqk, L1_attn_Wgate, L1_attn_bgate, L1_attn_Wproj, L1_attn_bproj)
    h = h + _L1_ffn_ref(_layernorm(h, axis=-1), L1_ffn_router_w, L1_ffn_experts_bias, L1_ffn_w1, L1_ffn_w3, L1_ffn_w2, L1_ffn_sw1, L1_ffn_sw3, L1_ffn_sw2)
    return h

_drawn_inputs = setup_inputs


def setup_inputs(seed=0):
    import zlib

    import numpy as np

    out = dict(_drawn_inputs(seed))
    spreads = {'L1_attn_bqk': (0.0, 0.8),
     'L1_attn_bgate': (0.0, 0.8),
     'L1_attn_bproj': (0.0, 0.1),
     'L1_ffn_experts_bias': (0.0, 0.8)}
    factors = {'L0_tok_b2': 8.0,
     'L0_attn_W_Q': 5.899,
     'L0_attn_W_K': 5.789,
     'L0_ffn_Ws1': 3.072,
     'L0_ffn_Ws2': 2.805,
     'L1_attn_Wqk': 8.0,
     'L1_attn_Wgate': 8.0,
     'L1_attn_Wproj': 8.0,
     'L1_ffn_router_w': 5.742,
     'L1_ffn_w1': 4.748,
     'L1_ffn_w3': 4.704,
     'L1_ffn_w2': 4.7,
     'L1_ffn_sw1': 3.386,
     'L1_ffn_sw3': 3.343,
     'L1_ffn_sw2': 3.355}
    for name, (base, spread) in spreads.items():
        noise = np.random.default_rng([zlib.crc32(name.encode()), seed]).standard_normal(out[name].shape)
        drawn = base * np.exp(spread * noise) if base else spread * noise
        out[name] = jnp.asarray(drawn.astype(out[name].dtype))
    for name, factor in factors.items():
        out[name] = (out[name] * factor).astype(out[name].dtype)
    return out
```

```python
from contextlib import ExitStack

import concourse.bass as bass
from concourse import mybir

P = 128
F32 = mybir.dt.float32
F32R = mybir.dt.float32r
BF16 = mybir.dt.bfloat16
I32 = mybir.dt.int32
U32 = mybir.dt.uint32
ALU = mybir.AluOpType
ACT = mybir.ActivationFunctionType
AX = mybir.AxisListType

B, S, D = 8, 512, 256
NT = B * S // P
TG = S // P
KD = D // P
RANK = 32
H, DK = 16, 16
HG = 4
NHG = H // HG
VW = 32
TERMS_Q = (0, 0, 0, 1, 1, 2)
TERMS_K = (0, 1, 2, 0, 1, 0)
NTERM = len(TERMS_Q)
KROWS = NTERM * DK
MROWS = 2
EPS = 1e-5
MASKED = -1e30
E0, F0 = 8, 128
E1N, F1 = 8, 512
HB = F1 // P
WINDOWS = [max(4, 256 // 2 ** h) for h in range(H)]


class Kit:

    used = []

    def __init__(self, nc, ctx, tag):
        self.nc, self.ctx, self.tag = nc, ctx, tag
        self.sems = []

    def sb(self, name, shape, dt=F32):
        return self.ctx.enter_context(self.nc.sbuf_tensor(f"{self.tag}_{name}", shape, dt))

    def ps(self, name, shape, dt=F32):
        return self.ctx.enter_context(self.nc.psum_tensor(f"{self.tag}_{name}", shape, dt))

    def sem(self, name):
        handle = self.ctx.enter_context(self.nc.semaphore(f"{self.tag}_{name}"))
        Kit.used.append(handle)
        self.sems.append(handle)
        return handle

    def open(self):
        with self.nc.Block() as block:
            @block.gpsimd
            def _(pool):
                for handle in self.sems:
                    pool.sem_inc(handle, 1)


def clear_semaphores(nc):
    numbers = sorted({h.num for h in Kit.used})
    Kit.used.clear()
    with nc.Block() as block:
        @block.gpsimd
        def _(pool):
            first = 0
            for n in range(1, len(numbers) + 1):
                if n == len(numbers) or numbers[n] != numbers[n - 1] + 1:
                    pool.sem_clear(range(numbers[first], numbers[n - 1] + 1))
                    first = n


def looped(eng, n, body):
    with eng.Fori(0, n - 1) as i:
        body(i, False)
    body(n - 1, True)


def split_passes(hi_a, lo_a, hi_b, lo_b):
    return ((hi_a, hi_b), (hi_a, lo_b), (lo_a, hi_b))


def embed(nc, res, ident, s_rows, ids, E1, w2t, b2, pos):
    with ExitStack() as ctx:
        k = Kit(nc, ctx, "emb")
        ids_sb = k.sb("ids", [P, NT], I32)
        rows = k.sb("rows", [P, NT, RANK])
        rowsT = k.sb("rowsT", [P, NT // TG, P])
        w_blk = k.sb("w_blk", [P, TG, D])
        posb = k.sb("posb", [P, TG, D])
        b2b = k.sb("b2b", [P, D])
        psT = k.ps("psT", [P, 2, 512])
        psO = k.ps("psO", [P, 4, 512])
        s_ids, s_w, s_pos = (k.sem(n) for n in ("ids", "w", "pos"))
        s_zero, s_bias, s_T, s_Tc, s_mm, s_res = (k.sem(n) for n in ("zero", "bias", "T", "Tc", "mm", "res"))
        block = ctx.enter_context(nc.Block())
        NG = NT // TG

        @block.sync
        def _(sp):
            sp.dma_start(ids_sb[:], ids).then_inc(s_ids, 16)
            sp.dma_start(posb[:], pos.rearrange("o (t p) d -> p (o t) d", p=P)).then_inc(s_pos, 16)
            sp.dma_start(b2b[:], b2.partition_broadcast(P)).then_inc(s_pos, 16)
            sp.wait_ge(s_zero, 1)
            for j in range(TG):
                sp.dma_start(w_blk[RANK * j:RANK * (j + 1), j, :], w2t).then_inc(s_w, 16)

        @block.gpsimd
        def _(pool):
            pool.wait_ge(s_ids, 16)
            for t in range(NT):
                pool.indirect_dma_start(out=rows[:, t, :], out_offset=None, in_=E1,
                                        in_offset=bass.IndirectOffsetOnAxis(ap=ids_sb[:, t:t + 1], axis=0)
                                        ).then_inc(s_rows, 16)

        @block.tensor
        def _(pe):
            pe.wait_ge(s_rows, 16 * NT)
            for g in range(NG):
                if g >= 2:
                    pe.wait_ge(s_Tc, g - 1)
                pe.transpose(psT[:, g % 2, 0:P], rows[:, TG * g:TG * (g + 1), :], ident[:]).then_inc(s_T, 1)
            pe.wait_ge(s_w, 16 * TG)
            for g in range(NG):
                pe.wait_ge(s_Tc, g + 1)
                for q in range(2):
                    n = 2 * g + q
                    if n >= 4:
                        pe.wait_ge(s_res, n - 3)
                    pe.matmul(psO[:, n % 4, :], rowsT[:, g, :], w_blk[:, 2 * q:2 * q + 2, :],
                              start=True, stop=True).then_inc(s_mm, 1)

        @block.scalar
        def _(act):
            for g in range(NG):
                act.wait_ge(s_T, g + 1)
                act.copy(rowsT[:, g, :], psT[:, g % 2, 0:P]).then_inc(s_Tc, 1)

        @block.vector
        def _(dve):
            dve.memset(w_blk[:], 0.0).then_inc(s_zero, 1)
            dve.wait_ge(s_pos, 32)
            dve.tensor_tensor(posb[:], posb[:], b2b[:].unsqueeze(1).to_broadcast([P, TG, D]), ALU.add).then_inc(s_bias, 1)
            dve.wait_ge(s_bias, 1)
            for n in range(2 * NG):
                dve.wait_ge(s_mm, n + 1)
                q = n % 2
                dve.tensor_tensor(res[:, 2 * n:2 * n + 2, :], psO[:, n % 4, :].rearrange("p (t d) -> p t d", d=D),
                                  posb[:, 2 * q:2 * q + 2, :], ALU.add).then_inc(s_res, 1)


class Norm:

    def __init__(self, k):
        self.stats = k.sb("ln_stats", [P, NT, 6])
        self.mv = k.sb("ln_mv", [P, NT, 2])
        self.dev = k.sb("ln_dev", [P, NT])
        self.rstd = k.sb("ln_rstd", [P, NT])
        self.s_stats, self.s_mv = k.sem("ln_stats"), k.sem("ln_mv")
        self.s_var, self.s_dev, self.s_done = k.sem("ln_var"), k.sem("ln_dev"), k.sem("ln_done")

    def vector(self, dve, res):
        with dve.Fori(0, NT) as t:
            dve.bn_stats(self.stats[:, t, :], res[:, t, :]).then_inc(self.s_stats, 1)
        dve.wait_ge(self.s_stats, NT + 1)
        for t in range(NT):
            dve.bn_aggr(self.mv[:, t, :], self.stats[:, t, :]).then_inc(self.s_mv, 1)
        dve.wait_ge(self.s_mv, NT + 1)
        dve.tensor_scalar(self.dev[:], self.mv[:, :, 1], EPS, None, ALU.add).then_inc(self.s_var, 1)
        dve.wait_ge(self.s_dev, 2)
        dve.reciprocal(self.rstd[:], self.dev[:]).then_inc(self.s_done, 1)
        dve.wait_ge(self.s_done, 2)

    def scalar(self, act):
        act.wait_ge(self.s_var, 2)
        act.activation(self.dev[:], self.dev[:], ACT.Sqrt).then_inc(self.s_dev, 1)

    def apply(self, dve, out, res, t):
        return dve.tensor_scalar(out, res[:, t, :], self.mv[:, t, 0:1], self.rstd[:, bass.ds(t, 1)],
                                 ALU.subtract, ALU.mult)


def load_split(k, name, src, shape):
    return dict(src=src, raw=k.sb(name + "_raw", shape), hi=k.sb(name + "_hi", shape, F32R),
                lo=k.sb(name + "_lo", shape, F32R))


def load_weights(sp, ws, s_raw):
    for w in ws:
        sp.dma_start(w["raw"][:], w["src"]).then_inc(s_raw, 16)


def split_weights(eng, ws, s_raw, s_hi, s_wt):
    eng.wait_ge(s_raw, 16 * len(ws) + 1)
    for n, w in enumerate(ws):
        eng.tensor_copy(w["hi"][:], w["raw"][:]).then_inc(s_hi, 1)
    for n, w in enumerate(ws):
        eng.wait_ge(s_hi, n + 2)
        eng.tensor_tensor(w["lo"][:], w["raw"][:], w["hi"][:].bitcast(F32), ALU.subtract).then_inc(s_wt, 1)


def project_qkv(nc, tag, res, ident, w_qk, w_v, bias_qk, rope, gate_w, gate_b, q_dram, k_dram, v_dram, gates):
    has_v = w_v is not None
    with ExitStack() as ctx:
        k = Kit(nc, ctx, tag)
        norm = Norm(k)
        ws = [load_split(k, "w_qk", w_qk, [P, KD, 2 * D])]
        if has_v:
            ws.append(load_split(k, "w_v", w_v, [P, KD, D]))
        else:
            ws.append(load_split(k, "w_g", gate_w, [P, KD, H]))
        xn = k.sb("xn", [P, TG, D])
        xTh, xTl = k.sb("xTh", [P, KD, S], F32R), k.sb("xTl", [P, KD, S], F32R)
        qk = k.sb("qk", [P, 2, 2 * D])
        qkr = k.sb("qkr", [P, TG, 2 * D])
        part = k.sb("part", [P, 3, 4, S], BF16)
        rest = k.sb("rest", [P, 4, S])
        vaug = k.sb("vaug", [P, TG, H, VW])
        one = k.sb("one", [P, 1])
        psT = k.ps("psT", [P, KD, S])
        psQ = k.ps("psQ", [P, 512])
        psV = k.ps("psV", [P, 512])
        psR = k.ps("psR", [P, 4, S])
        names = ("raw tab hi wt xn xT xTh xTl q v qs vs rot1 rot2 rot3 R h rest m l out ones vout gT gc gt").split()
        s = {n: k.sem(n) for n in names}
        if rope is not None:
            cos_sb, sin_sb = k.sb("cos", [P, TG, DK]), k.sb("sin", [P, TG, DK])
            rot = k.sb("rot", [P, 2, 2 * D])
        else:
            bias_sb = k.sb("bias", [P, 2 * D])
            gT_sb = k.sb("gT_sb", [P, S])
            glog = k.sb("glog", [P, NT, H])
            gb_sb = k.sb("gb_sb", [P, H])
            gmax, gsum = k.sb("gmax", [P, NT]), k.sb("gsum", [P, NT])
            s_gates = k.sem("gates")
        k.open()
        block = ctx.enter_context(nc.Block())

        @block.sync
        def _(sp):
            load_weights(sp, ws, s["raw"])
            if rope is not None:
                sp.dma_start(cos_sb[:], rope[0]).then_inc(s["tab"], 16)
                sp.dma_start(sin_sb[:], rope[1]).then_inc(s["tab"], 16)
            else:
                sp.dma_start(bias_sb[:], bias_qk.partition_broadcast(P)).then_inc(s["tab"], 16)
                sp.dma_start(gb_sb[:], gate_b.partition_broadcast(P)).then_inc(s["tab"], 16)

            def body(b, last):
                sp.wait_ge(s["ones"], 3)
                sp.wait_ge(s["vs"], TG * b + TG + 1)
                sp.dma_start(v_dram[b].rearrange("(t p) c -> p t c", p=P),
                             vaug[:].rearrange("p t h c -> p t (h c)")).then_inc(s["vout"], 16)
                sp.wait_ge(s["l"], b + 2)
                for c in range(2):
                    for r, term in enumerate(TERMS_Q):
                        dst = q_dram[b, 8 * c:8 * c + 8, DK * r:DK * (r + 1), :]
                        sp.dma_start(dst, part[:, term, c, :]).then_inc(s["out"], 16)
                    for term in range(3):
                        dst = k_dram[b, 8 * c:8 * c + 8, DK * term:DK * (term + 1), :]
                        sp.dma_start(dst, part[:, term, 2 + c, :]).then_inc(s["out"], 16)

            looped(sp, B, body)
            sp.wait_ge(s["out"], 16 * 18 * B + 1)
            sp.wait_ge(s["vout"], 16 * B + 1)

        @block.tensor
        def _(pe):
            def transposes(b):
                pe.wait_ge(s["xn"], TG * b + TG + 1)
                pe.wait_ge(s["xTl"], KD * b + 1)
                for i in range(TG):
                    for c in range(KD):
                        mm = pe.transpose(psT[:, c, P * i:P * (i + 1)], xn[:, i, P * c:P * (c + 1)], ident[:])
                mm.then_inc(s["xT"], 1)

            def body(b, last):
                pe.wait_ge(s["xTl"], KD * b + KD + 1)
                pe.wait_ge(s["xTh"], KD * b + KD + 1)
                for i in range(TG):
                    tok = slice(P * i, P * (i + 1))
                    pe.wait_ge(s["qs"], TG * b + i + 1)
                    n = 0
                    for a, w in split_passes(xTh, xTl, ws[0]["hi"], ws[0]["lo"]):
                        for c in range(KD):
                            mm = pe.matmul(psQ[:], a[:, c, tok], w[:, c, :], start=(n == 0), stop=(n == 5))
                            n += 1
                    mm.then_inc(s["q"], 1)
                    if has_v:
                        pe.wait_ge(s["vs"], TG * b + i + 1)
                        n = 0
                        for a, w in split_passes(xTh, xTl, ws[1]["hi"], ws[1]["lo"]):
                            for c in range(KD):
                                mm = pe.matmul(psV[:, 0:D], a[:, c, tok], w[:, c, :], start=(n == 0), stop=(n == 5))
                                n += 1
                        mm.then_inc(s["v"], 1)
                if not has_v:
                    pe.wait_ge(s["gt"], b + 1)
                    n = 0
                    for w, a in split_passes(ws[1]["hi"], ws[1]["lo"], xTh, xTl):
                        for c in range(KD):
                            mm = pe.matmul(psV[0:H, :], w[:, c, :], a[:, c, :], start=(n == 0), stop=(n == 5))
                            n += 1
                    mm.then_inc(s["gT"], 1)
                if not last:
                    transposes(b + 1)
                if not has_v:
                    pe.wait_ge(s["wt"], len(ws) + 1)
                    pe.wait_ge(s["gc"], b + 2)
                    for i in range(TG):
                        mm = pe.transpose(psV[:, P * i:P * (i + 1)], gT_sb[:, P * i:P * (i + 1)], ident[:])
                    mm.then_inc(s["v"], 1)
                pe.wait_ge(s["rest"], 2 * b + 1)
                pe.wait_ge(s["rot3" if rope is not None else "qs"], TG * b + TG + 1)
                for c in range(4):
                    for i in range(TG):
                        mm = pe.transpose(psR[:, c, P * i:P * (i + 1)], qkr[:, i, P * c:P * (c + 1)], ident[:])
                    if c % 2:
                        mm.then_inc(s["R"], 1)

            pe.wait_ge(s["wt"], len(ws) + 1)
            transposes(0)
            looped(pe, B, body)

        @block.scalar
        def _(act):
            norm.scalar(act)
            act.wait_ge(s["ones"], 4 if has_v else 5)

            def body(b, last):
                act.wait_ge(s["xT"], b + 2)
                if has_v:
                    act.wait_ge(s["v"], TG * b + 1)
                else:
                    act.wait_ge(s["gT"], b + 1)
                for c in range(KD):
                    act.copy(xTh[:, c, :], psT[:, c, :]).then_inc(s["xTh"], 1)
                for i in range(TG):
                    if has_v:
                        act.wait_ge(s["q"], TG * b + i + 2)
                        if i >= 2:
                            act.wait_ge(s["rot1"], TG * b + i)
                            act.wait_ge(s["rot2"], TG * b + i)
                        else:
                            act.wait_ge(s["rot1"], TG * b + 1)
                            act.wait_ge(s["rot2"], TG * b + 1)
                        act.copy(qk[:, i % 2, :], psQ[:]).then_inc(s["qs"], 1)
                        act.wait_ge(s["v"], TG * b + i + 2)
                        act.wait_ge(s["vout"], 16 * b + 1)
                        act.copy(vaug[:, i, :, 0:DK], psV[:, 0:D].rearrange("p (h d) -> p h d", d=DK)).then_inc(s["vs"], 1)
                    else:
                        act.wait_ge(s["qs"], TG * b + i + 2)
                        act.wait_ge(s["vout"], 16 * b + 1)
                        act.copy(vaug[:, i, :, 0:DK],
                                 qkr[:, i, D:2 * D].rearrange("p (h d) -> p h d", d=DK)).then_inc(s["vs"], 1)
                if not has_v:
                    act.wait_ge(s["gT"], b + 2)
                    act.copy(gT_sb[0:H, :], psV[0:H, :]).then_inc(s["gc"], 1)
                act.wait_ge(s["out"], 16 * 18 * b + 1)
                for q in range(2):
                    act.wait_ge(s["R"], 2 * b + q + 2)
                    act.copy(part[:, 0, 2 * q:2 * q + 2, :], psR[:, 2 * q:2 * q + 2, :]).then_inc(s["h"], 1)

            looped(act, B, body)
            if not has_v:
                act.wait_ge(s_gates, 3)
                act.activation(glog[:], glog[:], ACT.Exp).then_inc(s_gates, 1)

        @block.gpsimd
        def _(pool):
            split_weights(pool, ws, s["raw"], s["hi"], s["wt"])
            pool.memset(vaug[:, :, :, DK:VW], 0.0).then_inc(s["ones"], 1)
            pool.wait_ge(s["ones"], 2)
            pool.memset(vaug[:, :, :, DK:DK + 1], 1.0).then_inc(s["ones"], 1)
            pool.memset(one[:], 1.0).then_inc(s["ones"], 1)
            if not has_v:
                pool.memset(gT_sb[:], 0.0).then_inc(s["ones"], 1)
            pool.wait_ge(s["ones"], 4 if has_v else 5)
            if rope is not None:
                pool.wait_ge(s["tab"], 33)

            def body(b, last):
                if rope is not None:
                    for i in range(TG):
                        pool.wait_ge(s["qs"], TG * b + i + 2)
                        if i >= 2:
                            pool.wait_ge(s["rot3"], TG * b + i)
                        else:
                            pool.wait_ge(s["rot3"], TG * b + 1)
                        src = qk[:, i % 2, :].rearrange("p (h u d) -> p h u d", u=2, d=DK // 2)
                        dst = rot[:, i % 2, :].rearrange("p (h u d) -> p h u d", u=2, d=DK // 2)
                        for u in range(2):
                            sn = sin_sb[:, i, 8 * u:8 * u + 8].unsqueeze(1).to_broadcast([P, 2 * H, DK // 2])
                            ins = pool.tensor_tensor(dst[:, :, u, :], src[:, :, 1 - u, :], sn, ALU.mult)
                        ins.then_inc(s["rot2"], 1)
                pool.wait_ge(s["rest"], 2 * b + 3)
                pool.wait_ge(s["out"], 16 * 18 * b + 1)
                pool.tensor_tensor(part[:, 1], rest[:], one[:].unsqueeze(2).to_broadcast([P, 4, S]), ALU.mult).then_inc(s["m"], 1)
                pool.wait_ge(s["m"], b + 2)
                pool.tensor_tensor(part[:, 2], rest[:], part[:, 1], ALU.subtract).then_inc(s["l"], 1)

            looped(pool, B, body)

        @block.vector
        def _(dve):
            norm.vector(dve, res)
            dve.wait_ge(s["tab"], 33)

            def normed(b):
                dve.wait_ge(s["xT"], b + 1)
                for i in range(TG):
                    norm.apply(dve, xn[:, i, :], res, TG * b + i).then_inc(s["xn"], 1)

            def lows(b):
                for c in range(KD):
                    dve.wait_ge(s["xTh"], KD * b + c + 2)
                    dve.tensor_tensor(xTl[:, c, :], psT[:, c, :], xTh[:, c, :].bitcast(F32),
                                      ALU.subtract).then_inc(s["xTl"], 1)

            def body(b, last):
                if has_v:
                    dve.wait_ge(s["v"], TG * b + 1)
                else:
                    dve.wait_ge(s["gT"], b + 1)
                lows(b)
                if not last:
                    normed(b + 1)
                for i in range(TG):
                    dve.wait_ge(s["R"], 2 * b + 1)
                    if rope is not None:
                        dve.wait_ge(s["qs"], TG * b + i + 2)
                        cs = cos_sb[:, i, :].unsqueeze(1).to_broadcast([P, 2 * H, DK])
                        dve.tensor_tensor(qkr[:, i, :].rearrange("p (h d) -> p h d", d=DK),
                                          qk[:, i % 2, :].rearrange("p (h d) -> p h d", d=DK), cs,
                                          ALU.mult).then_inc(s["rot1"], 1)
                        dve.wait_ge(s["rot1"], TG * b + i + 2)
                        dve.wait_ge(s["rot2"], TG * b + i + 2)
                        dve.tensor_tensor(qkr[:, i, :], qkr[:, i, :], rot[:, i % 2, :], ALU.add).then_inc(s["rot3"], 1)
                    else:
                        dve.wait_ge(s["q"], TG * b + i + 2)
                        dve.wait_ge(s["vs"], TG * b + 1)
                        dve.tensor_tensor(qkr[:, i, :], psQ[:], bias_sb[:], ALU.add).then_inc(s["qs"], 1)
                if not has_v:
                    dve.wait_ge(s["v"], b + 2)
                    dve.tensor_tensor(glog[:, bass.ds(TG * b, TG), :],
                                      psV[:].rearrange("p (t c) -> p t c", c=P)[:, :, 0:H],
                                      gb_sb[:].unsqueeze(1).to_broadcast([P, TG, H]), ALU.add).then_inc(s["gt"], 1)
                dve.wait_ge(s["l"], b + 1)
                for q in range(2):
                    dve.wait_ge(s["h"], 2 * b + q + 2)
                    dve.tensor_tensor(rest[:, 2 * q:2 * q + 2, :], psR[:, 2 * q:2 * q + 2, :],
                                      part[:, 0, 2 * q:2 * q + 2, :], ALU.subtract).then_inc(s["rest"], 1)

            normed(0)
            looped(dve, B, body)
            if not has_v:
                dve.wait_ge(s["gt"], B + 1)
                dve.tensor_reduce(gmax[:], glog[:], AX.X, ALU.max).then_inc(s_gates, 1)
                dve.wait_ge(s_gates, 2)
                dve.tensor_tensor(glog[:], glog[:], gmax[:].unsqueeze(2).to_broadcast([P, NT, H]),
                                  ALU.subtract).then_inc(s_gates, 1)
                dve.wait_ge(s_gates, 4)
                dve.tensor_reduce(gsum[:], glog[:], AX.X, ALU.add).then_inc(s_gates, 1)
                dve.wait_ge(s_gates, 5)
                dve.reciprocal(gsum[:], gsum[:]).then_inc(s_gates, 1)
                dve.wait_ge(s_gates, 6)
                dve.tensor_tensor(gates[:], glog[:], gsum[:].unsqueeze(2).to_broadcast([P, NT, H]),
                                  ALU.mult).then_inc(s_gates, 1)
                dve.wait_ge(s_gates, 7)


class Unit:

    def __init__(self, n, i=None):
        self.n, self.i = n, i
        self.hg, self.par, self.buf = n % NHG, n % 2, n % 4

    def __sub__(self, d):
        return Unit(self.n - d, self.i)

    def of(self, per_four, static):
        return static if self.i is None else self.i * per_four + static

    @property
    def value(self):
        return self.of(NHG, self.n)

    @property
    def half(self):
        return self.of(NHG // 2, self.n // 2)

    @property
    def seq(self):
        return self.of(1, self.n // NHG)

    def exists(self):
        return self.i is not None or 0 <= self.n < B * NHG

    def after(self, d):
        return self.i is not None or self.n >= d

    def slots(self, counts, k=0):
        whole, part = divmod(self.n, NHG)
        return self.of(sum(counts), whole * sum(counts) + sum(counts[:part]) + k)

    def slot_par(self, counts, k):
        whole, part = divmod(self.n, NHG)
        return (whole * sum(counts) + sum(counts[:part]) + k) % 2


def query_slots(windows, hg):
    out = []
    if windows is None:
        out.append([(0, P * h, h, 0, 0, P) for h in range(HG)])
        out.append([(h // 2, 256 * (h % 2), h, 1, 0, 256) for h in range(HG)])
        for i in (2, 3):
            out += [[(n, 0, 2 * q + n, i, 0, P * (i + 1)) for n in range(2)] for q in range(2)]
        return out
    for h in range(HG):
        w = windows[HG * hg + h]
        if w > P:
            out += [[(n, 0, h, i + n, P * (i + n) - w, P + w) for n in range(m)] for i, m in ((0, 2), (2, 1), (3, 1))]
        else:
            out.append([(i // 2, 256 * (i % 2), h, i, P * i - w, P + w) for i in range(TG)])
    return out


def key_slots(windows, hg):
    out = []
    if windows is None:
        for j in (0, 1):
            out += [[(0, h, j, S - P * j)] for h in range(HG)]
        out += [[(256 * n, 2 * q + n, 2, 256) for n in range(2)] for q in range(2)]
        out.append([(P * h, h, 3, P) for h in range(HG)])
        return out
    for h in range(HG):
        w = windows[HG * hg + h]
        if w > P:
            out += [[(0, h, j, P + w)] for j in range(TG)]
        else:
            out += [[(256 * n, h, 2 * q + n, P + w) for n in range(2)] for q in range(2)]
    return out


def events(windows, u):
    na = len(query_slots(windows, u.hg)) if u.exists() else 0
    nb = len(key_slots(windows, (u - 2).hg)) if (u - 2).exists() else 0
    out, ia, ib = [], 0, 0
    while ia < na or ib < nb:
        if ia < na and (ib >= nb or ia * nb <= ib * na):
            out.append(("A", ia))
            ia += 1
        else:
            out.append(("B", ib))
            ib += 1
    steps, out = out, []
    if (u - 3).exists():
        out += [("PV", 0)]
    out += steps[:3]
    if (u - 1).exists():
        out += [("TOP", 0)]
    out += steps[3:8]
    if (u - 3).exists():
        out += [("OUT", 0)]
    return out + steps[8:]


def walk(eng, stage):
    for n in range(NHG):
        stage(Unit(n))
    with eng.Fori(1, B) as i:
        for n in range(NHG):
            stage(Unit(n, i))
    for n in range(3):
        stage(Unit(B * NHG + n))


def attend(nc, tag, windows, q_dram, k_dram, v_dram, m_dram, ident, gates, attn):
    NU = B * NHG
    kinds = sorted(set(windows), reverse=True) if windows else [None]
    na = [len(query_slots(windows, g)) for g in range(NHG)]
    nb = [len(key_slots(windows, g)) for g in range(NHG)]
    assert sum(na) % 2 == 0 and sum(nb) % 2 == 0
    reach = S if windows is None else P + max(windows)
    with ExitStack() as ctx:
        k = Kit(nc, ctx, tag)
        qa = k.sb("qa", [P, 4, HG, S], BF16)
        ka = k.sb("ka", [P, 4, HG, S], BF16)
        vu = k.sb("vu", [P, 4, TG, HG, VW])
        top = k.sb("top", [P, 2, HG, TG])
        topT = k.sb("topT", [HG * TG, 2, MROWS, P], BF16)
        idb = k.sb("idb", [P, P], BF16)
        wide = {w: (P + w if w else P) for w in kinds}
        mask_q = {w: k.sb(f"mask_q{w}", [P, wide[w]], BF16) for w in kinds}
        mask_k = {w: k.sb(f"mask_k{w}", [P, wide[w]], BF16) for w in kinds}
        never = k.sb("never", [P, 256], BF16)
        prob = k.sb("prob", [P, 2, HG, TG, reach])
        outT = k.sb("outT", [P, 2, S])
        rec = k.sb("rec", [P, 2, TG, HG])
        psA = k.ps("psA", [P, 2, 2, 512])
        psB = k.ps("psB", [P, 2, 512])
        psO = k.ps("psO", [P, 512])
        psM = k.ps("psM", [P, 512])
        s_load = [k.sem(f"load{n}") for n in range(2)]
        names = "const mask scoresA max topT_ps topT m_out m_in scoresB exp pv outT turned rec norm".split()
        s = {n: k.sem(n) for n in names}
        n_mask = 2 * len(kinds) * (3 if windows else 2)
        block = ctx.enter_context(nc.Block())

        def window(u, h):
            return windows[HG * u.hg + h] if windows else None

        @block.gpsimd
        def _(pool):
            pool.memset(never[:], MASKED).then_inc(s["const"], 1)
            pool.wait_ge(s["const"], 1)
            pool.memset(ka[KROWS:KROWS + MROWS], -1.0).then_inc(s["const"], 1)
            pool.wait_ge(s["const"], 2)
            pool.tensor_copy(idb[:], ident[:]).then_inc(s["const"], 1)
            pool.wait_ge(s["const"], 3)
            for w in kinds:
                pool.memset(mask_q[w][:], 0.0).then_inc(s["mask"], 1)
                pool.memset(mask_k[w][:], 0.0).then_inc(s["mask"], 1)
            pool.wait_ge(s["mask"], 2 * len(kinds))
            for w in kinds:
                pool.affine_select(out=mask_q[w][:], in_=mask_q[w][:], compare_op=ALU.is_ge, fill=MASKED,
                                   base=w or 0, pattern=[[-1, wide[w]]], channel_multiplier=1).then_inc(s["mask"], 1)
                pool.affine_select(out=mask_k[w][:], in_=mask_k[w][:], compare_op=ALU.is_ge, fill=MASKED,
                                   base=0, pattern=[[1, wide[w]]], channel_multiplier=-1).then_inc(s["mask"], 1)
            pool.wait_ge(s["mask"], 4 * len(kinds))
            for w in kinds:
                if w:
                    pool.affine_select(out=mask_q[w][:], in_=mask_q[w][:], compare_op=ALU.is_gt, fill=MASKED,
                                       base=0, pattern=[[1, wide[w]]], channel_multiplier=-1).then_inc(s["mask"], 1)
                    pool.affine_select(out=mask_k[w][:], in_=mask_k[w][:], compare_op=ALU.is_gt, fill=MASKED,
                                       base=w, pattern=[[-1, wide[w]]], channel_multiplier=1).then_inc(s["mask"], 1)

        @block.sync
        def _(sp):
            def loads(u):
                if not u.exists():
                    return
                h0 = HG * u.hg
                done = s_load[u.par]
                if u.after(4):
                    sp.wait_ge(s["exp"], (u - 3).slots(nb))
                kv = k_dram[bass.ds(u.seq, 1), h0:h0 + HG].rearrange("o h r n -> r (o h) n")
                sp.dma_start(qa[0:KROWS, u.buf], q_dram[bass.ds(u.seq, 1), h0:h0 + HG]
                             .rearrange("o h r n -> r (o h) n")).then_inc(done, 16)
                sp.dma_start(ka[0:3 * DK, u.buf], kv[0:3 * DK]).then_inc(done, 16)
                sp.dma_start(ka[3 * DK:5 * DK, u.buf], kv[0:2 * DK]).then_inc(done, 16)
                sp.dma_start(ka[5 * DK:6 * DK, u.buf], kv[0:DK]).then_inc(done, 16)
                if u.after(4):
                    sp.wait_ge(s["pv"], (u - 3).value)
                vsrc = v_dram[bass.ds(u.seq, 1), :, h0 * VW:(h0 + HG) * VW]
                sp.dma_start(vu[:, u.buf].rearrange("p t h c -> p t (h c)"),
                             vsrc.rearrange("o (t p) c -> p (o t) c", p=P)).then_inc(done, 16)

            def maxima(u):
                if not u.exists():
                    return
                sp.wait_ge(s["topT"], MROWS * u.value + MROWS)
                if u.after(2):
                    sp.wait_ge(s["m_in"], 16 * (u - 1).value)
                sp.dma_start(m_dram[u.par].rearrange("r (q n) -> q r n", n=P), topT[:, u.par]).then_inc(s["m_out"], 16)
                sp.wait_ge(s["m_out"], 16 * u.value + 16)
                sp.dma_start(qa[KROWS:KROWS + MROWS, u.buf].rearrange("r h n -> r (h n)"),
                             m_dram[u.par]).then_inc(s["m_in"], 16)

            def stage(u):
                if u.i is None and u.n == 0:
                    loads(u)
                maxima(u - 1)
                loads(Unit(u.n + 1, u.i))

            for n in range(NHG):
                stage(Unit(n))
            with sp.Fori(1, B - 1) as i:
                for n in range(NHG):
                    stage(Unit(n, i))
            for n in range(NHG * (B - 1), NHG * B + 3):
                stage(Unit(n))

        @block.tensor
        def _(pe):
            pe.wait_ge(s["mask"], n_mask)
            pe.wait_ge(s["const"], 3)

            def query_tile(u, slot, t):
                bank, col, h, i, k0, cols = t
                out = psA[:, slot, bank, col:col + cols]
                q = qa[0:KROWS, u.buf, h, P * i:P * (i + 1)]
                w = window(u, h)
                if w is None:
                    pe.matmul(out, q, ka[0:KROWS, u.buf, h, 0:cols], start=True, stop=True)
                    return pe.matmul(out[:, cols - P:cols], idb[:], mask_q[w][:], start=False, stop=True,
                                     skip_group_check=True)
                cut = max(0, -k0)
                if cut:
                    pe.matmul(out[:, 0:cut], idb[:], never[:, 0:cut], start=True, stop=False, skip_group_check=True)
                pe.matmul(out[:, cut:cols], idb[:], mask_q[w][:, cut:cols], start=(cut == 0), stop=False,
                          skip_group_check=True)
                return pe.matmul(out[:, cut:cols], q, ka[0:KROWS, u.buf, h, k0 + cut:k0 + cols],
                                 start=False, stop=True, skip_group_check=True)

            def key_tile(u, slot, t):
                col, h, j, cols = t
                out = psB[:, slot, col:col + cols]
                w = window(u, h)
                have = min(cols, S - P * j)
                keys = ka[0:KROWS + MROWS, u.buf, h, P * j:P * (j + 1)]
                qs = qa[0:KROWS + MROWS, u.buf, h, P * j:P * j + have]
                if w is None:
                    pe.matmul(out, keys, qs, start=True, stop=True)
                    return pe.matmul(out[:, 0:P], idb[:], mask_k[w][:], start=False, stop=True, skip_group_check=True)
                pe.matmul(out, idb[:], mask_k[w][:], start=True, stop=False, skip_group_check=True)
                return pe.matmul(out[:, 0:have], keys, qs, start=False, stop=True, skip_group_check=True)

            def stage(u):
                for what, n in events(windows, u):
                    if what == "A":
                        if n == 0:
                            pe.wait_ge(s_load[u.par], 80 * u.half + 80)
                        if u.after(1) or n >= 2:
                            pe.wait_ge(s["max"], u.slots(na, n - 1))
                        for t in query_slots(windows, u.hg)[n]:
                            mm = query_tile(u, u.slot_par(na, n), t)
                        mm.then_inc(s["scoresA"], 1)
                    elif what == "B":
                        v = u - 2
                        if n == 0:
                            pe.wait_ge(s["m_in"], 16 * v.value + 16)
                        if v.after(1) or n >= 2:
                            pe.wait_ge(s["exp"], v.slots(nb, n - 1))
                        for t in key_slots(windows, v.hg)[n]:
                            mm = key_tile(v, v.slot_par(nb, n), t)
                        mm.then_inc(s["scoresB"], 1)
                    elif what == "PV":
                        v = u - 3
                        pe.wait_ge(s["exp"], v.slots(nb, nb[v.hg]))
                        if v.after(1):
                            pe.wait_ge(s["outT"], v.value)
                        for j in range(TG):
                            for h in range(HG):
                                w = window(v, h)
                                have = min(P + w if w else S, S - P * j)
                                mm = pe.matmul(psO[VW * h:VW * (h + 1), P * j:P * j + have], vu[:, v.buf, j, h, :],
                                               prob[:, v.par, h, j, 0:have], start=(j == 0), stop=(j == TG - 1),
                                               tile_position=(0, VW * h), skip_group_check=True)
                        mm.then_inc(s["pv"], 1)
                    elif what == "TOP":
                        v = u - 1
                        pe.wait_ge(s["max"], v.slots(na, na[v.hg]))
                        if v.after(3):
                            pe.wait_ge(s["norm"], (v - 2).value)
                        pe.transpose(psM[0:HG * TG, 0:P], top[:, v.par].rearrange("p h t -> p (h t)"), ident[:]
                                     ).then_inc(s["topT_ps"], 1)
                    else:
                        v = u - 3
                        pe.wait_ge(s["outT"], v.value + 1)
                        w = u - 1 if (u - 1).exists() else Unit(NU - 1)
                        pe.wait_ge(s["topT"], MROWS * w.value + MROWS)
                        if v.after(1):
                            pe.wait_ge(s["norm"], v.value)
                        for i in range(TG):
                            mm = pe.transpose(psM[:, P * i:P * (i + 1)], outT[:, v.par, P * i:P * (i + 1)], ident[:])
                        mm.then_inc(s["turned"], 1)

            walk(pe, stage)

        @block.scalar
        def _(act):
            def stage(u):
                for what, n in events(windows, u):
                    if what == "B":
                        v = u - 2
                        if n == 0 and v.after(2):
                            act.wait_ge(s["pv"], (v - 1).value)
                        act.wait_ge(s["scoresB"], v.slots(nb, n + 1))
                        sl = key_slots(windows, v.hg)[n]
                        col, h, j, cols = sl[0]
                        bank = psB[:, v.slot_par(nb, n), :]
                        if len(sl) == 1:
                            src, dst = bank[:, 0:cols], prob[:, v.par, h, j, 0:cols]
                        else:
                            src = bank.rearrange("p (n q) -> p n q", q=512 // len(sl))[:, :, 0:cols]
                            dst = (prob[:, v.par, h:h + len(sl), j, 0:cols] if windows is None
                                   else prob[:, v.par, h, j:j + 2, 0:cols])
                        act.activation(dst, src, ACT.Exp, scale=0.25).then_inc(s["exp"], 1)
                    elif what == "PV":
                        v = u - 3
                        act.wait_ge(s["pv"], v.value + 1)
                        if v.after(2):
                            act.wait_ge(s["turned"], (v - 1).value)
                        act.copy(outT[:, v.par, :], psO[:]).then_inc(s["outT"], 1)
            walk(act, stage)

        @block.vector
        def _(dve):
            def stage(u):
                for what, n in events(windows, u):
                    if what == "A":
                        if n == 0 and u.after(2):
                            dve.wait_ge(s["topT_ps"], (u - 1).value)
                        dve.wait_ge(s["scoresA"], u.slots(na, n + 1))
                        sl = query_slots(windows, u.hg)[n]
                        bank, col, h, i, k0, cols = sl[0]
                        buf = psA[:, u.slot_par(na, n)]
                        same_head = windows is not None
                        dst = top[:, u.par, h, i:i + len(sl)] if same_head else top[:, u.par, h:h + len(sl), i]
                        if len(sl) == 1:
                            src = buf[:, 0:1, 0:cols]
                        elif len(sl) == 2:
                            src = buf[:, :, 0:cols]
                        elif cols == P and windows is None:
                            src = buf[:, 0, :].rearrange("p (h c) -> p h c", c=P)
                        else:
                            src = buf.rearrange("p b (i c) -> p (b i) c", c=256)[:, :, 0:cols]
                        dve.tensor_reduce(dst, src, AX.X, ALU.max).then_inc(s["max"], 1)
                    elif what == "TOP":
                        v = u - 1
                        dve.wait_ge(s["topT_ps"], v.value + 1)
                        if v.after(2):
                            dve.wait_ge(s["m_out"], 16 * (v - 1).value)
                        dve.tensor_copy(topT[:, v.par, 0, :], psM[0:HG * TG, 0:P]).then_inc(s["topT"], 1)
                        dve.wait_ge(s["topT"], MROWS * v.value + 1)
                        dve.tensor_tensor(topT[:, v.par, 1, :], psM[0:HG * TG, 0:P], topT[:, v.par, 0, :],
                                          ALU.subtract).then_inc(s["topT"], 1)
                    elif what == "OUT":
                        v = u - 3
                        dve.wait_ge(s["turned"], v.value + 1)
                        turned = psM[:].rearrange("p (t h c) -> p t h c", h=HG, c=VW)
                        per = 1 if windows is None else 2
                        dve.reciprocal(rec[:, v.par], turned[:, :, :, DK]).then_inc(s["rec"], 1)
                        dve.wait_ge(s["rec"], v.value * per + 1)
                        if windows is not None:
                            g = gates[:, bass.ds(v.seq * TG, TG), HG * v.hg:HG * v.hg + HG]
                            dve.tensor_tensor(rec[:, v.par], rec[:, v.par], g, ALU.mult).then_inc(s["rec"], 1)
                            dve.wait_ge(s["rec"], v.value * per + 2)
                        dst = attn[:, bass.ds(v.seq * TG, TG), HG * v.hg * DK:HG * (v.hg + 1) * DK]
                        dve.tensor_tensor(dst.rearrange("p t (h c) -> p t h c", c=DK), turned[:, :, :, 0:DK],
                                          rec[:, v.par].unsqueeze(3).to_broadcast([P, TG, HG, DK]),
                                          ALU.mult).then_inc(s["norm"], 1)

            walk(dve, stage)
            dve.wait_ge(s["norm"], NU)


def project_out(nc, tag, res, attn, ident, w_o, bias):
    with ExitStack() as ctx:
        k = Kit(nc, ctx, tag)
        ws = [load_split(k, "w_o", w_o, [P, KD, D])]
        xTh, xTl = k.sb("xTh", [P, 2, KD, S], F32R), k.sb("xTl", [P, 2, KD, S], F32R)
        bias_sb = k.sb("bias", [P, D])
        psT = k.ps("psT", [P, 2, KD, S])
        psY = k.ps("psY", [P, 4, 512])
        s = {n: k.sem(n) for n in "raw hi wt bias xT xTh xTl y res biased".split()}
        k.open()
        block = ctx.enter_context(nc.Block())

        @block.sync
        def _(sp):
            load_weights(sp, ws, s["raw"])
            if bias is not None:
                sp.dma_start(bias_sb[:], bias.partition_broadcast(P)).then_inc(s["bias"], 16)

        @block.gpsimd
        def _(pool):
            split_weights(pool, ws, s["raw"], s["hi"], s["wt"])

        @block.tensor
        def _(pe):
            def transposes(b):
                if b >= 2:
                    pe.wait_ge(s["xTl"], KD * (b - 1) + 1)
                for i in range(TG):
                    for c in range(KD):
                        mm = pe.transpose(psT[:, b % 2, c, P * i:P * (i + 1)],
                                          attn[:, TG * b + i, P * c:P * (c + 1)], ident[:])
                mm.then_inc(s["xT"], 1)

            transposes(0)
            pe.wait_ge(s["wt"], 2)
            for b in range(B):
                if b + 1 < B:
                    transposes(b + 1)
                pe.wait_ge(s["xTl"], KD * b + KD + 1)
                for i in range(TG):
                    m = TG * b + i
                    if m % 2 == 0 and m >= 8:
                        pe.wait_ge(s["res"], m // 2 - 2)
                    n = 0
                    for a, w in split_passes(xTh, xTl, ws[0]["hi"], ws[0]["lo"]):
                        for c in range(KD):
                            mm = pe.matmul(psY[:, m // 2 % 4, D * (m % 2):D * (m % 2 + 1)],
                                           a[:, b % 2, c, P * i:P * (i + 1)], w[:, c, :], start=(n == 0), stop=(n == 5))
                            n += 1
                    if m % 2:
                        mm.then_inc(s["y"], 1)

        @block.scalar
        def _(act):
            for b in range(B):
                act.wait_ge(s["xT"], b + 2)
                if b >= 2:
                    act.wait_ge(s["y"], 2 * (b - 1) + 1)
                for c in range(KD):
                    act.copy(xTh[:, b % 2, c, :], psT[:, b % 2, c, :]).then_inc(s["xTh"], 1)

        @block.vector
        def _(dve):
            if bias is not None:
                dve.wait_ge(s["bias"], 17)
                dve.tensor_tensor(res[:], res[:], bias_sb[:].unsqueeze(1).to_broadcast([P, NT, D]), ALU.add
                                  ).then_inc(s["biased"], 1)
                dve.wait_ge(s["biased"], 2)

            def add(b):
                for q in range(2):
                    m = 2 * b + q
                    dve.wait_ge(s["y"], m + 2)
                    dve.tensor_tensor(res[:, 2 * m:2 * m + 2, :], res[:, 2 * m:2 * m + 2, :],
                                      psY[:, m % 4, :].rearrange("p (t d) -> p t d", d=D), ALU.add).then_inc(s["res"], 1)

            for b in range(B):
                if b >= 2:
                    dve.wait_ge(s["y"], 2 * (b - 1) + 1)
                for c in range(KD):
                    dve.wait_ge(s["xTh"], KD * b + c + 2)
                    dve.tensor_tensor(xTl[:, b % 2, c, :], psT[:, b % 2, c, :], xTh[:, b % 2, c, :].bitcast(F32),
                                      ALU.subtract).then_inc(s["xTl"], 1)
                if b >= 1:
                    add(b - 1)
            add(B - 1)
            dve.wait_ge(s["res"], NT // 2 + 1)


class Router:

    weights_there = None

    def __init__(self, k, wr, experts):
        self.experts = experts
        self.w = load_split(k, "wr", wr, [P, KD, experts])
        self.logT = k.sb("logT", [P, S])
        self.log = k.sb("log", [P, NT, experts])
        self.best = k.sb("best", [P, NT, 8])
        self.place = k.sb("place", [P, NT, 8], U32)
        self.placef = k.sb("placef", [P, NT, 2])
        self.names = k.sb("names", [P, experts])
        self.gap = k.sb("gap", [P, NT])
        self.hot = k.sb("hot", [P, 2, NT, experts])
        self.ps = k.ps("psR", [P, 512])
        names = "logT_ps logT log_ps log best place placef names gap exp hot".split()
        self.s = {n: k.sem("router_" + n) for n in names}

    def pe_logits(self, pe, b, xh, xl):
        pe.wait_ge(*self.weights_there)
        pe.wait_ge(self.s["log"], b + 1)
        n = 0
        for w, x in split_passes(self.w["hi"], self.w["lo"], xh, xl):
            for c in range(KD):
                mm = pe.matmul(self.ps[0:self.experts, :], w[:, c, :], x[:, c, :], start=(n == 0), stop=(n == 5))
                n += 1
        mm.then_inc(self.s["logT_ps"], 1)

    def act_copy(self, act, b):
        act.wait_ge(self.s["names"], 3)
        act.wait_ge(self.s["logT_ps"], b + 2)
        act.copy(self.logT[0:self.experts, :], self.ps[0:self.experts, :]).then_inc(self.s["logT"], 1)

    def pe_turn(self, pe, b, ident):
        pe.wait_ge(*self.weights_there)
        pe.wait_ge(self.s["logT"], b + 2)
        for i in range(TG):
            mm = pe.transpose(self.ps[:, P * i:P * (i + 1)], self.logT[:, P * i:P * (i + 1)], ident[:])
        mm.then_inc(self.s["log_ps"], 1)

    def dve_logits(self, dve, b, bias=None):
        dve.wait_ge(self.s["log_ps"], b + 2)
        src = self.ps[:].rearrange("p (t c) -> p t c", c=P)[:, :, 0:self.experts]
        dst = self.log[:, bass.ds(TG * b, TG), :]
        if bias is None:
            dve.tensor_copy(dst, src).then_inc(self.s["log"], 1)
        else:
            dve.tensor_tensor(dst, src, bias[:].unsqueeze(1).to_broadcast([P, TG, self.experts]), ALU.add
                              ).then_inc(self.s["log"], 1)

    def pool_names(self, pool):
        pool.memset(self.logT[:], 0.0).then_inc(self.s["names"], 1)
        pool.iota(self.names[:], [[1, self.experts]], base=0, channel_multiplier=0,
                  allow_small_or_imprecise_dtypes=True).then_inc(self.s["names"], 1)

    def dve_pick(self, dve):
        dve.wait_ge(self.s["log"], B + 1)
        for t in range(NT):
            dve.max(self.best[:, t, :], self.log[:, t, :]).then_inc(self.s["best"], 1)
        dve.wait_ge(self.s["best"], NT + 1)
        dve.tensor_tensor(self.gap[:], self.best[:, :, 1], self.best[:, :, 0], ALU.subtract).then_inc(self.s["gap"], 1)
        for t in range(NT):
            dve.max_index(self.place[:, t, :], self.best[:, t, :], self.log[:, t, :]).then_inc(self.s["place"], 1)
        dve.wait_ge(self.s["place"], NT + 1)
        dve.tensor_copy(self.placef[:], self.place[:, :, 0:2]).then_inc(self.s["placef"], 1)
        dve.wait_ge(self.s["placef"], 2)
        dve.wait_ge(self.s["names"], 3)
        for n in range(2):
            dve.tensor_tensor(self.hot[:, n], self.names[:].unsqueeze(1).to_broadcast([P, NT, self.experts]),
                              self.placef[:, :, n:n + 1].to_broadcast([P, NT, self.experts]), ALU.is_equal
                              ).then_inc(self.s["hot"], 1)
        dve.wait_ge(self.s["exp"], 2)
        dve.wait_ge(self.s["hot"], 3)

    def act_exp(self, act):
        act.wait_ge(self.s["gap"], 2)
        act.activation(self.gap[:], self.gap[:], ACT.Exp).then_inc(self.s["exp"], 1)


class Turn:

    def __init__(self, k):
        self.norm = Norm(k)
        self.xn = k.sb("xn", [P, TG, D])
        self.ps = k.ps("psT", [P, KD, S])
        self.s = {n: k.sem(n) for n in "xn xT xTh xTl".split()}

    def dve_norm(self, dve, res, b):
        dve.wait_ge(self.s["xT"], b + 1)
        for i in range(TG):
            self.norm.apply(dve, self.xn[:, i, :], res, TG * b + i).then_inc(self.s["xn"], 1)

    def pe(self, pe, b, ident):
        pe.wait_ge(self.s["xn"], TG * b + TG + 1)
        pe.wait_ge(self.s["xTl"], KD * b + 1)
        for i in range(TG):
            for c in range(KD):
                mm = pe.transpose(self.ps[:, c, P * i:P * (i + 1)], self.xn[:, i, P * c:P * (c + 1)], ident[:])
        mm.then_inc(self.s["xT"], 1)

    def act_hi(self, act, b, xh):
        act.wait_ge(self.s["xT"], b + 2)
        for c in range(KD):
            act.copy(xh[:, c, bass.ds(b * S, S)], self.ps[:, c, :]).then_inc(self.s["xTh"], 1)

    def dve_lo(self, dve, b, xh, xl):
        for c in range(KD):
            dve.wait_ge(self.s["xTh"], KD * b + c + 2)
            dve.tensor_tensor(xl[:, c, bass.ds(b * S, S)], self.ps[:, c, :],
                              xh[:, c, bass.ds(b * S, S)].bitcast(F32), ALU.subtract).then_inc(self.s["xTl"], 1)


def ffn_sq(nc, a, res, ident):
    with ExitStack() as ctx:
        k = Kit(nc, ctx, "ffn0")
        xh, xl = k.sb("xh", [P, KD, B * S], F32R), k.sb("xl", [P, KD, B * S], F32R)
        share = k.sb("share", [P, NT, E0])
        any_sb = k.sb("any_sb", [1, 1], I32)
        with ExitStack() as ctx2:
            k2 = Kit(nc, ctx2, "ffn0a")
            turn, router = Turn(k2), Router(k2, a["wr0"], E0)
            ws = [load_split(k2, "ws1", a["ws1"], [P, KD, F0]), load_split(k2, "ws2", a["ws2"], [P, 1, D]), router.w]
            relu, act_f = k2.sb("relu", [P, S]), k2.sb("act_f", [P, S])
            act_h, act_l = k2.sb("act_h", [P, S], F32R), k2.sb("act_l", [P, S], F32R)
            lost, most = k2.sb("lost", [P, NT]), k2.sb("most", [P, 1])
            any_f = k2.sb("any_f", [1, 1])
            psH = k2.ps("psH", [P, S])
            psY = k2.ps("psY", [P, 2, 512])
            s = {n: k2.sem(n) for n in "raw hi wt hid relu act acth actl y res lost share most mostT any".split()}
            router.weights_there = s["wt"], len(ws) + 1
            k2.open()
            block = ctx2.enter_context(nc.Block())

            @block.sync
            def _(sp):
                load_weights(sp, ws, s["raw"])

            @block.gpsimd
            def _(pool):
                split_weights(pool, ws, s["raw"], s["hi"], s["wt"])
                router.pool_names(pool)

                def body(b, last):
                    pool.wait_ge(s["acth"], b + 2)
                    pool.wait_ge(s["y"], 2 * b + 1)
                    pool.tensor_tensor(act_l[:], act_f[:], act_h[:].bitcast(F32), ALU.subtract).then_inc(s["actl"], 1)
                looped(pool, B, body)

            @block.tensor
            def _(pe):
                pe.wait_ge(s["wt"], len(ws) + 1)
                turn.pe(pe, 0, ident)

                def body(b, last):
                    pe.wait_ge(turn.s["xTl"], KD * b + KD + 1)
                    gh, gl = (x[:, :, bass.ds(b * S, S)] for x in (xh, xl))
                    pe.wait_ge(s["relu"], b + 1)
                    n = 0
                    for w, x in split_passes(ws[0]["hi"], ws[0]["lo"], gh, gl):
                        for c in range(KD):
                            mm = pe.matmul(psH[:], w[:, c, :], x[:, c, :], start=(n == 0), stop=(n == 5))
                            n += 1
                    mm.then_inc(s["hid"], 1)
                    router.pe_logits(pe, b, gh, gl)
                    if not last:
                        turn.pe(pe, b + 1, ident)
                    router.pe_turn(pe, b, ident)
                    pe.wait_ge(s["actl"], b + 2)
                    for q in range(2):
                        pe.wait_ge(s["res"], (2 * b + q - 1 if q else 2 * b) + 1)
                        for i in (2 * q, 2 * q + 1):
                            for n, (x, w) in enumerate(split_passes(act_h, act_l, ws[1]["hi"], ws[1]["lo"])):
                                mm = pe.matmul(psY[:, q, D * (i % 2):D * (i % 2 + 1)], x[:, P * i:P * (i + 1)],
                                               w[:, 0, :], start=(n == 0), stop=(n == 2))
                        mm.then_inc(s["y"], 1)
                looped(pe, B, body)
                pe.wait_ge(s["most"], 2)
                pe.transpose(router.ps[0:1, 0:P], most[:], ident[:]).then_inc(s["mostT"], 1)

            @block.scalar
            def _(act):
                turn.norm.scalar(act)

                def body(b, last):
                    turn.act_hi(act, b, xh)
                    act.wait_ge(s["hid"], b + 2)
                    act.wait_ge(s["act"], b + 1)
                    act.activation(relu[:], psH[:], ACT.Relu).then_inc(s["relu"], 1)
                    act.wait_ge(s["act"], b + 2)
                    act.wait_ge(s["y"], 2 * b + 1)
                    act.copy(act_h[:], act_f[:]).then_inc(s["acth"], 1)
                    router.act_copy(act, b)
                looped(act, B, body)
                router.act_exp(act)

            @block.vector
            def _(dve):
                turn.norm.vector(dve, res)
                turn.dve_norm(dve, res, 0)

                def body(b, last):
                    turn.dve_lo(dve, b, xh, xl)
                    if not last:
                        turn.dve_norm(dve, res, b + 1)
                    dve.wait_ge(s["relu"], b + 2)
                    dve.wait_ge(s["actl"], b + 1)
                    dve.tensor_tensor(act_f[:], relu[:], relu[:], ALU.mult).then_inc(s["act"], 1)
                    router.dve_logits(dve, b)
                    for q in range(2):
                        dve.wait_ge(s["y"], 2 * b + q + 2)
                        r = res[:, bass.ds(TG * b + 2 * q, 2), :]
                        dve.tensor_tensor(r, r, psY[:, q, :].rearrange("p (t d) -> p t d", d=D), ALU.add
                                          ).then_inc(s["res"], 1)
                looped(dve, B, body)
                router.dve_pick(dve)
                dve.tensor_scalar(lost[:], router.gap[:], 1.0, 1.0, ALU.add, ALU.is_le).then_inc(s["lost"], 1)
                dve.wait_ge(s["lost"], 2)
                dve.tensor_tensor(share[:], router.hot[:, 0], lost[:].unsqueeze(2).to_broadcast([P, NT, E0]),
                                  ALU.mult).then_inc(s["share"], 1)
                dve.tensor_reduce(most[:], lost[:], AX.X, ALU.max).then_inc(s["most"], 1)
                dve.wait_ge(s["mostT"], 2)
                dve.tensor_reduce(any_f[:], router.ps[0:1, 0:P], AX.X, ALU.max).then_inc(s["any"], 1)
                dve.wait_ge(s["any"], 2)
                dve.tensor_copy(any_sb[:], any_f[:]).then_inc(s["any"], 1)
                dve.wait_ge(s["any"], 3)
                dve.wait_ge(s["share"], 2)
        ffn_sq_routed(nc, a, res, xh, xl, share, any_sb)


def ffn_sq_routed(nc, a, res, xh, xl, share, any_sb):
    with ExitStack() as ctx:
        k = Kit(nc, ctx, "ffn0b")
        w1 = load_split(k, "w1", None, [P, KD, F0])
        w2 = load_split(k, "w2", None, [P, 1, D])
        ws = (w1, w2)
        relu, act_f = k.sb("relu", [P, S]), k.sb("act_f", [P, S])
        act_h, act_l = k.sb("act_h", [P, S], F32R), k.sb("act_l", [P, S], F32R)
        psH = k.ps("psH", [P, S])
        psY = k.ps("psY", [P, TG, 512])
        one = k.sb("one", [P, 1])
        s = {n: k.sem(n) for n in "one raw hi wt hid relu act acth actl y res".split()}
        k.open()
        block = ctx.enter_context(nc.Block())
        last_b = B - 1

        def routed(eng, body):
            there = eng.value_load(any_sb[0:1, 0:1], min_val=0, max_val=1)
            with eng.If(there):
                body()

        @block.sync
        def _(sp):
            def run():
                with sp.Fori(0, E0) as e:
                    sp.wait_ge(s["wt"], 2 * e + 1)
                    sp.dma_start(w1["raw"][:], a["w1_0"][bass.ds(e, 1)].rearrange("o p k f -> p (o k) f")
                                 ).then_inc(s["raw"], 16)
                    sp.dma_start(w2["raw"][:], a["w2_0"][bass.ds(e, 1)].rearrange("o f d -> f o d")
                                 ).then_inc(s["raw"], 16)
            routed(sp, run)

        @block.gpsimd
        def _(pool):
            def run():
                pool.memset(one[:], 1.0).then_inc(s["one"], 1)
                pool.wait_ge(s["one"], 2)
                with pool.Fori(0, E0) as e:
                    pool.wait_ge(s["raw"], 32 * e + 33)
                    pool.wait_ge(s["y"], B * e + 1)
                    for n, w in enumerate(ws):
                        pool.tensor_tensor(w["hi"][:], w["raw"][:], one[:].unsqueeze(2).to_broadcast(w["raw"].shape), ALU.mult).then_inc(s["hi"], 1)
                    for n, w in enumerate(ws):
                        pool.wait_ge(s["hi"], 2 * e + n + 2)
                        pool.tensor_tensor(w["lo"][:], w["raw"][:], w["hi"][:].bitcast(F32), ALU.subtract
                                           ).then_inc(s["wt"], 1)
                    with pool.Fori(0, B) as b:
                        pool.wait_ge(s["acth"], e * B + b + 2)
                        pool.tensor_tensor(act_l[:], act_f[:], act_h[:].bitcast(F32), ALU.subtract
                                           ).then_inc(s["actl"], 1)
            routed(pool, run)

        @block.tensor
        def _(pe):
            def run():
                with pe.Fori(0, E0) as e:
                    with pe.Fori(0, B) as b:
                        pe.wait_ge(s["wt"], 2 * e + 3)
                        pe.wait_ge(s["relu"], e * B + b + 1)
                        n = 0
                        for w, x in split_passes(w1["hi"], w1["lo"], xh, xl):
                            for c in range(KD):
                                mm = pe.matmul(psH[:], w[:, c, :], x[:, c, bass.ds(b * S, S)], start=(n == 0), stop=(n == 5))
                                n += 1
                        mm.then_inc(s["hid"], 1)
                        pe.wait_ge(s["actl"], e * B + b + 2)
                        pe.wait_ge(s["res"], TG * (e * B + b) + 1)
                        for i in range(TG):
                            for n, (x, w) in enumerate(split_passes(act_h, act_l, w2["hi"], w2["lo"])):
                                mm = pe.matmul(psY[:, i, 0:D], x[:, P * i:P * (i + 1)], w[:, 0, :],
                                               start=(n == 0), stop=(n == 2))
                        mm.then_inc(s["y"], 1)
            routed(pe, run)

        @block.scalar
        def _(act):
            def run():
                with act.Fori(0, E0) as e:
                    with act.Fori(0, B) as b:
                        act.wait_ge(s["hid"], e * B + b + 2)
                        act.activation(relu[:], psH[:], ACT.Relu).then_inc(s["relu"], 1)
                        act.wait_ge(s["act"], e * B + b + 2)
                        act.wait_ge(s["y"], e * B + b + 1)
                        act.copy(act_h[:], act_f[:]).then_inc(s["acth"], 1)
            routed(act, run)

        @block.vector
        def _(dve):
            def run():
                with dve.Fori(0, E0) as e:
                    with dve.Fori(0, B) as b:
                        dve.wait_ge(s["relu"], e * B + b + 2)
                        dve.wait_ge(s["actl"], e * B + b + 1)
                        dve.tensor_tensor(act_f[:], relu[:], relu[:], ALU.mult).then_inc(s["act"], 1)
                        dve.wait_ge(s["y"], e * B + b + 2)
                        dve.wait_ge(s["res"], TG * (e * B + b) + 1)
                        for i in range(TG):
                            r = res[:, b * TG + i, :]
                            dve.scalar_tensor_tensor(r, psY[:, i, 0:D], share[:, b * TG + i, bass.ds(e, 1)], r,
                                                     ALU.mult, ALU.add).then_inc(s["res"], 1)
                dve.wait_ge(s["res"], TG * E0 * B + 1)
            routed(dve, run)


def ffn_swiglu(nc, a, res, ident):
    TT = 256
    NTT = B * S // TT
    with ExitStack() as ctx:
        k = Kit(nc, ctx, "ffn1")
        xh, xl = k.sb("xh", [P, KD, B * S], F32R), k.sb("xl", [P, KD, B * S], F32R)
        share = k.sb("share", [P, NT, E1N + 1])
        with ExitStack() as ctx2:
            k2 = Kit(nc, ctx2, "ffn1a")
            turn, router = Turn(k2), Router(k2, a["wr1"], E1N)
            bias = k2.sb("bias", [P, E1N])
            first, second = k2.sb("first", [P, NT]), k2.sb("second", [P, NT])
            part = k2.sb("part", [P, 2, NT, E1N])
            s = {n: k2.sem(n) for n in "raw hi wt bias share".split()}
            router.weights_there = s["wt"], 2
            k2.open()
            block = ctx2.enter_context(nc.Block())

            @block.sync
            def _(sp):
                load_weights(sp, [router.w], s["raw"])
                sp.dma_start(bias[:], a["br1"].partition_broadcast(P)).then_inc(s["bias"], 16)

            @block.gpsimd
            def _(pool):
                split_weights(pool, [router.w], s["raw"], s["hi"], s["wt"])
                router.pool_names(pool)

            @block.tensor
            def _(pe):
                pe.wait_ge(s["wt"], 2)
                turn.pe(pe, 0, ident)

                def body(b, last):
                    pe.wait_ge(turn.s["xTl"], KD * b + KD + 1)
                    gh, gl = (x[:, :, bass.ds(b * S, S)] for x in (xh, xl))
                    router.pe_logits(pe, b, gh, gl)
                    if not last:
                        turn.pe(pe, b + 1, ident)
                    router.pe_turn(pe, b, ident)
                looped(pe, B, body)

            @block.scalar
            def _(act):
                turn.norm.scalar(act)

                def body(b, last):
                    turn.act_hi(act, b, xh)
                    router.act_copy(act, b)
                looped(act, B, body)
                router.act_exp(act)

            @block.vector
            def _(dve):
                turn.norm.vector(dve, res)
                dve.wait_ge(s["bias"], 17)
                turn.dve_norm(dve, res, 0)

                def body(b, last):
                    turn.dve_lo(dve, b, xh, xl)
                    if not last:
                        turn.dve_norm(dve, res, b + 1)
                    router.dve_logits(dve, b, bias)
                looped(dve, B, body)
                router.dve_pick(dve)
                dve.tensor_scalar(first[:], router.gap[:], 1.0, None, ALU.add).then_inc(s["share"], 1)
                dve.wait_ge(s["share"], 2)
                dve.reciprocal(first[:], first[:]).then_inc(s["share"], 1)
                dve.wait_ge(s["share"], 3)
                dve.tensor_tensor(second[:], router.gap[:], first[:], ALU.mult).then_inc(s["share"], 1)
                dve.wait_ge(s["share"], 4)
                for n, w in enumerate((first, second)):
                    dve.tensor_tensor(part[:, n], router.hot[:, n], w[:].unsqueeze(2).to_broadcast([P, NT, E1N]),
                                      ALU.mult).then_inc(s["share"], 1)
                dve.memset(share[:, :, E1N:E1N + 1], 1.0).then_inc(s["share"], 1)
                dve.wait_ge(s["share"], 7)
                dve.tensor_tensor(share[:, :, 0:E1N], part[:, 0], part[:, 1], ALU.add).then_inc(s["share"], 1)
                dve.wait_ge(s["share"], 8)

        ctx.enter_context(ExitStack())
        kb = Kit(nc, ctx, "ffn1b")
        raw13 = kb.sb("raw13", [P, 2, KD, F1])
        raw2 = kb.sb("raw2", [P, HB, D])
        w13 = [kb.sb("w13_hi", [P, 2, 2, KD, F1], F32R), kb.sb("w13_lo", [P, 2, 2, KD, F1], F32R)]
        w2 = [kb.sb("w2_hi", [P, 2, HB, D], F32R), kb.sb("w2_lo", [P, 2, HB, D], F32R)]
        sil = kb.sb("sil", [P, 2, TT])
        act_f = kb.sb("act_f", [P, 2, TT])
        act_h, act_l = kb.sb("act_h", [P, 2, HB, TT], F32R), kb.sb("act_l", [P, 2, HB, TT], F32R)
        psG = kb.ps("psG", [P, 2, 2, 512])
        psY = kb.ps("psY", [P, 2, 512])
        one = kb.sb("one", [P, 1])
        s = {n: kb.sem(n) for n in "one raw hi wt gate sil act acth actl y res".split()}
        NE = E1N + 1
        kb.open()
        block = ctx.enter_context(nc.Block())

        def experts(eng, body):
            with eng.Fori(0, E1N // 2) as i:
                body(2 * i, 0)
                body(2 * i + 1, 1)
            body(E1N, 0)

        def tiles(eng, e, body):
            with eng.Fori(0, NTT // 2) as i:
                for n in range(2):
                    body(2 * i + n, n, e * NTT + 2 * i + n)

        @block.sync
        def _(sp):
            def body(e, par):
                sp.wait_ge(s["wt"], 2 * e + 1)
                sp.dma_start(raw13[:].rearrange("p a k f -> p (a k f)"),
                             a["w13"][bass.ds(e, 1)].rearrange("o p a k f -> p (o a k f)")).then_inc(s["raw"], 16)
                sp.dma_start(raw2[:].rearrange("p h d -> p (h d)"),
                             a["w2_1"][bass.ds(e, 1)].rearrange("o p h d -> p (o h d)")).then_inc(s["raw"], 16)
            experts(sp, body)

        @block.gpsimd
        def _(pool):
            for name, n in (("act", 1), ("actl", 1), ("res", 2), ("y", 1)):
                pool.sem_inc(s[name], n)

            def split(e, par, first=False):
                pool.wait_ge(s["raw"], 32 * e + 33)
                if not first:
                    pool.wait_ge(s["y"], (e - 1) * NTT + 2)
                pool.tensor_tensor(w13[0][:, par], raw13[:], one[:].unsqueeze(2).unsqueeze(3).to_broadcast([P, 2, KD, F1]),
                                   ALU.mult).then_inc(s["hi"], 1)
                pool.tensor_tensor(w2[0][:, par], raw2[:], one[:].unsqueeze(2).to_broadcast([P, HB, D]), ALU.mult
                                   ).then_inc(s["hi"], 1)
                pool.wait_ge(s["hi"], 2 * e + 2)
                pool.tensor_tensor(w13[1][:, par], raw13[:], w13[0][:, par].bitcast(F32), ALU.subtract
                                   ).then_inc(s["wt"], 1)
                pool.wait_ge(s["hi"], 2 * e + 3)
                pool.tensor_tensor(w2[1][:, par], raw2[:], w2[0][:, par].bitcast(F32), ALU.subtract
                                   ).then_inc(s["wt"], 1)

            def low_parts(e, par):
                def body(i, ip, m):
                    for hb in range(HB):
                        n = HB * m + hb
                        pool.wait_ge(s["acth"], n + 2)
                        pool.tensor_tensor(act_l[:, ip, hb, :], act_f[:, hb % 2, :],
                                           act_h[:, ip, hb, :].bitcast(F32), ALU.subtract).then_inc(s["actl"], 1)
                tiles(pool, e, body)

            pool.memset(one[:], 1.0).then_inc(s["one"], 1)
            pool.wait_ge(s["one"], 2)
            split(0, 0, first=True)
            with pool.Fori(0, E1N // 2) as i:
                split(2 * i + 1, 1, first=False)
                low_parts(2 * i, 0)
                split(2 * i + 2, 0)
                low_parts(2 * i + 1, 1)
            low_parts(E1N, 0)

        @block.tensor
        def _(pe):
            def body(e, par):
                pe.wait_ge(s["wt"], 2 * e + 3)

                def hidden(i, ip, m):
                    for hb in range(HB):
                        n = HB * m + hb
                        pe.wait_ge(s["act"], n + 1)
                        cols = slice(P * hb, P * (hb + 1))
                        for g in range(2):
                            q = 0
                            for w, x in split_passes(w13[0], w13[1], xh, xl):
                                for c in range(KD):
                                    mm = pe.matmul(psG[:, hb % 2, g, 0:TT], w[:, par, g, c, cols],
                                                   x[:, c, bass.ds(i * TT, TT)], start=(q == 0), stop=(q == 5))
                                    q += 1
                            mm.then_inc(s["gate"], 1)

                def down(ip, m):
                    pe.wait_ge(s["actl"], HB * m + HB + 2)
                    pe.wait_ge(s["res"], 2 * m + 1)
                    for t in range(2):
                        q = 0
                        for x, w in split_passes(act_h, act_l, w2[0], w2[1]):
                            for hb in range(HB):
                                mm = pe.matmul(psY[:, ip, D * t:D * (t + 1)], x[:, ip, hb, P * t:P * (t + 1)],
                                               w[:, par, hb, :], start=(q == 0), stop=(q == 3 * HB - 1))
                                q += 1
                    mm.then_inc(s["y"], 1)

                m0 = e * NTT
                hidden(0, 0, m0)
                with pe.Fori(0, NTT // 2 - 1) as i:
                    hidden(2 * i + 1, 1, m0 + 2 * i + 1)
                    down(0, m0 + 2 * i)
                    hidden(2 * i + 2, 0, m0 + 2 * i + 2)
                    down(1, m0 + 2 * i + 1)
                hidden(NTT - 1, 1, m0 + NTT - 1)
                down(0, m0 + NTT - 2)
                down(1, m0 + NTT - 1)
            experts(pe, body)

        @block.scalar
        def _(act):
            def body(e, par):
                def tile(i, ip, m):
                    for hb in range(HB):
                        n = HB * m + hb
                        act.wait_ge(s["gate"], 2 * n + 2)
                        act.wait_ge(s["act"], n + 1)
                        act.activation(sil[:, hb % 2, :], psG[:, hb % 2, 0, 0:TT], ACT.Silu).then_inc(s["sil"], 1)
                        act.wait_ge(s["act"], n + 3)
                        if hb == 0:
                            act.wait_ge(s["y"], m + 1)
                        act.copy(act_h[:, ip, hb, :], act_f[:, hb % 2, :]).then_inc(s["acth"], 1)
                tiles(act, e, tile)
            experts(act, body)

        @block.vector
        def _(dve):
            def body(e, par):
                def gated(i, ip, m):
                    for hb in range(HB):
                        n = HB * m + hb
                        dve.wait_ge(s["gate"], 2 * n + 3)
                        dve.wait_ge(s["sil"], n + 2)
                        dve.wait_ge(s["actl"], n + 1)
                        dve.tensor_tensor(act_f[:, hb % 2, :], psG[:, hb % 2, 1, 0:TT], sil[:, hb % 2, :], ALU.mult
                                          ).then_inc(s["act"], 1)

                def add(i, ip, m):
                    dve.wait_ge(s["y"], m + 3)
                    for t in range(2):
                        r = res[:, 2 * i + t, :]
                        if isinstance(e, int):
                            w = share[:, 2 * i + t, e:e + 1]
                        else:
                            w = share[:, 2 * i + t, bass.ds(e, 1)]
                        dve.scalar_tensor_tensor(r, psY[:, ip, D * t:D * (t + 1)], w, r, ALU.mult, ALU.add
                                                 ).then_inc(s["res"], 1)

                m0 = e * NTT
                gated(0, 0, m0)
                with dve.Fori(0, NTT // 2 - 1) as i:
                    gated(2 * i + 1, 1, m0 + 2 * i + 1)
                    add(2 * i, 0, m0 + 2 * i)
                    gated(2 * i + 2, 0, m0 + 2 * i + 2)
                    add(2 * i + 1, 1, m0 + 2 * i + 1)
                gated(NTT - 1, 1, m0 + NTT - 1)
                add(NTT - 2, 0, m0 + NTT - 2)
                add(NTT - 1, 1, m0 + NTT - 1)
                dve.wait_ge(s["res"], 2 * (m0 + NTT) + 3)
            experts(dve, body)


def tower(nc, a):
    out = a["out"]
    Kit.used.clear()
    with ExitStack() as ctx:
        k = Kit(nc, ctx, "m")
        res = k.sb("res", [P, NT, D])
        ident = k.sb("ident", [P, P])
        s_id = k.sem("ident")
        s_rows = ctx.enter_context(nc.semaphore("gathered"))
        q_dram = nc.dram_tensor("q_parts", (B, H, KROWS, S), BF16).ap()
        k_dram = nc.dram_tensor("k_parts", (B, H, 3 * DK, S), BF16).ap()
        v_dram = nc.dram_tensor("v_rows", (B, S, H * VW), F32).ap()
        m_dram = nc.dram_tensor("maxima", (2, MROWS, HG * S), BF16).ap()
        with nc.Block() as block:
            @block.gpsimd
            def _(pool):
                pool.memset(ident[:], 0.0).then_inc(s_id, 1)
                pool.wait_ge(s_id, 1)
                pool.affine_select(out=ident[:], in_=ident[:], compare_op=ALU.not_equal, fill=1.0, base=0,
                                   pattern=[[-1, P]], channel_multiplier=1).then_inc(s_id, 1)
                pool.wait_ge(s_id, 2)
        embed(nc, res, ident, s_rows, a["ids"], a["E1"], a["tok_w2t"], a["b2"], a["pos"])
        with nc.sbuf_tensor("attn0", [P, NT, D], F32) as attn:
            project_qkv(nc, "qkv0", res, ident, a["w_qk0"], a["w_v0"], None, (a["cos"], a["sin"]), None, None,
                    q_dram, k_dram, v_dram, None)
            attend(nc, "att0", None, q_dram, k_dram, v_dram, m_dram, ident, None, attn)
            project_out(nc, "out0", res, attn, ident, a["w_o0"], None)
        ffn_sq(nc, a, res, ident)
        Kit.used.remove(s_id)
        clear_semaphores(nc)
        with nc.sbuf_tensor("attn1", [P, NT, D], F32) as attn, nc.sbuf_tensor("gates", [P, NT, H], F32) as gates:
            project_qkv(nc, "qkv1", res, ident, a["w_qk1"], None, a["bqk"], None, a["w_g1"], a["bgate"],
                    q_dram, k_dram, v_dram, gates)
            attend(nc, "att1", WINDOWS, q_dram, k_dram, v_dram, m_dram, ident, gates, attn)
            project_out(nc, "out1", res, attn, ident, a["w_o1"], a["bproj"])
        ffn_swiglu(nc, a, res, ident)
        s_out = k.sem("out")
        with nc.Block() as block:
            @block.sync
            def _(sp):
                sp.dma_start(out.rearrange("b (t p) d -> p (b t) d", p=P), res[:]).then_inc(s_out, 16)
                sp.wait_ge(s_out, 16)


def host_layout(np, x, L0_tok_E1, L0_tok_W2, L0_tok_b2, L0_tok_pos_emb, L0_attn_W_Q, L0_attn_W_K, L0_attn_W_V,
                L0_attn_W_O, L0_ffn_Ws1, L0_ffn_Ws2, L0_ffn_W1, L0_ffn_W2, L0_ffn_Wr, L1_attn_Wqk, L1_attn_bqk,
                L1_attn_Wgate, L1_attn_bgate, L1_attn_Wproj, L1_attn_bproj, L1_ffn_router_w, L1_ffn_experts_bias,
                L1_ffn_w1, L1_ffn_w3, L1_ffn_w2, L1_ffn_sw1, L1_ffn_sw3, L1_ffn_sw2):
    c = np.ascontiguousarray

    def rows(w):
        return c(w.reshape(-1, P, w.shape[-1]).transpose(1, 0, 2))

    theta = (1.0 / np.float32(10000.0) ** (np.arange(0, DK, 2, dtype=np.float32) / np.float32(DK))).astype(np.float32)
    ang = np.outer(np.arange(S, dtype=np.float32), theta).astype(np.float32)
    cos, sin = np.cos(ang), np.sin(ang)
    place = lambda t: c(t.reshape(TG, P, DK).transpose(1, 0, 2).astype(np.float32))
    return dict(
        ids=c(x.reshape(NT, P).T), E1=L0_tok_E1, tok_w2t=c(L0_tok_W2.T), b2=L0_tok_b2, pos=L0_tok_pos_emb,
        cos=place(np.concatenate([cos, cos], 1)), sin=place(np.concatenate([-sin, sin], 1)),
        w_qk0=rows(np.concatenate([L0_attn_W_Q.T, L0_attn_W_K.T], 1)), w_v0=rows(L0_attn_W_V.T),
        w_o0=rows(L0_attn_W_O.T),
        ws1=rows(L0_ffn_Ws1), ws2=rows(L0_ffn_Ws2),
        wr0=rows(L0_ffn_Wr), w1_0=c(L0_ffn_W1.reshape(E0, KD, P, F0).transpose(0, 2, 1, 3)), w2_0=L0_ffn_W2,
        w_qk1=rows(L1_attn_Wqk), bqk=L1_attn_bqk, w_g1=rows(L1_attn_Wgate), bgate=L1_attn_bgate,
        w_o1=rows(L1_attn_Wproj), bproj=L1_attn_bproj,
        wr1=rows(L1_ffn_router_w.T), br1=L1_ffn_experts_bias,
        w13=c(np.stack([np.concatenate([L1_ffn_w1, L1_ffn_sw1]), np.concatenate([L1_ffn_w3, L1_ffn_sw3])], 1)
              .reshape(E1N + 1, 2, KD, P, F1).transpose(0, 3, 1, 2, 4)),
        w2_1=c(np.concatenate([L1_ffn_w2, L1_ffn_sw2]).reshape(E1N + 1, HB, P, D).transpose(0, 2, 1, 3)),
    )


def kernel(**inputs):
    import numpy as np
    import concourse.bacc as bacc
    from concourse.bass_utils import run_bass_kernel_spmd

    arrays = {f"in_{name}": np.ascontiguousarray(x) for name, x in host_layout(np, **inputs).items()}
    nc = bacc.Bacc("TRN2", target_bir_lowering=False, num_devices=1)
    a = {name[3:]: nc.dram_tensor(name, x.shape, mybir.dt.from_np(x.dtype), kind="ExternalInput").ap()
         for name, x in arrays.items()}
    a["out"] = nc.dram_tensor("out_0", (B, S, D), F32, kind="ExternalOutput").ap()
    tower(nc, a)
    r = run_bass_kernel_spmd(nc, [arrays], core_ids=[0])
    return r.results[0]["out_0"]
```

```python
from contextlib import ExitStack

import concourse.bass as bass
from concourse import mybir

P = 128
F32 = mybir.dt.float32
F32R = mybir.dt.float32r
BF16 = mybir.dt.bfloat16
I32 = mybir.dt.int32
U32 = mybir.dt.uint32
ALU = mybir.AluOpType
ACT = mybir.ActivationFunctionType
AX = mybir.AxisListType

B, S, D = 8, 512, 256
NT = B * S // P
TG = S // P
KD = D // P
RANK = 32
H, DK = 16, 16
HG = 4
NHG = H // HG
VW = 32
TERMS_Q = (0, 0, 0, 1, 1, 2)
TERMS_K = (0, 1, 2, 0, 1, 0)
NTERM = len(TERMS_Q)
KROWS = NTERM * DK
MROWS = 2
EPS = 1e-5
MASKED = -1e30
E0, F0 = 8, 128
E1N, F1 = 8, 512
HB = F1 // P
WINDOWS = [max(4, 256 // 2 ** h) for h in range(H)]


class Kit:

    used = []

    def __init__(self, nc, ctx, tag):
        self.nc, self.ctx, self.tag = nc, ctx, tag
        self.sems = []

    def sb(self, name, shape, dt=F32):
        return self.ctx.enter_context(self.nc.sbuf_tensor(f"{self.tag}_{name}", shape, dt))

    def ps(self, name, shape, dt=F32):
        return self.ctx.enter_context(self.nc.psum_tensor(f"{self.tag}_{name}", shape, dt))

    def sem(self, name):
        handle = self.ctx.enter_context(self.nc.semaphore(f"{self.tag}_{name}"))
        Kit.used.append(handle)
        self.sems.append(handle)
        return handle

    def open(self, more=()):
        with self.nc.Block() as block:
            @block.gpsimd
            def _(pool):
                for handle in self.sems:
                    pool.sem_inc(handle, 1)
                for handle, n in more:
                    pool.sem_inc(handle, n)


def clear_semaphores(nc):
    numbers = sorted({h.num for h in Kit.used})
    Kit.used.clear()
    with nc.Block() as block:
        @block.gpsimd
        def _(pool):
            first = 0
            for n in range(1, len(numbers) + 1):
                if n == len(numbers) or numbers[n] != numbers[n - 1] + 1:
                    pool.sem_clear(range(numbers[first], numbers[n - 1] + 1))
                    first = n


def looped(eng, n, body):
    with eng.Fori(0, n - 1) as i:
        body(i, False)
    body(n - 1, True)


def split_passes(hi_a, lo_a, hi_b, lo_b):
    return ((hi_a, hi_b), (hi_a, lo_b), (lo_a, hi_b))


def embed(nc, res, ident, s_rows, ids, E1, w2t, b2, pos):
    with ExitStack() as ctx:
        k = Kit(nc, ctx, "emb")
        ids_sb = k.sb("ids", [P, NT], I32)
        rows = k.sb("rows", [P, NT, RANK])
        rowsT = k.sb("rowsT", [P, NT // TG, P])
        w_blk = k.sb("w_blk", [P, TG, D])
        posb = k.sb("posb", [P, TG, D])
        b2b = k.sb("b2b", [P, D])
        psT = k.ps("psT", [P, 2, 512])
        psO = k.ps("psO", [P, 4, 512])
        s_ids, s_w, s_pos = (k.sem(n) for n in ("ids", "w", "pos"))
        s_zero, s_bias, s_T, s_Tc, s_mm, s_res = (k.sem(n) for n in ("zero", "bias", "T", "Tc", "mm", "res"))
        block = ctx.enter_context(nc.Block())
        NG = NT // TG

        @block.sync
        def _(sp):
            sp.dma_start(ids_sb[:], ids).then_inc(s_ids, 16)
            sp.dma_start(posb[:], pos.rearrange("o (t p) d -> p (o t) d", p=P)).then_inc(s_pos, 16)
            sp.dma_start(b2b[:], b2.partition_broadcast(P)).then_inc(s_pos, 16)
            sp.wait_ge(s_zero, 1)
            for j in range(TG):
                sp.dma_start(w_blk[RANK * j:RANK * (j + 1), j, :], w2t).then_inc(s_w, 16)

        @block.gpsimd
        def _(pool):
            pool.wait_ge(s_ids, 16)
            for t in range(NT):
                pool.indirect_dma_start(out=rows[:, t, :], out_offset=None, in_=E1,
                                        in_offset=bass.IndirectOffsetOnAxis(ap=ids_sb[:, t:t + 1], axis=0)
                                        ).then_inc(s_rows, 16)

        @block.tensor
        def _(pe):
            pe.wait_ge(s_rows, 16 * NT)
            for g in range(NG):
                if g >= 2:
                    pe.wait_ge(s_Tc, g - 1)
                pe.transpose(psT[:, g % 2, 0:P], rows[:, TG * g:TG * (g + 1), :], ident[:]).then_inc(s_T, 1)
            pe.wait_ge(s_w, 16 * TG)
            for g in range(NG):
                pe.wait_ge(s_Tc, g + 1)
                for q in range(2):
                    n = 2 * g + q
                    if n >= 4:
                        pe.wait_ge(s_res, n - 3)
                    pe.matmul(psO[:, n % 4, :], rowsT[:, g, :], w_blk[:, 2 * q:2 * q + 2, :],
                              start=True, stop=True).then_inc(s_mm, 1)

        @block.scalar
        def _(act):
            for g in range(NG):
                act.wait_ge(s_T, g + 1)
                act.copy(rowsT[:, g, :], psT[:, g % 2, 0:P]).then_inc(s_Tc, 1)

        @block.vector
        def _(dve):
            dve.memset(w_blk[:], 0.0).then_inc(s_zero, 1)
            dve.wait_ge(s_pos, 32)
            dve.tensor_tensor(posb[:], posb[:], b2b[:].unsqueeze(1).to_broadcast([P, TG, D]), ALU.add).then_inc(s_bias, 1)
            dve.wait_ge(s_bias, 1)
            for n in range(2 * NG):
                dve.wait_ge(s_mm, n + 1)
                q = n % 2
                dve.tensor_tensor(res[:, 2 * n:2 * n + 2, :], psO[:, n % 4, :].rearrange("p (t d) -> p t d", d=D),
                                  posb[:, 2 * q:2 * q + 2, :], ALU.add).then_inc(s_res, 1)


class Norm:

    def __init__(self, k):
        self.stats = k.sb("ln_stats", [P, NT, 6])
        self.mv = k.sb("ln_mv", [P, NT, 2])
        self.dev = k.sb("ln_dev", [P, NT])
        self.rstd = k.sb("ln_rstd", [P, NT])
        self.s_stats, self.s_mv = k.sem("ln_stats"), k.sem("ln_mv")
        self.s_var, self.s_dev, self.s_done = k.sem("ln_var"), k.sem("ln_dev"), k.sem("ln_done")

    def vector(self, dve, res):
        with dve.Fori(0, NT) as t:
            dve.bn_stats(self.stats[:, t, :], res[:, t, :]).then_inc(self.s_stats, 1)
        dve.wait_ge(self.s_stats, NT + 1)
        for t in range(NT):
            dve.bn_aggr(self.mv[:, t, :], self.stats[:, t, :]).then_inc(self.s_mv, 1)
        dve.wait_ge(self.s_mv, NT + 1)
        dve.tensor_scalar(self.dev[:], self.mv[:, :, 1], EPS, None, ALU.add).then_inc(self.s_var, 1)
        dve.wait_ge(self.s_dev, 2)
        dve.reciprocal(self.rstd[:], self.dev[:]).then_inc(self.s_done, 1)
        dve.wait_ge(self.s_done, 2)

    def scalar(self, act):
        act.wait_ge(self.s_var, 2)
        act.activation(self.dev[:], self.dev[:], ACT.Sqrt).then_inc(self.s_dev, 1)

    def apply(self, dve, out, res, t):
        return dve.tensor_scalar(out, res[:, t, :], self.mv[:, t, 0:1], self.rstd[:, bass.ds(t, 1)],
                                 ALU.subtract, ALU.mult)


def load_split(k, name, src, shape):
    return dict(src=src, raw=k.sb(name + "_raw", shape), hi=k.sb(name + "_hi", shape, F32R),
                lo=k.sb(name + "_lo", shape, F32R))


def load_weights(sp, ws, s_raw):
    for w in ws:
        sp.dma_start(w["raw"][:], w["src"]).then_inc(s_raw, 16)


def split_weights(eng, ws, s_raw, s_hi, s_wt):
    eng.wait_ge(s_raw, 16 * len(ws) + 1)
    for n, w in enumerate(ws):
        eng.tensor_copy(w["hi"][:], w["raw"][:]).then_inc(s_hi, 1)
    for n, w in enumerate(ws):
        eng.wait_ge(s_hi, n + 2)
        eng.tensor_tensor(w["lo"][:], w["raw"][:], w["hi"][:].bitcast(F32), ALU.subtract).then_inc(s_wt, 1)


def project_qkv(nc, tag, res, ident, w_qk, w_v, bias_qk, rope, gate_w, gate_b, q_dram, k_dram, v_dram, gates):
    has_v = w_v is not None
    with ExitStack() as ctx:
        k = Kit(nc, ctx, tag)
        norm = Norm(k)
        ws = [load_split(k, "w_qk", w_qk, [P, KD, 2 * D])]
        if has_v:
            ws.append(load_split(k, "w_v", w_v, [P, KD, D]))
        else:
            ws.append(load_split(k, "w_g", gate_w, [P, KD, H]))
        xn = k.sb("xn", [P, TG, D])
        xTh, xTl = k.sb("xTh", [P, KD, S], F32R), k.sb("xTl", [P, KD, S], F32R)
        qk = k.sb("qk", [P, 2, 2 * D])
        qkr = k.sb("qkr", [P, TG, 2 * D])
        part = k.sb("part", [P, 3, 4, S], BF16)
        rest = k.sb("rest", [P, 4, S])
        vaug = k.sb("vaug", [P, TG, H, VW])
        one = k.sb("one", [P, 1])
        psT = k.ps("psT", [P, KD, S])
        psQ = k.ps("psQ", [P, 512])
        psV = k.ps("psV", [P, 512])
        psR = k.ps("psR", [P, 4, S])
        names = ("raw tab hi wt xn xT xTh xTl q v qs vs rot1 rot2 rot3 R h rest m l out ones vout gT gc gt").split()
        s = {n: k.sem(n) for n in names}
        if rope is not None:
            cos_sb, sin_sb = k.sb("cos", [P, TG, DK]), k.sb("sin", [P, TG, DK])
            rot = k.sb("rot", [P, 2, 2 * D])
        else:
            bias_sb = k.sb("bias", [P, 2 * D])
            gT_sb = k.sb("gT_sb", [P, S])
            glog = k.sb("glog", [P, NT, H])
            gb_sb = k.sb("gb_sb", [P, H])
            gmax, gsum = k.sb("gmax", [P, NT]), k.sb("gsum", [P, NT])
            s_gates = k.sem("gates")
        k.open()
        block = ctx.enter_context(nc.Block())

        @block.sync
        def _(sp):
            load_weights(sp, ws, s["raw"])
            if rope is not None:
                sp.dma_start(cos_sb[:], rope[0]).then_inc(s["tab"], 16)
                sp.dma_start(sin_sb[:], rope[1]).then_inc(s["tab"], 16)
            else:
                sp.dma_start(bias_sb[:], bias_qk.partition_broadcast(P)).then_inc(s["tab"], 16)
                sp.dma_start(gb_sb[:], gate_b.partition_broadcast(P)).then_inc(s["tab"], 16)

            def body(b, last):
                sp.wait_ge(s["ones"], 3)
                sp.wait_ge(s["vs"], TG * b + TG + 1)
                sp.dma_start(v_dram[b].rearrange("(t p) c -> p t c", p=P),
                             vaug[:].rearrange("p t h c -> p t (h c)")).then_inc(s["vout"], 16)
                sp.wait_ge(s["l"], b + 2)
                for c in range(2):
                    for r, term in enumerate(TERMS_Q):
                        dst = q_dram[b, 8 * c:8 * c + 8, DK * r:DK * (r + 1), :]
                        sp.dma_start(dst, part[:, term, c, :]).then_inc(s["out"], 16)
                    for term in range(3):
                        dst = k_dram[b, 8 * c:8 * c + 8, DK * term:DK * (term + 1), :]
                        sp.dma_start(dst, part[:, term, 2 + c, :]).then_inc(s["out"], 16)

            looped(sp, B, body)
            sp.wait_ge(s["out"], 16 * 18 * B + 1)
            sp.wait_ge(s["vout"], 16 * B + 1)

        @block.tensor
        def _(pe):
            def transposes(b):
                pe.wait_ge(s["xn"], TG * b + TG + 1)
                pe.wait_ge(s["xTl"], KD * b + 1)
                for i in range(TG):
                    for c in range(KD):
                        mm = pe.transpose(psT[:, c, P * i:P * (i + 1)], xn[:, i, P * c:P * (c + 1)], ident[:])
                mm.then_inc(s["xT"], 1)

            def body(b, last):
                pe.wait_ge(s["xTl"], KD * b + KD + 1)
                pe.wait_ge(s["xTh"], KD * b + KD + 1)
                for i in range(TG):
                    tok = slice(P * i, P * (i + 1))
                    pe.wait_ge(s["qs"], TG * b + i + 1)
                    n = 0
                    for a, w in split_passes(xTh, xTl, ws[0]["hi"], ws[0]["lo"]):
                        for c in range(KD):
                            mm = pe.matmul(psQ[:], a[:, c, tok], w[:, c, :], start=(n == 0), stop=(n == 5))
                            n += 1
                    mm.then_inc(s["q"], 1)
                    if has_v:
                        pe.wait_ge(s["vs"], TG * b + i + 1)
                        n = 0
                        for a, w in split_passes(xTh, xTl, ws[1]["hi"], ws[1]["lo"]):
                            for c in range(KD):
                                mm = pe.matmul(psV[:, 0:D], a[:, c, tok], w[:, c, :], start=(n == 0), stop=(n == 5))
                                n += 1
                        mm.then_inc(s["v"], 1)
                if not has_v:
                    pe.wait_ge(s["gt"], b + 1)
                    n = 0
                    for w, a in split_passes(ws[1]["hi"], ws[1]["lo"], xTh, xTl):
                        for c in range(KD):
                            mm = pe.matmul(psV[0:H, :], w[:, c, :], a[:, c, :], start=(n == 0), stop=(n == 5))
                            n += 1
                    mm.then_inc(s["gT"], 1)
                if not last:
                    transposes(b + 1)
                if not has_v:
                    pe.wait_ge(s["wt"], len(ws) + 1)
                    pe.wait_ge(s["gc"], b + 2)
                    for i in range(TG):
                        mm = pe.transpose(psV[:, P * i:P * (i + 1)], gT_sb[:, P * i:P * (i + 1)], ident[:])
                    mm.then_inc(s["v"], 1)
                pe.wait_ge(s["rest"], 2 * b + 1)
                pe.wait_ge(s["rot3" if rope is not None else "qs"], TG * b + TG + 1)
                for c in range(4):
                    for i in range(TG):
                        mm = pe.transpose(psR[:, c, P * i:P * (i + 1)], qkr[:, i, P * c:P * (c + 1)], ident[:])
                    if c % 2:
                        mm.then_inc(s["R"], 1)

            pe.wait_ge(s["wt"], len(ws) + 1)
            transposes(0)
            looped(pe, B, body)

        @block.scalar
        def _(act):
            norm.scalar(act)
            act.wait_ge(s["ones"], 4 if has_v else 5)

            def body(b, last):
                act.wait_ge(s["xT"], b + 2)
                if has_v:
                    act.wait_ge(s["v"], TG * b + 1)
                else:
                    act.wait_ge(s["gT"], b + 1)
                for c in range(KD):
                    act.copy(xTh[:, c, :], psT[:, c, :]).then_inc(s["xTh"], 1)
                for i in range(TG):
                    if has_v:
                        act.wait_ge(s["q"], TG * b + i + 2)
                        if i >= 2:
                            act.wait_ge(s["rot1"], TG * b + i)
                            act.wait_ge(s["rot2"], TG * b + i)
                        else:
                            act.wait_ge(s["rot1"], TG * b + 1)
                            act.wait_ge(s["rot2"], TG * b + 1)
                        act.copy(qk[:, i % 2, :], psQ[:]).then_inc(s["qs"], 1)
                        act.wait_ge(s["v"], TG * b + i + 2)
                        act.wait_ge(s["vout"], 16 * b + 1)
                        act.copy(vaug[:, i, :, 0:DK], psV[:, 0:D].rearrange("p (h d) -> p h d", d=DK)).then_inc(s["vs"], 1)
                    else:
                        act.wait_ge(s["qs"], TG * b + i + 2)
                        act.wait_ge(s["vout"], 16 * b + 1)
                        act.copy(vaug[:, i, :, 0:DK],
                                 qkr[:, i, D:2 * D].rearrange("p (h d) -> p h d", d=DK)).then_inc(s["vs"], 1)
                if not has_v:
                    act.wait_ge(s["gT"], b + 2)
                    act.copy(gT_sb[0:H, :], psV[0:H, :]).then_inc(s["gc"], 1)
                act.wait_ge(s["out"], 16 * 18 * b + 1)
                for q in range(2):
                    act.wait_ge(s["R"], 2 * b + q + 2)
                    act.copy(part[:, 0, 2 * q:2 * q + 2, :], psR[:, 2 * q:2 * q + 2, :]).then_inc(s["h"], 1)

            looped(act, B, body)
            if not has_v:
                act.wait_ge(s_gates, 3)
                act.activation(glog[:], glog[:], ACT.Exp).then_inc(s_gates, 1)

        @block.gpsimd
        def _(pool):
            split_weights(pool, ws, s["raw"], s["hi"], s["wt"])
            pool.memset(vaug[:, :, :, DK:VW], 0.0).then_inc(s["ones"], 1)
            pool.wait_ge(s["ones"], 2)
            pool.memset(vaug[:, :, :, DK:DK + 1], 1.0).then_inc(s["ones"], 1)
            pool.memset(one[:], 1.0).then_inc(s["ones"], 1)
            if not has_v:
                pool.memset(gT_sb[:], 0.0).then_inc(s["ones"], 1)
            pool.wait_ge(s["ones"], 4 if has_v else 5)
            if rope is not None:
                pool.wait_ge(s["tab"], 33)

            def body(b, last):
                if rope is not None:
                    for i in range(TG):
                        pool.wait_ge(s["qs"], TG * b + i + 2)
                        if i >= 2:
                            pool.wait_ge(s["rot3"], TG * b + i)
                        else:
                            pool.wait_ge(s["rot3"], TG * b + 1)
                        src = qk[:, i % 2, :].rearrange("p (h u d) -> p h u d", u=2, d=DK // 2)
                        dst = rot[:, i % 2, :].rearrange("p (h u d) -> p h u d", u=2, d=DK // 2)
                        for u in range(2):
                            sn = sin_sb[:, i, 8 * u:8 * u + 8].unsqueeze(1).to_broadcast([P, 2 * H, DK // 2])
                            ins = pool.tensor_tensor(dst[:, :, u, :], src[:, :, 1 - u, :], sn, ALU.mult)
                        ins.then_inc(s["rot2"], 1)
                pool.wait_ge(s["rest"], 2 * b + 3)
                pool.wait_ge(s["out"], 16 * 18 * b + 1)
                pool.tensor_tensor(part[:, 1], rest[:], one[:].unsqueeze(2).to_broadcast([P, 4, S]), ALU.mult).then_inc(s["m"], 1)
                pool.wait_ge(s["m"], b + 2)
                pool.tensor_tensor(part[:, 2], rest[:], part[:, 1], ALU.subtract).then_inc(s["l"], 1)

            looped(pool, B, body)

        @block.vector
        def _(dve):
            norm.vector(dve, res)
            dve.wait_ge(s["tab"], 33)

            def normed(b):
                dve.wait_ge(s["xT"], b + 1)
                for i in range(TG):
                    norm.apply(dve, xn[:, i, :], res, TG * b + i).then_inc(s["xn"], 1)

            def lows(b):
                for c in range(KD):
                    dve.wait_ge(s["xTh"], KD * b + c + 2)
                    dve.tensor_tensor(xTl[:, c, :], psT[:, c, :], xTh[:, c, :].bitcast(F32),
                                      ALU.subtract).then_inc(s["xTl"], 1)

            def body(b, last):
                if has_v:
                    dve.wait_ge(s["v"], TG * b + 1)
                else:
                    dve.wait_ge(s["gT"], b + 1)
                lows(b)
                if not last:
                    normed(b + 1)
                for i in range(TG):
                    dve.wait_ge(s["R"], 2 * b + 1)
                    if rope is not None:
                        dve.wait_ge(s["qs"], TG * b + i + 2)
                        cs = cos_sb[:, i, :].unsqueeze(1).to_broadcast([P, 2 * H, DK])
                        dve.tensor_tensor(qkr[:, i, :].rearrange("p (h d) -> p h d", d=DK),
                                          qk[:, i % 2, :].rearrange("p (h d) -> p h d", d=DK), cs,
                                          ALU.mult).then_inc(s["rot1"], 1)
                        dve.wait_ge(s["rot1"], TG * b + i + 2)
                        dve.wait_ge(s["rot2"], TG * b + i + 2)
                        dve.tensor_tensor(qkr[:, i, :], qkr[:, i, :], rot[:, i % 2, :], ALU.add).then_inc(s["rot3"], 1)
                    else:
                        dve.wait_ge(s["q"], TG * b + i + 2)
                        dve.wait_ge(s["vs"], TG * b + 1)
                        dve.tensor_tensor(qkr[:, i, :], psQ[:], bias_sb[:], ALU.add).then_inc(s["qs"], 1)
                if not has_v:
                    dve.wait_ge(s["v"], b + 2)
                    dve.tensor_tensor(glog[:, bass.ds(TG * b, TG), :],
                                      psV[:].rearrange("p (t c) -> p t c", c=P)[:, :, 0:H],
                                      gb_sb[:].unsqueeze(1).to_broadcast([P, TG, H]), ALU.add).then_inc(s["gt"], 1)
                dve.wait_ge(s["l"], b + 1)
                for q in range(2):
                    dve.wait_ge(s["h"], 2 * b + q + 2)
                    dve.tensor_tensor(rest[:, 2 * q:2 * q + 2, :], psR[:, 2 * q:2 * q + 2, :],
                                      part[:, 0, 2 * q:2 * q + 2, :], ALU.subtract).then_inc(s["rest"], 1)

            normed(0)
            looped(dve, B, body)
            if not has_v:
                dve.wait_ge(s["gt"], B + 1)
                dve.tensor_reduce(gmax[:], glog[:], AX.X, ALU.max).then_inc(s_gates, 1)
                dve.wait_ge(s_gates, 2)
                dve.tensor_tensor(glog[:], glog[:], gmax[:].unsqueeze(2).to_broadcast([P, NT, H]),
                                  ALU.subtract).then_inc(s_gates, 1)
                dve.wait_ge(s_gates, 4)
                dve.tensor_reduce(gsum[:], glog[:], AX.X, ALU.add).then_inc(s_gates, 1)
                dve.wait_ge(s_gates, 5)
                dve.reciprocal(gsum[:], gsum[:]).then_inc(s_gates, 1)
                dve.wait_ge(s_gates, 6)
                dve.tensor_tensor(gates[:], glog[:], gsum[:].unsqueeze(2).to_broadcast([P, NT, H]),
                                  ALU.mult).then_inc(s_gates, 1)
                dve.wait_ge(s_gates, 7)


class Unit:

    def __init__(self, n, i=None):
        self.n, self.i = n, i
        self.hg, self.par, self.buf = n % NHG, n % 2, n % 4

    def __sub__(self, d):
        return Unit(self.n - d, self.i)

    def of(self, per_four, static):
        return static if self.i is None else self.i * per_four + static

    @property
    def value(self):
        return self.of(NHG, self.n)

    @property
    def half(self):
        return self.of(NHG // 2, self.n // 2)

    @property
    def seq(self):
        return self.of(1, self.n // NHG)

    def exists(self):
        return self.i is not None or 0 <= self.n < B * NHG

    def after(self, d):
        return self.i is not None or self.n >= d

    def slots(self, counts, k=0):
        whole, part = divmod(self.n, NHG)
        return self.of(sum(counts), whole * sum(counts) + sum(counts[:part]) + k)

    def slot_par(self, counts, k):
        whole, part = divmod(self.n, NHG)
        return (whole * sum(counts) + sum(counts[:part]) + k) % 2


def query_slots(windows, hg):
    out = []
    if windows is None:
        out.append([(0, P * h, h, 0, 0, P) for h in range(HG)])
        out.append([(h // 2, 256 * (h % 2), h, 1, 0, 256) for h in range(HG)])
        for i in (2, 3):
            out += [[(n, 0, 2 * q + n, i, 0, P * (i + 1)) for n in range(2)] for q in range(2)]
        return out
    for h in range(HG):
        w = windows[HG * hg + h]
        if w > P:
            out += [[(n, 0, h, i + n, P * (i + n) - w, P + w) for n in range(m)] for i, m in ((0, 2), (2, 1), (3, 1))]
        else:
            out.append([(i // 2, 256 * (i % 2), h, i, P * i - w, P + w) for i in range(TG)])
    return out


def key_slots(windows, hg):
    out = []
    if windows is None:
        for j in (0, 1):
            out += [[(0, h, j, S - P * j)] for h in range(HG)]
        out += [[(256 * n, 2 * q + n, 2, 256) for n in range(2)] for q in range(2)]
        out.append([(P * h, h, 3, P) for h in range(HG)])
        return out
    for h in range(HG):
        w = windows[HG * hg + h]
        if w > P:
            out += [[(0, h, j, P + w)] for j in range(TG)]
        else:
            out += [[(256 * n, h, 2 * q + n, P + w) for n in range(2)] for q in range(2)]
    return out


def events(windows, u):
    na = len(query_slots(windows, u.hg)) if u.exists() else 0
    nb = len(key_slots(windows, (u - 2).hg)) if (u - 2).exists() else 0
    out, ia, ib = [], 0, 0
    while ia < na or ib < nb:
        if ia < na and (ib >= nb or ia * nb <= ib * na):
            out.append(("A", ia))
            ia += 1
        else:
            out.append(("B", ib))
            ib += 1
    steps, out = out, []
    if (u - 3).exists():
        out += [("PV", 0)]
    out += steps[:3]
    if (u - 1).exists():
        out += [("TOP", 0)]
    out += steps[3:8]
    if (u - 3).exists():
        out += [("OUT", 0)]
    return out + steps[8:]


def walk(eng, stage):
    for n in range(NHG):
        stage(Unit(n))
    with eng.Fori(1, B) as i:
        for n in range(NHG):
            stage(Unit(n, i))
    for n in range(3):
        stage(Unit(B * NHG + n))


def attend(nc, tag, windows, q_dram, k_dram, v_dram, m_dram, ident, gates, attn, beside=None):
    NU = B * NHG
    kinds = sorted(set(windows), reverse=True) if windows else [None]
    na = [len(query_slots(windows, g)) for g in range(NHG)]
    nb = [len(key_slots(windows, g)) for g in range(NHG)]
    assert sum(na) % 2 == 0 and sum(nb) % 2 == 0
    reach = S if windows is None else P + max(windows)
    with ExitStack() as ctx:
        k = Kit(nc, ctx, tag)
        qa = k.sb("qa", [P, 4, HG, S], BF16)
        ka = k.sb("ka", [P, 4, HG, S], BF16)
        vu = k.sb("vu", [P, 4, TG, HG, VW])
        top = k.sb("top", [P, 2, HG, TG])
        topT = k.sb("topT", [HG * TG, 2, MROWS, P], BF16)
        idb = k.sb("idb", [P, P], BF16)
        wide = {w: (P + w if w else P) for w in kinds}
        mask_q = {w: k.sb(f"mask_q{w}", [P, wide[w]], BF16) for w in kinds}
        mask_k = {w: k.sb(f"mask_k{w}", [P, wide[w]], BF16) for w in kinds}
        never = k.sb("never", [P, 256], BF16)
        prob = k.sb("prob", [P, 2, HG, TG, reach])
        outT = k.sb("outT", [P, 2, S])
        rec = k.sb("rec", [P, 2, TG, HG])
        psA = k.ps("psA", [P, 2, 2, 512])
        psB = k.ps("psB", [P, 2, 512])
        psO = k.ps("psO", [P, 512])
        psM = k.ps("psM", [P, 512])
        s_load = [k.sem(f"load{n}") for n in range(2)]
        names = "const mask scoresA max topT_ps topT m_out m_in scoresB exp pv outT turned rec norm".split()
        s = {n: k.sem(n) for n in names}
        n_mask = 2 * len(kinds) * (3 if windows else 2)
        block = ctx.enter_context(nc.Block())

        def window(u, h):
            return windows[HG * u.hg + h] if windows else None

        @block.gpsimd
        def _(pool):
            pool.memset(never[:], MASKED).then_inc(s["const"], 1)
            pool.wait_ge(s["const"], 1)
            pool.memset(ka[KROWS:KROWS + MROWS], -1.0).then_inc(s["const"], 1)
            pool.wait_ge(s["const"], 2)
            pool.tensor_copy(idb[:], ident[:]).then_inc(s["const"], 1)
            pool.wait_ge(s["const"], 3)
            for w in kinds:
                pool.memset(mask_q[w][:], 0.0).then_inc(s["mask"], 1)
                pool.memset(mask_k[w][:], 0.0).then_inc(s["mask"], 1)
            pool.wait_ge(s["mask"], 2 * len(kinds))
            for w in kinds:
                pool.affine_select(out=mask_q[w][:], in_=mask_q[w][:], compare_op=ALU.is_ge, fill=MASKED,
                                   base=w or 0, pattern=[[-1, wide[w]]], channel_multiplier=1).then_inc(s["mask"], 1)
                pool.affine_select(out=mask_k[w][:], in_=mask_k[w][:], compare_op=ALU.is_ge, fill=MASKED,
                                   base=0, pattern=[[1, wide[w]]], channel_multiplier=-1).then_inc(s["mask"], 1)
            pool.wait_ge(s["mask"], 4 * len(kinds))
            for w in kinds:
                if w:
                    pool.affine_select(out=mask_q[w][:], in_=mask_q[w][:], compare_op=ALU.is_gt, fill=MASKED,
                                       base=0, pattern=[[1, wide[w]]], channel_multiplier=-1).then_inc(s["mask"], 1)
                    pool.affine_select(out=mask_k[w][:], in_=mask_k[w][:], compare_op=ALU.is_gt, fill=MASKED,
                                       base=w, pattern=[[-1, wide[w]]], channel_multiplier=1).then_inc(s["mask"], 1)
            if beside is not None:
                beside(pool)

        @block.sync
        def _(sp):
            def loads(u):
                if not u.exists():
                    return
                h0 = HG * u.hg
                done = s_load[u.par]
                if u.after(4):
                    sp.wait_ge(s["exp"], (u - 3).slots(nb))
                kv = k_dram[bass.ds(u.seq, 1), h0:h0 + HG].rearrange("o h r n -> r (o h) n")
                sp.dma_start(qa[0:KROWS, u.buf], q_dram[bass.ds(u.seq, 1), h0:h0 + HG]
                             .rearrange("o h r n -> r (o h) n")).then_inc(done, 16)
                sp.dma_start(ka[0:3 * DK, u.buf], kv[0:3 * DK]).then_inc(done, 16)
                sp.dma_start(ka[3 * DK:5 * DK, u.buf], kv[0:2 * DK]).then_inc(done, 16)
                sp.dma_start(ka[5 * DK:6 * DK, u.buf], kv[0:DK]).then_inc(done, 16)
                if u.after(4):
                    sp.wait_ge(s["pv"], (u - 3).value)
                vsrc = v_dram[bass.ds(u.seq, 1), :, h0 * VW:(h0 + HG) * VW]
                sp.dma_start(vu[:, u.buf].rearrange("p t h c -> p t (h c)"),
                             vsrc.rearrange("o (t p) c -> p (o t) c", p=P)).then_inc(done, 16)

            def maxima(u):
                if not u.exists():
                    return
                sp.wait_ge(s["topT"], MROWS * u.value + MROWS)
                if u.after(2):
                    sp.wait_ge(s["m_in"], 16 * (u - 1).value)
                sp.dma_start(m_dram[u.par].rearrange("r (q n) -> q r n", n=P), topT[:, u.par]).then_inc(s["m_out"], 16)
                sp.wait_ge(s["m_out"], 16 * u.value + 16)
                sp.dma_start(qa[KROWS:KROWS + MROWS, u.buf].rearrange("r h n -> r (h n)"),
                             m_dram[u.par]).then_inc(s["m_in"], 16)

            def stage(u):
                if u.i is None and u.n == 0:
                    loads(u)
                maxima(u - 1)
                loads(Unit(u.n + 1, u.i))

            for n in range(NHG):
                stage(Unit(n))
            with sp.Fori(1, B - 1) as i:
                for n in range(NHG):
                    stage(Unit(n, i))
            for n in range(NHG * (B - 1), NHG * B + 3):
                stage(Unit(n))

        @block.tensor
        def _(pe):
            pe.wait_ge(s["mask"], n_mask)
            pe.wait_ge(s["const"], 3)

            def query_tile(u, slot, t):
                bank, col, h, i, k0, cols = t
                out = psA[:, slot, bank, col:col + cols]
                q = qa[0:KROWS, u.buf, h, P * i:P * (i + 1)]
                w = window(u, h)
                if w is None:
                    pe.matmul(out, q, ka[0:KROWS, u.buf, h, 0:cols], start=True, stop=True)
                    return pe.matmul(out[:, cols - P:cols], idb[:], mask_q[w][:], start=False, stop=True,
                                     skip_group_check=True)
                cut = max(0, -k0)
                if cut:
                    pe.matmul(out[:, 0:cut], idb[:], never[:, 0:cut], start=True, stop=False, skip_group_check=True)
                pe.matmul(out[:, cut:cols], idb[:], mask_q[w][:, cut:cols], start=(cut == 0), stop=False,
                          skip_group_check=True)
                return pe.matmul(out[:, cut:cols], q, ka[0:KROWS, u.buf, h, k0 + cut:k0 + cols],
                                 start=False, stop=True, skip_group_check=True)

            def key_tile(u, slot, t):
                col, h, j, cols = t
                out = psB[:, slot, col:col + cols]
                w = window(u, h)
                have = min(cols, S - P * j)
                keys = ka[0:KROWS + MROWS, u.buf, h, P * j:P * (j + 1)]
                qs = qa[0:KROWS + MROWS, u.buf, h, P * j:P * j + have]
                if w is None:
                    pe.matmul(out, keys, qs, start=True, stop=True)
                    return pe.matmul(out[:, 0:P], idb[:], mask_k[w][:], start=False, stop=True, skip_group_check=True)
                pe.matmul(out, idb[:], mask_k[w][:], start=True, stop=False, skip_group_check=True)
                return pe.matmul(out[:, 0:have], keys, qs, start=False, stop=True, skip_group_check=True)

            def stage(u):
                for what, n in events(windows, u):
                    if what == "A":
                        if n == 0:
                            pe.wait_ge(s_load[u.par], 80 * u.half + 80)
                        if u.after(1) or n >= 2:
                            pe.wait_ge(s["max"], u.slots(na, n - 1))
                        for t in query_slots(windows, u.hg)[n]:
                            mm = query_tile(u, u.slot_par(na, n), t)
                        mm.then_inc(s["scoresA"], 1)
                    elif what == "B":
                        v = u - 2
                        if n == 0:
                            pe.wait_ge(s["m_in"], 16 * v.value + 16)
                        if v.after(1) or n >= 2:
                            pe.wait_ge(s["exp"], v.slots(nb, n - 1))
                        for t in key_slots(windows, v.hg)[n]:
                            mm = key_tile(v, v.slot_par(nb, n), t)
                        mm.then_inc(s["scoresB"], 1)
                    elif what == "PV":
                        v = u - 3
                        pe.wait_ge(s["exp"], v.slots(nb, nb[v.hg]))
                        if v.after(1):
                            pe.wait_ge(s["outT"], v.value)
                        for j in range(TG):
                            for h in range(HG):
                                w = window(v, h)
                                have = min(P + w if w else S, S - P * j)
                                mm = pe.matmul(psO[VW * h:VW * (h + 1), P * j:P * j + have], vu[:, v.buf, j, h, :],
                                               prob[:, v.par, h, j, 0:have], start=(j == 0), stop=(j == TG - 1),
                                               tile_position=(0, VW * h), skip_group_check=True)
                        mm.then_inc(s["pv"], 1)
                    elif what == "TOP":
                        v = u - 1
                        pe.wait_ge(s["max"], v.slots(na, na[v.hg]))
                        if v.after(3):
                            pe.wait_ge(s["norm"], (v - 2).value)
                        pe.transpose(psM[0:HG * TG, 0:P], top[:, v.par].rearrange("p h t -> p (h t)"), ident[:]
                                     ).then_inc(s["topT_ps"], 1)
                    else:
                        v = u - 3
                        pe.wait_ge(s["outT"], v.value + 1)
                        w = u - 1 if (u - 1).exists() else Unit(NU - 1)
                        pe.wait_ge(s["topT"], MROWS * w.value + MROWS)
                        if v.after(1):
                            pe.wait_ge(s["norm"], v.value)
                        for i in range(TG):
                            mm = pe.transpose(psM[:, P * i:P * (i + 1)], outT[:, v.par, P * i:P * (i + 1)], ident[:])
                        mm.then_inc(s["turned"], 1)

            walk(pe, stage)

        @block.scalar
        def _(act):
            def stage(u):
                for what, n in events(windows, u):
                    if what == "B":
                        v = u - 2
                        if n == 0 and v.after(2):
                            act.wait_ge(s["pv"], (v - 1).value)
                        act.wait_ge(s["scoresB"], v.slots(nb, n + 1))
                        sl = key_slots(windows, v.hg)[n]
                        col, h, j, cols = sl[0]
                        bank = psB[:, v.slot_par(nb, n), :]
                        if len(sl) == 1:
                            src, dst = bank[:, 0:cols], prob[:, v.par, h, j, 0:cols]
                        else:
                            src = bank.rearrange("p (n q) -> p n q", q=512 // len(sl))[:, :, 0:cols]
                            dst = (prob[:, v.par, h:h + len(sl), j, 0:cols] if windows is None
                                   else prob[:, v.par, h, j:j + 2, 0:cols])
                        act.activation(dst, src, ACT.Exp, scale=0.25).then_inc(s["exp"], 1)
                    elif what == "PV":
                        v = u - 3
                        act.wait_ge(s["pv"], v.value + 1)
                        if v.after(2):
                            act.wait_ge(s["turned"], (v - 1).value)
                        act.copy(outT[:, v.par, :], psO[:]).then_inc(s["outT"], 1)
            walk(act, stage)

        @block.vector
        def _(dve):
            def stage(u):
                for what, n in events(windows, u):
                    if what == "A":
                        if n == 0 and u.after(2):
                            dve.wait_ge(s["topT_ps"], (u - 1).value)
                        dve.wait_ge(s["scoresA"], u.slots(na, n + 1))
                        sl = query_slots(windows, u.hg)[n]
                        bank, col, h, i, k0, cols = sl[0]
                        buf = psA[:, u.slot_par(na, n)]
                        same_head = windows is not None
                        dst = top[:, u.par, h, i:i + len(sl)] if same_head else top[:, u.par, h:h + len(sl), i]
                        if len(sl) == 1:
                            src = buf[:, 0:1, 0:cols]
                        elif len(sl) == 2:
                            src = buf[:, :, 0:cols]
                        elif cols == P and windows is None:
                            src = buf[:, 0, :].rearrange("p (h c) -> p h c", c=P)
                        else:
                            src = buf.rearrange("p b (i c) -> p (b i) c", c=256)[:, :, 0:cols]
                        dve.tensor_reduce(dst, src, AX.X, ALU.max).then_inc(s["max"], 1)
                    elif what == "TOP":
                        v = u - 1
                        dve.wait_ge(s["topT_ps"], v.value + 1)
                        if v.after(2):
                            dve.wait_ge(s["m_out"], 16 * (v - 1).value)
                        dve.tensor_copy(topT[:, v.par, 0, :], psM[0:HG * TG, 0:P]).then_inc(s["topT"], 1)
                        dve.wait_ge(s["topT"], MROWS * v.value + 1)
                        dve.tensor_tensor(topT[:, v.par, 1, :], psM[0:HG * TG, 0:P], topT[:, v.par, 0, :],
                                          ALU.subtract).then_inc(s["topT"], 1)
                    elif what == "OUT":
                        v = u - 3
                        dve.wait_ge(s["turned"], v.value + 1)
                        turned = psM[:].rearrange("p (t h c) -> p t h c", h=HG, c=VW)
                        per = 1 if windows is None else 2
                        dve.reciprocal(rec[:, v.par], turned[:, :, :, DK]).then_inc(s["rec"], 1)
                        dve.wait_ge(s["rec"], v.value * per + 1)
                        if windows is not None:
                            g = gates[:, bass.ds(v.seq * TG, TG), HG * v.hg:HG * v.hg + HG]
                            dve.tensor_tensor(rec[:, v.par], rec[:, v.par], g, ALU.mult).then_inc(s["rec"], 1)
                            dve.wait_ge(s["rec"], v.value * per + 2)
                        dst = attn[:, bass.ds(v.seq * TG, TG), HG * v.hg * DK:HG * (v.hg + 1) * DK]
                        dve.tensor_tensor(dst.rearrange("p t (h c) -> p t h c", c=DK), turned[:, :, :, 0:DK],
                                          rec[:, v.par].unsqueeze(3).to_broadcast([P, TG, HG, DK]),
                                          ALU.mult).then_inc(s["norm"], 1)

            walk(dve, stage)
            dve.wait_ge(s["norm"], NU)


def project_out(nc, tag, res, attn, ident, w_o, bias):
    with ExitStack() as ctx:
        k = Kit(nc, ctx, tag)
        ws = [load_split(k, "w_o", w_o, [P, KD, D])]
        xTh, xTl = k.sb("xTh", [P, 2, KD, S], F32R), k.sb("xTl", [P, 2, KD, S], F32R)
        bias_sb = k.sb("bias", [P, D])
        psT = k.ps("psT", [P, 2, KD, S])
        psY = k.ps("psY", [P, 4, 512])
        s = {n: k.sem(n) for n in "raw hi wt bias xT xTh xTl y res biased".split()}
        k.open()
        block = ctx.enter_context(nc.Block())

        @block.sync
        def _(sp):
            load_weights(sp, ws, s["raw"])
            if bias is not None:
                sp.dma_start(bias_sb[:], bias.partition_broadcast(P)).then_inc(s["bias"], 16)

        @block.gpsimd
        def _(pool):
            split_weights(pool, ws, s["raw"], s["hi"], s["wt"])

        @block.tensor
        def _(pe):
            def transposes(b):
                if b >= 2:
                    pe.wait_ge(s["xTl"], KD * (b - 1) + 1)
                for i in range(TG):
                    for c in range(KD):
                        mm = pe.transpose(psT[:, b % 2, c, P * i:P * (i + 1)],
                                          attn[:, TG * b + i, P * c:P * (c + 1)], ident[:])
                mm.then_inc(s["xT"], 1)

            transposes(0)
            pe.wait_ge(s["wt"], 2)
            for b in range(B):
                if b + 1 < B:
                    transposes(b + 1)
                pe.wait_ge(s["xTl"], KD * b + KD + 1)
                for i in range(TG):
                    m = TG * b + i
                    if m % 2 == 0 and m >= 8:
                        pe.wait_ge(s["res"], m // 2 - 2)
                    n = 0
                    for a, w in split_passes(xTh, xTl, ws[0]["hi"], ws[0]["lo"]):
                        for c in range(KD):
                            mm = pe.matmul(psY[:, m // 2 % 4, D * (m % 2):D * (m % 2 + 1)],
                                           a[:, b % 2, c, P * i:P * (i + 1)], w[:, c, :], start=(n == 0), stop=(n == 5))
                            n += 1
                    if m % 2:
                        mm.then_inc(s["y"], 1)

        @block.scalar
        def _(act):
            for b in range(B):
                act.wait_ge(s["xT"], b + 2)
                if b >= 2:
                    act.wait_ge(s["y"], 2 * (b - 1) + 1)
                for c in range(KD):
                    act.copy(xTh[:, b % 2, c, :], psT[:, b % 2, c, :]).then_inc(s["xTh"], 1)

        @block.vector
        def _(dve):
            if bias is not None:
                dve.wait_ge(s["bias"], 17)
                dve.tensor_tensor(res[:], res[:], bias_sb[:].unsqueeze(1).to_broadcast([P, NT, D]), ALU.add
                                  ).then_inc(s["biased"], 1)
                dve.wait_ge(s["biased"], 2)

            def add(b):
                for q in range(2):
                    m = 2 * b + q
                    dve.wait_ge(s["y"], m + 2)
                    dve.tensor_tensor(res[:, 2 * m:2 * m + 2, :], res[:, 2 * m:2 * m + 2, :],
                                      psY[:, m % 4, :].rearrange("p (t d) -> p t d", d=D), ALU.add).then_inc(s["res"], 1)

            for b in range(B):
                if b >= 2:
                    dve.wait_ge(s["y"], 2 * (b - 1) + 1)
                for c in range(KD):
                    dve.wait_ge(s["xTh"], KD * b + c + 2)
                    dve.tensor_tensor(xTl[:, b % 2, c, :], psT[:, b % 2, c, :], xTh[:, b % 2, c, :].bitcast(F32),
                                      ALU.subtract).then_inc(s["xTl"], 1)
                if b >= 1:
                    add(b - 1)
            add(B - 1)
            dve.wait_ge(s["res"], NT // 2 + 1)


class Router:

    weights_there = None

    def __init__(self, k, wr, experts, hot=None):
        self.experts = experts
        self.w = load_split(k, "wr", wr, [P, KD, experts])
        self.logT = k.sb("logT", [P, S])
        self.log = k.sb("log", [P, NT, experts])
        self.best = k.sb("best", [P, NT, 8])
        self.place = k.sb("place", [P, NT, 8], U32)
        self.placef = k.sb("placef", [P, NT, 2])
        self.names = k.sb("names", [P, experts])
        self.gap = k.sb("gap", [P, NT])
        self.hot = k.sb("hot", [P, 2, NT, experts]) if hot is None else hot
        self.ps = k.ps("psR", [P, 512])
        names = "logT_ps logT log_ps log best place placef names gap exp hot".split()
        self.s = {n: k.sem("router_" + n) for n in names}

    def pe_logits(self, pe, b, xh, xl):
        pe.wait_ge(*self.weights_there)
        pe.wait_ge(self.s["log"], b + 1)
        n = 0
        for w, x in split_passes(self.w["hi"], self.w["lo"], xh, xl):
            for c in range(KD):
                mm = pe.matmul(self.ps[0:self.experts, :], w[:, c, :], x[:, c, :], start=(n == 0), stop=(n == 5))
                n += 1
        mm.then_inc(self.s["logT_ps"], 1)

    def act_copy(self, act, b):
        act.wait_ge(self.s["names"], 3)
        act.wait_ge(self.s["logT_ps"], b + 2)
        act.copy(self.logT[0:self.experts, :], self.ps[0:self.experts, :]).then_inc(self.s["logT"], 1)

    def pe_turn(self, pe, b, ident):
        pe.wait_ge(*self.weights_there)
        pe.wait_ge(self.s["logT"], b + 2)
        for i in range(TG):
            mm = pe.transpose(self.ps[:, P * i:P * (i + 1)], self.logT[:, P * i:P * (i + 1)], ident[:])
        mm.then_inc(self.s["log_ps"], 1)

    def dve_logits(self, dve, b, bias=None):
        dve.wait_ge(self.s["log_ps"], b + 2)
        src = self.ps[:].rearrange("p (t c) -> p t c", c=P)[:, :, 0:self.experts]
        dst = self.log[:, bass.ds(TG * b, TG), :]
        if bias is None:
            dve.tensor_copy(dst, src).then_inc(self.s["log"], 1)
        else:
            dve.tensor_tensor(dst, src, bias[:].unsqueeze(1).to_broadcast([P, TG, self.experts]), ALU.add
                              ).then_inc(self.s["log"], 1)

    def pool_names(self, pool):
        pool.memset(self.logT[:], 0.0).then_inc(self.s["names"], 1)
        pool.iota(self.names[:], [[1, self.experts]], base=0, channel_multiplier=0,
                  allow_small_or_imprecise_dtypes=True).then_inc(self.s["names"], 1)

    def dve_pick(self, dve):
        dve.wait_ge(self.s["log"], B + 1)
        for t in range(NT):
            dve.max(self.best[:, t, :], self.log[:, t, :]).then_inc(self.s["best"], 1)
        dve.wait_ge(self.s["best"], NT + 1)
        dve.tensor_tensor(self.gap[:], self.best[:, :, 1], self.best[:, :, 0], ALU.subtract).then_inc(self.s["gap"], 1)
        for t in range(NT):
            dve.max_index(self.place[:, t, :], self.best[:, t, :], self.log[:, t, :]).then_inc(self.s["place"], 1)
        dve.wait_ge(self.s["place"], NT + 1)
        dve.tensor_copy(self.placef[:], self.place[:, :, 0:2]).then_inc(self.s["placef"], 1)
        dve.wait_ge(self.s["placef"], 2)
        dve.wait_ge(self.s["names"], 3)
        for n in range(2):
            dve.tensor_tensor(self.hot[:, n], self.names[:].unsqueeze(1).to_broadcast([P, NT, self.experts]),
                              self.placef[:, :, n:n + 1].to_broadcast([P, NT, self.experts]), ALU.is_equal
                              ).then_inc(self.s["hot"], 1)
        dve.wait_ge(self.s["exp"], 2)
        dve.wait_ge(self.s["hot"], 3)

    def act_exp(self, act):
        act.wait_ge(self.s["gap"], 2)
        act.activation(self.gap[:], self.gap[:], ACT.Exp).then_inc(self.s["exp"], 1)


class Turn:

    def __init__(self, k, rows=None):
        self.norm = Norm(k)
        self.rows = rows
        self.xn = k.sb("xn", [P, TG, D])
        self.ps = k.ps("psT", [P, KD, S])
        self.s = {n: k.sem(n) for n in "xn xT xTh xTl stored".split()}

    def store(self, sp, b):
        sp.wait_ge(self.s["xn"], TG * b + TG + 1)
        sp.dma_start(self.rows[bass.ds(b * S, S), :].rearrange("(t p) d -> p t d", p=P), self.xn[:]
                     ).then_inc(self.s["stored"], 16)

    def dve_norm(self, dve, res, b):
        dve.wait_ge(self.s["xT"], b + 1)
        if self.rows is not None:
            dve.wait_ge(self.s["stored"], 16 * b + 1)
        for i in range(TG):
            self.norm.apply(dve, self.xn[:, i, :], res, TG * b + i).then_inc(self.s["xn"], 1)

    def pe(self, pe, b, ident):
        pe.wait_ge(self.s["xn"], TG * b + TG + 1)
        pe.wait_ge(self.s["xTl"], KD * b + 1)
        for i in range(TG):
            for c in range(KD):
                mm = pe.transpose(self.ps[:, c, P * i:P * (i + 1)], self.xn[:, i, P * c:P * (c + 1)], ident[:])
        mm.then_inc(self.s["xT"], 1)

    def act_hi(self, act, b, xh):
        act.wait_ge(self.s["xT"], b + 2)
        for c in range(KD):
            act.copy(xh[:, c, bass.ds(b * S, S)], self.ps[:, c, :]).then_inc(self.s["xTh"], 1)

    def dve_lo(self, dve, b, xh, xl):
        for c in range(KD):
            dve.wait_ge(self.s["xTh"], KD * b + c + 2)
            dve.tensor_tensor(xl[:, c, bass.ds(b * S, S)], self.ps[:, c, :],
                              xh[:, c, bass.ds(b * S, S)].bitcast(F32), ALU.subtract).then_inc(self.s["xTl"], 1)


def ffn_sq(nc, a, res, ident):
    with ExitStack() as ctx:
        k = Kit(nc, ctx, "ffn0")
        xh, xl = k.sb("xh", [P, KD, B * S], F32R), k.sb("xl", [P, KD, B * S], F32R)
        share = k.sb("share", [P, NT, E0])
        any_sb = k.sb("any_sb", [1, 1], I32)
        with ExitStack() as ctx2:
            k2 = Kit(nc, ctx2, "ffn0a")
            turn, router = Turn(k2), Router(k2, a["wr0"], E0)
            ws = [load_split(k2, "ws1", a["ws1"], [P, KD, F0]), load_split(k2, "ws2", a["ws2"], [P, 1, D]), router.w]
            relu, act_f = k2.sb("relu", [P, S]), k2.sb("act_f", [P, S])
            act_h, act_l = k2.sb("act_h", [P, S], F32R), k2.sb("act_l", [P, S], F32R)
            lost, most = k2.sb("lost", [P, NT]), k2.sb("most", [P, 1])
            any_f = k2.sb("any_f", [1, 1])
            psH = k2.ps("psH", [P, S])
            psY = k2.ps("psY", [P, 2, 512])
            s = {n: k2.sem(n) for n in "raw hi wt hid relu act acth actl y res lost share most mostT any".split()}
            router.weights_there = s["wt"], len(ws) + 1
            k2.open()
            block = ctx2.enter_context(nc.Block())

            @block.sync
            def _(sp):
                load_weights(sp, ws, s["raw"])

            @block.gpsimd
            def _(pool):
                split_weights(pool, ws, s["raw"], s["hi"], s["wt"])
                router.pool_names(pool)

                def body(b, last):
                    pool.wait_ge(s["acth"], b + 2)
                    pool.wait_ge(s["y"], 2 * b + 1)
                    pool.tensor_tensor(act_l[:], act_f[:], act_h[:].bitcast(F32), ALU.subtract).then_inc(s["actl"], 1)
                looped(pool, B, body)

            @block.tensor
            def _(pe):
                pe.wait_ge(s["wt"], len(ws) + 1)
                turn.pe(pe, 0, ident)

                def body(b, last):
                    pe.wait_ge(turn.s["xTl"], KD * b + KD + 1)
                    gh, gl = (x[:, :, bass.ds(b * S, S)] for x in (xh, xl))
                    pe.wait_ge(s["relu"], b + 1)
                    n = 0
                    for w, x in split_passes(ws[0]["hi"], ws[0]["lo"], gh, gl):
                        for c in range(KD):
                            mm = pe.matmul(psH[:], w[:, c, :], x[:, c, :], start=(n == 0), stop=(n == 5))
                            n += 1
                    mm.then_inc(s["hid"], 1)
                    router.pe_logits(pe, b, gh, gl)
                    if not last:
                        turn.pe(pe, b + 1, ident)
                    router.pe_turn(pe, b, ident)
                    pe.wait_ge(s["actl"], b + 2)
                    for q in range(2):
                        pe.wait_ge(s["res"], (2 * b + q - 1 if q else 2 * b) + 1)
                        for i in (2 * q, 2 * q + 1):
                            for n, (x, w) in enumerate(split_passes(act_h, act_l, ws[1]["hi"], ws[1]["lo"])):
                                mm = pe.matmul(psY[:, q, D * (i % 2):D * (i % 2 + 1)], x[:, P * i:P * (i + 1)],
                                               w[:, 0, :], start=(n == 0), stop=(n == 2))
                        mm.then_inc(s["y"], 1)
                looped(pe, B, body)
                pe.wait_ge(s["most"], 2)
                pe.transpose(router.ps[0:1, 0:P], most[:], ident[:]).then_inc(s["mostT"], 1)

            @block.scalar
            def _(act):
                turn.norm.scalar(act)

                def body(b, last):
                    turn.act_hi(act, b, xh)
                    act.wait_ge(s["hid"], b + 2)
                    act.wait_ge(s["act"], b + 1)
                    act.activation(relu[:], psH[:], ACT.Relu).then_inc(s["relu"], 1)
                    act.wait_ge(s["act"], b + 2)
                    act.wait_ge(s["y"], 2 * b + 1)
                    act.copy(act_h[:], act_f[:]).then_inc(s["acth"], 1)
                    router.act_copy(act, b)
                looped(act, B, body)
                router.act_exp(act)

            @block.vector
            def _(dve):
                turn.norm.vector(dve, res)
                turn.dve_norm(dve, res, 0)

                def body(b, last):
                    turn.dve_lo(dve, b, xh, xl)
                    if not last:
                        turn.dve_norm(dve, res, b + 1)
                    dve.wait_ge(s["relu"], b + 2)
                    dve.wait_ge(s["actl"], b + 1)
                    dve.tensor_tensor(act_f[:], relu[:], relu[:], ALU.mult).then_inc(s["act"], 1)
                    router.dve_logits(dve, b)
                    for q in range(2):
                        dve.wait_ge(s["y"], 2 * b + q + 2)
                        r = res[:, bass.ds(TG * b + 2 * q, 2), :]
                        dve.tensor_tensor(r, r, psY[:, q, :].rearrange("p (t d) -> p t d", d=D), ALU.add
                                          ).then_inc(s["res"], 1)
                looped(dve, B, body)
                router.dve_pick(dve)
                dve.tensor_scalar(lost[:], router.gap[:], 1.0, 1.0, ALU.add, ALU.is_le).then_inc(s["lost"], 1)
                dve.wait_ge(s["lost"], 2)
                dve.tensor_tensor(share[:], router.hot[:, 0], lost[:].unsqueeze(2).to_broadcast([P, NT, E0]),
                                  ALU.mult).then_inc(s["share"], 1)
                dve.tensor_reduce(most[:], lost[:], AX.X, ALU.max).then_inc(s["most"], 1)
                dve.wait_ge(s["mostT"], 2)
                dve.tensor_reduce(any_f[:], router.ps[0:1, 0:P], AX.X, ALU.max).then_inc(s["any"], 1)
                dve.wait_ge(s["any"], 2)
                dve.tensor_copy(any_sb[:], any_f[:]).then_inc(s["any"], 1)
                dve.wait_ge(s["any"], 3)
                dve.wait_ge(s["share"], 2)
        ffn_sq_routed(nc, a, res, xh, xl, share, any_sb)


def ffn_sq_routed(nc, a, res, xh, xl, share, any_sb):
    with ExitStack() as ctx:
        k = Kit(nc, ctx, "ffn0b")
        w1 = load_split(k, "w1", None, [P, KD, F0])
        w2 = load_split(k, "w2", None, [P, 1, D])
        ws = (w1, w2)
        relu, act_f = k.sb("relu", [P, S]), k.sb("act_f", [P, S])
        act_h, act_l = k.sb("act_h", [P, S], F32R), k.sb("act_l", [P, S], F32R)
        psH = k.ps("psH", [P, S])
        psY = k.ps("psY", [P, TG, 512])
        one = k.sb("one", [P, 1])
        s = {n: k.sem(n) for n in "one raw hi wt hid relu act acth actl y res".split()}
        k.open()
        block = ctx.enter_context(nc.Block())
        last_b = B - 1

        def routed(eng, body):
            there = eng.value_load(any_sb[0:1, 0:1], min_val=0, max_val=1)
            with eng.If(there):
                body()

        @block.sync
        def _(sp):
            def run():
                with sp.Fori(0, E0) as e:
                    sp.wait_ge(s["wt"], 2 * e + 1)
                    sp.dma_start(w1["raw"][:], a["w1_0"][bass.ds(e, 1)].rearrange("o p k f -> p (o k) f")
                                 ).then_inc(s["raw"], 16)
                    sp.dma_start(w2["raw"][:], a["w2_0"][bass.ds(e, 1)].rearrange("o f d -> f o d")
                                 ).then_inc(s["raw"], 16)
            routed(sp, run)

        @block.gpsimd
        def _(pool):
            def run():
                pool.memset(one[:], 1.0).then_inc(s["one"], 1)
                pool.wait_ge(s["one"], 2)
                with pool.Fori(0, E0) as e:
                    pool.wait_ge(s["raw"], 32 * e + 33)
                    pool.wait_ge(s["y"], B * e + 1)
                    for n, w in enumerate(ws):
                        pool.tensor_tensor(w["hi"][:], w["raw"][:], one[:].unsqueeze(2).to_broadcast(w["raw"].shape), ALU.mult).then_inc(s["hi"], 1)
                    for n, w in enumerate(ws):
                        pool.wait_ge(s["hi"], 2 * e + n + 2)
                        pool.tensor_tensor(w["lo"][:], w["raw"][:], w["hi"][:].bitcast(F32), ALU.subtract
                                           ).then_inc(s["wt"], 1)
                    with pool.Fori(0, B) as b:
                        pool.wait_ge(s["acth"], e * B + b + 2)
                        pool.tensor_tensor(act_l[:], act_f[:], act_h[:].bitcast(F32), ALU.subtract
                                           ).then_inc(s["actl"], 1)
            routed(pool, run)

        @block.tensor
        def _(pe):
            def run():
                with pe.Fori(0, E0) as e:
                    with pe.Fori(0, B) as b:
                        pe.wait_ge(s["wt"], 2 * e + 3)
                        pe.wait_ge(s["relu"], e * B + b + 1)
                        n = 0
                        for w, x in split_passes(w1["hi"], w1["lo"], xh, xl):
                            for c in range(KD):
                                mm = pe.matmul(psH[:], w[:, c, :], x[:, c, bass.ds(b * S, S)], start=(n == 0), stop=(n == 5))
                                n += 1
                        mm.then_inc(s["hid"], 1)
                        pe.wait_ge(s["actl"], e * B + b + 2)
                        pe.wait_ge(s["res"], TG * (e * B + b) + 1)
                        for i in range(TG):
                            for n, (x, w) in enumerate(split_passes(act_h, act_l, w2["hi"], w2["lo"])):
                                mm = pe.matmul(psY[:, i, 0:D], x[:, P * i:P * (i + 1)], w[:, 0, :],
                                               start=(n == 0), stop=(n == 2))
                        mm.then_inc(s["y"], 1)
            routed(pe, run)

        @block.scalar
        def _(act):
            def run():
                with act.Fori(0, E0) as e:
                    with act.Fori(0, B) as b:
                        act.wait_ge(s["hid"], e * B + b + 2)
                        act.activation(relu[:], psH[:], ACT.Relu).then_inc(s["relu"], 1)
                        act.wait_ge(s["act"], e * B + b + 2)
                        act.wait_ge(s["y"], e * B + b + 1)
                        act.copy(act_h[:], act_f[:]).then_inc(s["acth"], 1)
            routed(act, run)

        @block.vector
        def _(dve):
            def run():
                with dve.Fori(0, E0) as e:
                    with dve.Fori(0, B) as b:
                        dve.wait_ge(s["relu"], e * B + b + 2)
                        dve.wait_ge(s["actl"], e * B + b + 1)
                        dve.tensor_tensor(act_f[:], relu[:], relu[:], ALU.mult).then_inc(s["act"], 1)
                        dve.wait_ge(s["y"], e * B + b + 2)
                        dve.wait_ge(s["res"], TG * (e * B + b) + 1)
                        for i in range(TG):
                            r = res[:, b * TG + i, :]
                            dve.scalar_tensor_tensor(r, psY[:, i, 0:D], share[:, b * TG + i, bass.ds(e, 1)], r,
                                                     ALU.mult, ALU.add).then_inc(s["res"], 1)
                dve.wait_ge(s["res"], TG * E0 * B + 1)
            routed(dve, run)


TILES = B * S * 2 // P + E1N
WCOLS = 2 * KD * F1 + HB * D
CUT = 1024


def split_experts(nc, ctx, tag, raw_dram, hi_dram, lo_dram, sems):
    k = Kit(nc, ctx, tag)
    raw, hi, lo = k.sb("raw", [P, 2, CUT]), k.sb("hi", [P, 2, CUT], F32R), k.sb("lo", [P, 2, CUT], F32R)
    one = k.sb("one", [P, 1])
    s_hi, s_lo, s_own = k.sem("hi"), k.sem("lo"), k.sem("own")
    s_raw, s_stored = sems
    n_cut = (E1N + 1) * WCOLS // CUT
    assert WCOLS % CUT == 0 and n_cut % 2 == 1

    def program(pool):
        pool.memset(one[:], 1.0).then_inc(s_hi, 1)
        pool.wait_ge(s_hi, 1)

        def load(n, par):
            pool.dma_start(raw[:, par, :], raw_dram[bass.ds(n, 1)].rearrange("o p c -> p (o c)")).then_inc(s_raw[par], 16)

        def split(n, par, i, first=False, last=False):
            pool.wait_ge(s_raw[par], 16 * i + 16)
            if not last:
                pool.sem_inc(s_own, 1)
                load(n + 1, 1 - par)
            if not first:
                pool.wait_ge(s_stored[par], 32 * i)
            pool.tensor_tensor(hi[:, par, :], raw[:, par, :], one[:].to_broadcast([P, CUT]), ALU.mult).then_inc(s_hi, 1)
            pool.wait_ge(s_hi, n + 2)
            pool.tensor_tensor(lo[:, par, :], raw[:, par, :], hi[:, par, :].bitcast(F32), ALU.subtract).then_inc(s_lo, 1)
            pool.wait_ge(s_lo, n + 1)
            pool.sem_inc(s_own, 1)
            for part, dst in ((hi, hi_dram), (lo, lo_dram)):
                pool.dma_start(dst[bass.ds(n, 1)].rearrange("o p c -> p (o c)"), part[:, par, :].bitcast(F32)).then_inc(s_stored[par], 16)

        load(0, 0)
        split(0, 0, 0, first=True)
        split(1, 1, 0, first=True)
        with pool.Fori(1, n_cut // 2) as i:
            split(2 * i, 0, i)
            split(2 * i + 1, 1, i)
        split(n_cut - 1, 0, n_cut // 2, last=True)
        pool.wait_ge(s_stored[0], 32 * (n_cut // 2 + 1))
        pool.wait_ge(s_stored[1], 32 * (n_cut // 2))
    return program


def ffn_swiglu(nc, a, res, ident, dram, s_soft):
    with ExitStack() as ctx:
        k = Kit(nc, ctx, "ffn1")
        first, second = k.sb("first", [P, NT]), k.sb("second", [P, NT])
        weights_due, weights_at = k.sb("weights_due", [1, TILES], I32), k.sb("weights_at", [1, TILES], I32)
        load_plan = k.sb("load_plan", [1, 2, E1N], I32)
        with ExitStack() as ctx1:
            k1 = Kit(nc, ctx1, "ffn1s")
            xh, xl = k1.sb("xh", [P, KD, B * S], F32R), k1.sb("xl", [P, KD, B * S], F32R)
            hot = k1.sb("hot", [P, 2, NT, E1N])
            route(nc, a, res, ident, xh, xl, hot, first, second, dram)
            shared_expert(nc, res, ident, xh, xl, hot, weights_due, weights_at, load_plan, dram, s_soft)
        routed_experts(nc, ident, weights_due, weights_at, load_plan, dram, s_soft)
        combine(nc, a["out"], res, first, second, dram)


def route(nc, a, res, ident, xh, xl, hot, first, second, dram):
    with ExitStack() as ctx:
        k = Kit(nc, ctx, "ffn1a")
        turn, router = Turn(k, dram["rows"]), Router(k, a["wr1"], E1N, hot)
        bias = k.sb("bias", [P, E1N])
        none = k.sb("none", [P, D])
        s = {n: k.sem(n) for n in "raw hi wt bias share none filler".split()}
        router.weights_there = s["wt"], 2
        k.open()
        block = ctx.enter_context(nc.Block())

        @block.sync
        def _(sp):
            load_weights(sp, [router.w], s["raw"])
            sp.dma_start(bias[:], a["br1"].partition_broadcast(P)).then_inc(s["bias"], 16)

            def body(b, last):
                turn.store(sp, b)
            looped(sp, B, body)
            sp.wait_ge(s["none"], 2)
            sp.dma_start(dram["rows"][B * S:B * S + P, :], none[:]).then_inc(s["filler"], 16)
            sp.wait_ge(s["filler"], 17)
            sp.wait_ge(turn.s["stored"], 16 * B + 1)

        @block.gpsimd
        def _(pool):
            split_weights(pool, [router.w], s["raw"], s["hi"], s["wt"])
            router.pool_names(pool)
            pool.memset(none[:], 0.0).then_inc(s["none"], 1)

        @block.tensor
        def _(pe):
            pe.wait_ge(s["wt"], 2)
            turn.pe(pe, 0, ident)

            def body(b, last):
                pe.wait_ge(turn.s["xTl"], KD * b + KD + 1)
                gh, gl = (x[:, :, bass.ds(b * S, S)] for x in (xh, xl))
                router.pe_logits(pe, b, gh, gl)
                if not last:
                    turn.pe(pe, b + 1, ident)
                router.pe_turn(pe, b, ident)
            looped(pe, B, body)

        @block.scalar
        def _(act):
            turn.norm.scalar(act)

            def body(b, last):
                turn.act_hi(act, b, xh)
                router.act_copy(act, b)
            looped(act, B, body)
            router.act_exp(act)

        @block.vector
        def _(dve):
            turn.norm.vector(dve, res)
            dve.wait_ge(s["bias"], 17)
            turn.dve_norm(dve, res, 0)

            def body(b, last):
                turn.dve_lo(dve, b, xh, xl)
                if not last:
                    turn.dve_norm(dve, res, b + 1)
                router.dve_logits(dve, b, bias)
            looped(dve, B, body)
            router.dve_pick(dve)
            dve.tensor_scalar(first[:], router.gap[:], 1.0, None, ALU.add).then_inc(s["share"], 1)
            dve.wait_ge(s["share"], 2)
            dve.reciprocal(first[:], first[:]).then_inc(s["share"], 1)
            dve.wait_ge(s["share"], 3)
            dve.tensor_tensor(second[:], router.gap[:], first[:], ALU.mult).then_inc(s["share"], 1)
            dve.wait_ge(s["share"], 4)


class Sort:

    PAD = NT // 2

    def __init__(self, k, hot, weights_due, weights_at, load_plan, dram, s_soft):
        self.hot, self.due, self.at, self.load_plan, self.dram, self.soft = hot, weights_due, weights_at, load_plan, dram, s_soft
        E = E1N
        self.tri_f, self.tri = k.sb("tri_f", [P, P]), k.sb("tri", [P, P], F32R)
        self.all_f, self.all = k.sb("all_f", [P, P]), k.sb("all", [P, P], F32R)
        self.both = k.sb("both", [P, NT, E], F32R)
        self.run = k.sb("run", [P, 2, self.PAD + NT, E])
        self.thresholds = k.sb("thresholds", [P, NT])
        self.above = k.sb("above", [P, E, NT])
        self.size = k.sb("size", [P, 2, E])
        self.ends = k.sb("ends", [P, 2, 2, E // 2 + E])
        self.base = k.sb("base", [P, E])
        self.slot = k.sb("slot", [P, NT, E])
        self.mine = k.sb("mine", [P, 2, NT, E])
        self.slotf = k.sb("slotf", [P, 2, NT])
        self.sloti = k.sb("sloti", [P, 2, NT], I32)
        self.number = k.sb("number", [1, TILES])
        self.more = k.sb("more", [1, 2, E])
        self.past = k.sb("past", [1, 2, TILES, E])
        self.order = k.sb("order", [1, TILES])
        self.rounds = k.sb("rounds", [1, 2, TILES])
        self.which = k.sb("which", [1, 2, TILES])
        self.after, self.none = k.sb("after", [1, E]), k.sb("none", [1, E])
        self.pick = k.sb("pick", [1, 3, E, E])
        self.plan = k.sb("plan", [1, 2, E])
        self.entry = k.sb("entry", [P, NT, 2, 2], I32)
        self.filler = k.sb("filler", [P, TILES, 2], I32)
        self.ps = k.ps("psS", [P, 2, NT * E])
        names = "fixed parts both ranked sorted ready slots filled entered".split()
        self.s = {n: k.sem("sort_" + n) for n in names}

    def pool_constants(self, pool):
        s, E = self.s, E1N
        pool.iota(self.filler[:, :, 0], [[0, TILES]], base=B * S, channel_multiplier=1).then_inc(s["filled"], 1)
        pool.iota(self.filler[:, :, 1], [[P, TILES]], base=2 * B * S, channel_multiplier=1).then_inc(s["filled"], 1)
        pool.memset(self.tri_f[:], 1.0).then_inc(s["fixed"], 1)
        pool.memset(self.all_f[:], 1.0).then_inc(s["fixed"], 1)
        pool.wait_ge(s["fixed"], 3)
        pool.affine_select(out=self.tri_f[:], in_=self.tri_f[:], compare_op=ALU.is_gt, fill=0.0, base=0,
                           pattern=[[1, P]], channel_multiplier=-1).then_inc(s["fixed"], 1)
        pool.wait_ge(s["fixed"], 4)
        pool.tensor_copy(self.tri[:], self.tri_f[:]).then_inc(s["fixed"], 1)
        pool.tensor_copy(self.all[:], self.all_f[:]).then_inc(s["fixed"], 1)
        for n in range(2):
            pool.memset(self.run[:, n, 0:self.PAD, :], 0.0).then_inc(s["parts"], 1)
            pool.memset(self.ends[:, n, :, 0:E // 2], 0.0).then_inc(s["parts"], 1)
        pool.iota(self.thresholds[:], [[P, NT]], base=0, channel_multiplier=0,
                  allow_small_or_imprecise_dtypes=True).then_inc(s["parts"], 1)
        pool.iota(self.number[:], [[1, TILES]], base=0, channel_multiplier=0,
                  allow_small_or_imprecise_dtypes=True).then_inc(s["parts"], 1)
        pool.iota(self.entry[:, :, :, 0], [[P, NT], [0, 2]], base=0, channel_multiplier=1).then_inc(s["parts"], 1)
        pool.iota(self.entry[:, :, :, 1], [[P, NT], [B * S, 2]], base=0, channel_multiplier=1).then_inc(s["parts"], 1)
        pool.wait_ge(s["parts"], 9)

    def sync_fill(self, sp):
        sp.wait_ge(self.s["filled"], 3)
        sp.dma_start(self.dram["table"].rearrange("(m p) c -> p m c", p=P), self.filler[:]).then_inc(self.s["entered"], 16)

    def pool_scatter(self, pool):
        pool.wait_ge(self.s["slots"], 2)
        pool.wait_ge(self.s["entered"], 17)
        for t in range(NT):
            for n in range(2):
                pool.indirect_dma_start(out=self.dram["table"], in_=self.entry[:, t, n, :], in_offset=None,
                                        out_offset=bass.IndirectOffsetOnAxis(ap=self.sloti[:, n, t:t + 1], axis=0)
                                        ).then_inc(self.soft["entries"], 16)
        pool.wait_ge(self.soft["entries"], 16 * 2 * NT)

    def pe_rank(self, pe):
        pe.wait_ge(self.s["fixed"], 6)
        pe.wait_ge(self.s["both"], 2)
        both = self.both[:].rearrange("p t e -> p (t e)")
        pe.matmul(self.ps[:, 0, :], self.tri[:], both, start=True, stop=True)
        pe.matmul(self.ps[:, 1, :], self.all[:], both, start=True, stop=True).then_inc(self.s["ranked"], 1)

    def dve(self, dve):
        s, E, pad = self.s, E1N, self.PAD
        dve.wait_ge(s["parts"], 9)
        dve.tensor_tensor(self.both[:], self.hot[:, 0], self.hot[:, 1], ALU.add).then_inc(s["both"], 1)
        dve.wait_ge(s["ranked"], 2)
        rank, total = (self.ps[:, n, :].rearrange("p (t e) -> p t e", e=E) for n in range(2))
        dve.tensor_copy(self.run[:, 0, pad:, :], total).then_inc(s["sorted"], 1)
        n = 1
        for step in (1, 2, 4, 8, 16):
            src, dst = self.run[:, (n - 1) % 2], self.run[:, n % 2]
            dve.wait_ge(s["sorted"], n + 1)
            dve.tensor_tensor(dst[:, pad:, :], src[:, pad:, :], src[:, pad - step:pad - step + NT, :], ALU.add
                              ).then_inc(s["sorted"], 1)
            n += 1
        run = self.run[:, (n - 1) % 2]
        dve.wait_ge(s["sorted"], n + 1)
        dve.tensor_tensor(self.above[:], run[:, pad + NT - 1, :].unsqueeze(2).to_broadcast([P, E, NT]),
                          self.thresholds[:].unsqueeze(1).to_broadcast([P, E, NT]), ALU.is_gt).then_inc(s["sorted"], 1)
        dve.tensor_tensor(self.slot[:], rank, run[:, pad - 1:pad - 1 + NT, :], ALU.add).then_inc(s["sorted"], 1)
        dve.wait_ge(s["sorted"], n + 3)
        dve.tensor_reduce(self.size[:, 0, :], self.above[:], AX.X, ALU.add).then_inc(s["sorted"], 1)
        dve.tensor_copy(self.size[:, 1, :], self.above[:, :, 0]).then_inc(s["sorted"], 1)
        dve.wait_ge(s["sorted"], n + 5)
        dve.tensor_copy(self.ends[:, 0, :, E // 2:], self.size[:]).then_inc(s["sorted"], 1)
        n += 5
        for q, step in enumerate((1, 2, 4)):
            src, dst = self.ends[:, q % 2], self.ends[:, 1 - q % 2]
            dve.wait_ge(s["sorted"], n + 1)
            dve.tensor_tensor(dst[:, :, E // 2:], src[:, :, E // 2:], src[:, :, E // 2 - step:E // 2 - step + E], ALU.add
                              ).then_inc(s["sorted"], 1)
            n += 1
        ends = self.ends[:, 1, 0]
        dve.wait_ge(s["sorted"], n + 1)
        dve.tensor_scalar(self.base[:], ends[:, E // 2 - 1:E // 2 - 1 + E], float(P), None, ALU.mult
                          ).then_inc(s["sorted"], 1)
        dve.wait_ge(s["sorted"], n + 2)
        dve.tensor_tensor(self.slot[:], self.slot[:], self.base[:].unsqueeze(1).to_broadcast([P, NT, E]), ALU.add
                          ).then_inc(s["sorted"], 1)
        dve.wait_ge(s["sorted"], n + 3)
        for c in range(2):
            dve.tensor_tensor(self.mine[:, c], self.slot[:], self.hot[:, c], ALU.mult).then_inc(s["sorted"], 1)
        dve.wait_ge(s["sorted"], n + 5)
        dve.tensor_reduce(self.slotf[:], self.mine[:], AX.X, ALU.add).then_inc(s["sorted"], 1)
        dve.wait_ge(s["sorted"], n + 6)
        dve.tensor_copy(self.sloti[:], self.slotf[:]).then_inc(s["slots"], 1)
        self.dve_plan(dve, n + 5)

    def dve_plan(self, dve, n):
        s, E = self.s, E1N
        ends, rank = self.ends[0:1, 1, 0, E // 2:], self.ends[0:1, 1, 1, E // 2:]
        before = self.ends[0:1, 1, 1, E // 2 - 1:E // 2 - 1 + E]

        def over(x, m):
            return x.unsqueeze(1).to_broadcast([1, m, E])

        def numbers(m):
            return self.number[:, 0:m].unsqueeze(2).to_broadcast([1, m, E])

        dve.tensor_tensor(self.more[:, 0], ends, self.ends[0:1, 1, 0, E // 2 + E - 1:].to_broadcast([1, E]), ALU.is_lt
                          ).then_inc(s["sorted"], 1)
        dve.tensor_scalar(self.after[:], before, 3.0, None, ALU.add).then_inc(s["sorted"], 1)
        dve.tensor_tensor(self.past[:, 0], over(ends, TILES), numbers(TILES), ALU.is_le).then_inc(s["sorted"], 1)
        dve.tensor_tensor(self.pick[:, 0], over(rank, E), numbers(E), ALU.is_le).then_inc(s["sorted"], 1)
        dve.tensor_tensor(self.none[:], self.ends[0:1, 1, 1, E // 2 + E - 1:].to_broadcast([1, E]), self.number[:, 0:E],
                          ALU.is_le).then_inc(s["sorted"], 1)
        n += 1
        dve.wait_ge(s["sorted"], n + 5)
        dve.tensor_tensor(self.more[:, 1], self.more[:, 0], self.size[0:1, 1, :], ALU.mult).then_inc(s["sorted"], 1)
        dve.tensor_tensor(self.pick[:, 1], over(self.after[:], E), numbers(E), ALU.is_le).then_inc(s["sorted"], 1)
        dve.tensor_reduce(self.plan[:, 0], self.pick[:, 0], AX.X, ALU.add).then_inc(s["sorted"], 1)
        dve.wait_ge(s["sorted"], n + 8)
        dve.tensor_tensor(self.past[:, 1], self.past[:, 0], over(self.more[:, 1], TILES), ALU.mult).then_inc(s["sorted"], 1)
        dve.tensor_tensor(self.pick[:, 2], self.pick[:, 1], over(self.size[0:1, 0, :], E), ALU.mult).then_inc(s["sorted"], 1)
        dve.tensor_scalar(self.plan[:, 0], self.plan[:, 0], float(E - 1), None, ALU.min).then_inc(s["sorted"], 1)
        dve.wait_ge(s["sorted"], n + 11)
        dve.tensor_reduce(self.order[:], self.past[:, 1], AX.X, ALU.add).then_inc(s["sorted"], 1)
        dve.tensor_reduce(self.plan[:, 1], self.pick[:, 2], AX.X, ALU.add).then_inc(s["sorted"], 1)
        dve.wait_ge(s["sorted"], n + 13)
        dve.scalar_tensor_tensor(self.plan[:, 1], self.none[:], float(TILES), self.plan[:, 1], ALU.mult, ALU.add
                                 ).then_inc(s["sorted"], 1)
        n += 1
        dve.wait_ge(s["sorted"], n + 13)
        dve.tensor_scalar(self.which[:, 0], self.order[:], 32.0, 33.0, ALU.mult, ALU.add).then_inc(s["sorted"], 1)
        for q in range(2):
            dve.tensor_scalar(self.rounds[:, q], self.order[:], 3.0 * q + 3.0, 3.0, ALU.is_ge, ALU.mult).then_inc(s["sorted"], 1)
        dve.tensor_scalar(self.plan[:, 1], self.plan[:, 1], float(TILES), 2.0, ALU.min, ALU.add).then_inc(s["sorted"], 1)
        dve.wait_ge(s["sorted"], n + 17)
        dve.tensor_tensor(self.which[:, 1], self.order[:], self.rounds[:, 0], ALU.subtract).then_inc(s["sorted"], 1)
        dve.wait_ge(s["sorted"], n + 18)
        dve.tensor_tensor(self.which[:, 1], self.which[:, 1], self.rounds[:, 1], ALU.subtract).then_inc(s["sorted"], 1)
        dve.wait_ge(s["sorted"], n + 19)
        dve.tensor_copy(self.due[:], self.which[:, 0]).then_inc(s["ready"], 1)
        dve.tensor_copy(self.at[:], self.which[:, 1]).then_inc(s["ready"], 1)
        dve.tensor_copy(self.load_plan[:], self.plan[:]).then_inc(s["ready"], 1)
        dve.wait_ge(s["ready"], 4)


def shared_expert(nc, res, ident, xh, xl, hot, weights_due, weights_at, load_plan, dram, s_soft):
    TT = 256
    NTT = B * S // TT
    with ExitStack() as ctx:
        k = Kit(nc, ctx, "ffn1b")
        sort = Sort(k, hot, weights_due, weights_at, load_plan, dram, s_soft)
        w_h, w_l = k.sb("w_h", [P, WCOLS], F32R), k.sb("w_l", [P, WCOLS], F32R)
        w13 = [w[:, 0:2 * KD * F1].rearrange("p (g k f) -> p g k f", g=2, k=KD) for w in (w_h, w_l)]
        w2 = [w[:, 2 * KD * F1:].rearrange("p (h d) -> p h d", d=D) for w in (w_h, w_l)]
        sil = k.sb("sil", [P, 2, TT])
        act_f = k.sb("act_f", [P, 2, TT])
        act_h, act_l = k.sb("act_h", [P, 2, HB, TT], F32R), k.sb("act_l", [P, 2, HB, TT], F32R)
        psG = k.ps("psG", [P, 2, 2, 512])
        psY = k.ps("psY", [P, 2, 512])
        s = {n: k.sem(n) for n in "wt gate sil act acth actl y res".split()}
        k.open([(s["act"], 1), (s["actl"], 1), (s["y"], 1), (s["res"], 2)])
        block = ctx.enter_context(nc.Block())

        @block.sync
        def _(sp):
            sort.sync_fill(sp)
            for dst, src in ((w_h, dram["w_hi"]), (w_l, dram["w_lo"])):
                per = WCOLS // CUT
                sp.dma_start(dst[:].bitcast(F32).rearrange("p (n c) -> p n c", n=per),
                             src[E1N * per:(E1N + 1) * per].rearrange("n p c -> p n c")).then_inc(s["wt"], 16)

        @block.gpsimd
        def _(pool):
            sort.pool_constants(pool)
            sort.pool_scatter(pool)

        @block.tensor
        def _(pe):
            def hidden(i, ip):
                for hb in range(HB):
                    n = HB * i + hb
                    pe.wait_ge(s["act"], n + 1)
                    cols = slice(P * hb, P * (hb + 1))
                    for g in range(2):
                        q = 0
                        for w, x in split_passes(w13[0], w13[1], xh, xl):
                            for c in range(KD):
                                mm = pe.matmul(psG[:, hb % 2, g, 0:TT], w[:, g, c, cols],
                                               x[:, c, bass.ds(i * TT, TT)], start=(q == 0), stop=(q == 5))
                                q += 1
                        mm.then_inc(s["gate"], 1)

            def down(i, ip):
                pe.wait_ge(s["actl"], HB * i + HB + 2)
                pe.wait_ge(s["res"], 2 * i + 1)
                for t in range(2):
                    q = 0
                    for x, w in split_passes(act_h, act_l, w2[0], w2[1]):
                        for hb in range(HB):
                            mm = pe.matmul(psY[:, ip, D * t:D * (t + 1)], x[:, ip, hb, P * t:P * (t + 1)],
                                           w[:, hb, :], start=(q == 0), stop=(q == 3 * HB - 1))
                            q += 1
                mm.then_inc(s["y"], 1)

            sort.pe_rank(pe)
            pe.wait_ge(s["wt"], 33)
            hidden(0, 0)
            with pe.Fori(0, NTT // 2 - 1) as i:
                hidden(2 * i + 1, 1)
                down(2 * i, 0)
                hidden(2 * i + 2, 0)
                down(2 * i + 1, 1)
            hidden(NTT - 1, 1)
            down(NTT - 2, 0)
            down(NTT - 1, 1)

        @block.scalar
        def _(act):
            with act.Fori(0, NTT // 2) as j:
                for ip in range(2):
                    i = 2 * j + ip
                    for hb in range(HB):
                        n = HB * i + hb
                        act.wait_ge(s["gate"], 2 * n + 2)
                        act.wait_ge(s["act"], n + 1)
                        act.activation(sil[:, hb % 2, :], psG[:, hb % 2, 0, 0:TT], ACT.Silu).then_inc(s["sil"], 1)
                        act.wait_ge(s["act"], n + 3)
                        if hb == 0:
                            act.wait_ge(s["y"], i + 1)
                        act.copy(act_h[:, ip, hb, :], act_f[:, hb % 2, :]).then_inc(s["acth"], 1)

        @block.vector
        def _(dve):
            def gated(i, ip):
                def low(hb):
                    dve.wait_ge(s["acth"], HB * i + hb + 2)
                    dve.tensor_tensor(act_l[:, ip, hb, :], act_f[:, hb % 2, :], act_h[:, ip, hb, :].bitcast(F32),
                                      ALU.subtract).then_inc(s["actl"], 1)

                for hb in range(HB):
                    n = HB * i + hb
                    dve.wait_ge(s["gate"], 2 * n + 3)
                    dve.wait_ge(s["sil"], n + 2)
                    dve.wait_ge(s["actl"], n + 1)
                    dve.tensor_tensor(act_f[:, hb % 2, :], psG[:, hb % 2, 1, 0:TT], sil[:, hb % 2, :], ALU.mult
                                      ).then_inc(s["act"], 1)
                    if hb:
                        low(hb - 1)
                low(HB - 1)

            def add(i, ip):
                dve.wait_ge(s["y"], i + 3)
                r = res[:, bass.ds(2 * i, 2), :]
                dve.tensor_tensor(r, r, psY[:, ip, :].rearrange("p (t d) -> p t d", d=D), ALU.add).then_inc(s["res"], 2)

            sort.dve(dve)
            gated(0, 0)
            with dve.Fori(0, NTT // 2 - 1) as i:
                gated(2 * i + 1, 1)
                add(2 * i, 0)
                gated(2 * i + 2, 0)
                add(2 * i + 1, 1)
            gated(NTT - 1, 1)
            add(NTT - 2, 0)
            add(NTT - 1, 1)
            dve.wait_ge(s["res"], 2 * NTT + 3)


class Step:

    def __init__(self, i, n):
        self.i, self.n = i, n
        self.value = 4 * i + n
        self.buf, self.par = n % 4, n % 2
        self.before = i + n // 4

    def __add__(self, d):
        return Step(self.i, self.n + d)

    def __sub__(self, d):
        return self + -d

    def exists(self):
        return not isinstance(self.value, int) or 0 <= self.value < TILES

    def first(self):
        return isinstance(self.value, int) and self.value < 4


def step_walk(eng, stage):
    for n in range(4):
        stage(Step(0, n))
    with eng.Fori(1, TILES // 4 - 1) as i:
        for n in range(4):
            stage(Step(i, n))
    for n in range(TILES - 4, TILES + 3):
        stage(Step(0, n))


def routed_experts(nc, ident, weights_due, weights_at, load_plan, dram, s_soft):
    assert TILES % 4 == 0
    with ExitStack() as ctx:
        k = Kit(nc, ctx, "ffn1c")
        table = k.sb("table", [P, TILES, 2], I32)
        take, put = k.sb("take", [P, 4], I32), k.sb("put", [P, 4], I32)
        rows = k.sb("rows", [P, 4, D])
        w_h, w_l = k.sb("w_h", [P, 3, WCOLS], F32R), k.sb("w_l", [P, 3, WCOLS], F32R)
        xh, xl = k.sb("xh", [P, 2, D], F32R), k.sb("xl", [P, 2, D], F32R)
        sil, hid = k.sb("sil", [P, 2, F1]), k.sb("hid", [P, 2, F1])
        hh, hl = k.sb("hh", [P, 2, F1], F32R), k.sb("hl", [P, 2, F1], F32R)
        y = k.sb("y", [P, 4, D])
        psG = k.ps("psG", [P, 2, 2, F1])
        psX, psH, psY = (k.ps(n, [P, 512]) for n in ("psX", "psH", "psY"))
        s = {n: k.sem(n) for n in "table took puts own w xT xTh xTl gate sil act hT hTh hTl y ys".split()}
        k.open([(s["act"], 1), (s["gate"], 2), (s["y"], 1), (s["hT"], 1)])
        block = ctx.enter_context(nc.Block())
        got, placed = s_soft["got"], s_soft["placed"]

        @block.sync
        def _(sp):
            sp.dma_start(table[:], dram["table"].rearrange("(m p) c -> p m c", p=P)).then_inc(s["table"], 16)
            per = WCOLS // CUT
            for n in range(E1N):
                expert = sp.value_load(load_plan[0:1, 0, n:n + 1], min_val=0, max_val=E1N - 1)
                if n:
                    sp.wait_ge(s["w"], 32 * n + 1)
                if n >= 3:
                    through = sp.value_load(load_plan[0:1, 1, n:n + 1], min_val=2, max_val=TILES + 2)
                    sp.wait_ge(s["y"], through)
                for dst, src in ((w_h, dram["w_hi"]), (w_l, dram["w_lo"])):
                    sp.dma_start(dst[:, n % 3, :].bitcast(F32).rearrange("p (n c) -> p n c", n=per),
                                 src[bass.ds(expert * per, per)].rearrange("n p c -> p n c")).then_inc(s["w"], 16)
            sp.wait_ge(s["w"], 32 * E1N + 1)

        @block.gpsimd
        def _(pool):
            def gather(t):
                if not t.exists():
                    return
                if not t.first():
                    pool.wait_ge(s["xT"], (t - 4).value + 2)
                pool.sem_inc(s["own"], 1)
                pool.tensor_copy(take[:, t.buf:t.buf + 1], table[:, bass.ds(t.value, 1), 0]).then_inc(s["took"], 1)
                pool.wait_ge(s["took"], t.value + 2)
                pool.sem_inc(s["own"], 1)
                pool.indirect_dma_start(out=rows[:, t.buf, :], out_offset=None, in_=dram["rows"],
                                        in_offset=bass.IndirectOffsetOnAxis(ap=take[:, t.buf:t.buf + 1], axis=0)
                                        ).then_inc(got[t.buf], 16)

            def scatter(t):
                if not t.exists():
                    return
                pool.wait_ge(s["ys"], t.value + 2)
                if not t.first():
                    pool.wait_ge(placed[t.buf], 16 * t.before)
                pool.sem_inc(s["own"], 1)
                pool.tensor_copy(put[:, t.buf:t.buf + 1], table[:, bass.ds(t.value, 1), 1]).then_inc(s["puts"], 1)
                pool.wait_ge(s["puts"], t.value + 2)
                pool.sem_inc(s["own"], 1)
                pool.indirect_dma_start(out=dram["outputs"], in_=y[:, t.buf, :], in_offset=None,
                                        out_offset=bass.IndirectOffsetOnAxis(ap=put[:, t.buf:t.buf + 1], axis=0)
                                        ).then_inc(placed[t.buf], 16)

            def stage(t):
                gather(t + 3)
                scatter(t - 2)

            pool.wait_ge(s["table"], 17)
            for n in range(3):
                gather(Step(0, n))
            step_walk(pool, stage)
            for n in range(4):
                pool.wait_ge(placed[n], 16 * (TILES // 4))

        @block.tensor
        def _(pe):
            def turn_rows(t):
                if not t.exists():
                    return
                pe.wait_ge(got[t.buf], 16 * t.before + 16)
                pe.wait_ge(s["xTl"], t.value + 1)
                for c in range(KD):
                    mm = pe.transpose(psX[:, P * c:P * (c + 1)], rows[:, t.buf, P * c:P * (c + 1)], ident[:])
                mm.then_inc(s["xT"], 1)

            def hidden(t):
                if not t.exists():
                    return
                at = pe.value_load(weights_at[0:1, bass.ds(t.value, 1)], min_val=0, max_val=2)
                due = pe.value_load(weights_due[0:1, bass.ds(t.value, 1)], min_val=33, max_val=32 * E1N + 1)
                pe.wait_ge(s["xTl"], t.value + 2)
                pe.wait_ge(s["act"], t.value + 1)
                pe.wait_ge(s["w"], due)
                for g in range(2):
                    q = 0
                    for x, w in split_passes(xh, xl, w_h, w_l):
                        for c in range(KD):
                            col = (g * KD + c) * F1
                            mm = pe.matmul(psG[:, t.par, g, :], x[:, t.par, P * c:P * (c + 1)],
                                           w[:, bass.ds(at, 1), col:col + F1], start=(q == 0), stop=(q == 5))
                            q += 1
                    mm.then_inc(s["gate"], 1)

            def turn_hidden(t):
                if not t.exists():
                    return
                pe.wait_ge(s["act"], t.value + 3)
                pe.wait_ge(s["hTl"], t.value + 1)
                for c in range(HB):
                    mm = pe.transpose(psH[:, P * c:P * (c + 1)], hid[:, t.par, P * c:P * (c + 1)], ident[:])
                mm.then_inc(s["hT"], 1)

            def output(t):
                if not t.exists():
                    return
                at = pe.value_load(weights_at[0:1, bass.ds(t.value, 1)], min_val=0, max_val=2)
                pe.wait_ge(s["hTl"], t.value + 2)
                pe.wait_ge(s["ys"], t.value + 1)
                q = 0
                for x, w in split_passes(hh, hl, w_h, w_l):
                    for c in range(HB):
                        col = 2 * KD * F1 + c * D
                        mm = pe.matmul(psY[:, 0:D], x[:, t.par, P * c:P * (c + 1)],
                                       w[:, bass.ds(at, 1), col:col + D], start=(q == 0), stop=(q == 3 * HB - 1))
                        q += 1
                mm.then_inc(s["y"], 1)

            def stage(t):
                turn_rows(t + 1)
                hidden(t)
                turn_hidden(t - 1)
                output(t - 2)

            turn_rows(Step(0, 0))
            step_walk(pe, stage)

        @block.scalar
        def _(act):
            def high_rows(t):
                if not t.exists():
                    return
                act.wait_ge(s["xT"], t.value + 2)
                act.wait_ge(s["gate"], 2 * t.value + 1)
                act.copy(xh[:, t.par, :], psX[:, 0:D]).then_inc(s["xTh"], 1)

            def silu(t):
                if not t.exists():
                    return
                act.wait_ge(s["gate"], 2 * t.value + 4)
                act.wait_ge(s["act"], t.value + 1)
                act.activation(sil[:, t.par, :], psG[:, t.par, 0, :], ACT.Silu).then_inc(s["sil"], 1)

            def high_hidden(t):
                if not t.exists():
                    return
                act.wait_ge(s["hT"], t.value + 3)
                act.wait_ge(s["y"], t.value + 1)
                act.copy(hh[:, t.par, :], psH[:]).then_inc(s["hTh"], 1)

            def output(t):
                if not t.exists():
                    return
                act.wait_ge(s["y"], t.value + 3)
                if not t.first():
                    act.wait_ge(placed[t.buf], 16 * t.before)
                act.copy(y[:, t.buf, :], psY[:, 0:D]).then_inc(s["ys"], 1)

            def stage(t):
                high_rows(t + 1)
                silu(t)
                high_hidden(t - 1)
                output(t - 2)

            high_rows(Step(0, 0))
            step_walk(act, stage)

        @block.vector
        def _(dve):
            def low_rows(t):
                if not t.exists():
                    return
                dve.wait_ge(s["xTh"], t.value + 2)
                dve.tensor_tensor(xl[:, t.par, :], psX[:, 0:D], xh[:, t.par, :].bitcast(F32), ALU.subtract
                                  ).then_inc(s["xTl"], 1)

            def gated(t):
                if not t.exists():
                    return
                dve.wait_ge(s["gate"], 2 * t.value + 5)
                dve.wait_ge(s["sil"], t.value + 2)
                dve.wait_ge(s["hT"], t.value + 1)
                dve.tensor_tensor(hid[:, t.par, :], psG[:, t.par, 1, :], sil[:, t.par, :], ALU.mult
                                  ).then_inc(s["act"], 1)

            def low_hidden(t):
                if not t.exists():
                    return
                dve.wait_ge(s["hTh"], t.value + 2)
                dve.tensor_tensor(hl[:, t.par, :], psH[:], hh[:, t.par, :].bitcast(F32), ALU.subtract
                                  ).then_inc(s["hTl"], 1)

            def stage(t):
                low_rows(t + 1)
                gated(t)
                low_hidden(t - 1)

            low_rows(Step(0, 0))
            step_walk(dve, stage)


def combine(nc, out, res, first, second, dram):
    with ExitStack() as ctx:
        k = Kit(nc, ctx, "ffn1d")
        rows = k.sb("rows", [P, 2, 2, TG, D])
        s = {n: k.sem(n) for n in ("first", "second")}
        s_in, s_out = [k.sem(f"in{n}") for n in range(2)], k.sem("out")
        block = ctx.enter_context(nc.Block())

        @block.sync
        def _(sp):
            for b in range(B):
                if b >= 2:
                    sp.wait_ge(s["second"], TG * (b - 1))
                for n in range(2):
                    r0 = B * S * n + S * b
                    sp.dma_start(rows[:, b % 2, n], dram["outputs"][r0:r0 + S, :].rearrange("(t p) d -> p t d", p=P)
                                 ).then_inc(s_in[b % 2], 16)

        @block.vector
        def _(dve):
            for b in range(B):
                dve.wait_ge(s_in[b % 2], 32 * (b // 2 + 1))
                for n, (w, done) in enumerate(((first, s["first"]), (second, s["second"]))):
                    for i in range(TG):
                        t = TG * b + i
                        if n:
                            dve.wait_ge(s["first"], t + 1)
                        dve.scalar_tensor_tensor(res[:, t, :], rows[:, b % 2, n, i, :], w[:, t:t + 1], res[:, t, :],
                                                 ALU.mult, ALU.add).then_inc(done, 1)

        @block.scalar
        def _(act):
            for b in range(B):
                act.wait_ge(s["second"], TG * (b + 1))
                act.dma_start(out[b].rearrange("(t p) d -> p t d", p=P), res[:, TG * b:TG * (b + 1), :]).then_inc(s_out, 16)
            act.wait_ge(s_out, 16 * B)
def second_ffn_space(nc, ctx):
    pieces = (E1N + 1) * WCOLS // CUT
    dram = dict(
        w_hi=nc.dram_tensor("experts_hi", (pieces, P, CUT), F32).ap(),
        w_lo=nc.dram_tensor("experts_lo", (pieces, P, CUT), F32).ap(),
        rows=nc.dram_tensor("normed_rows", (B * S + P, D), F32).ap(),
        table=nc.dram_tensor("slots", (TILES * P, 2), I32).ap(),
        outputs=nc.dram_tensor("expert_rows", (2 * B * S + TILES * P, D), F32).ap())
    sem = lambda name: ctx.enter_context(nc.semaphore(name))
    soft = dict(raw=[sem(f"piece_loaded{n}") for n in range(2)], stored=[sem(f"piece_stored{n}") for n in range(2)],
                entries=sem("entries"), got=[sem(f"rows_got{n}") for n in range(4)],
                placed=[sem(f"rows_placed{n}") for n in range(4)])
    return dram, soft


def tower(nc, a):
    Kit.used.clear()
    with ExitStack() as ctx:
        k = Kit(nc, ctx, "m")
        res = k.sb("res", [P, NT, D])
        ident = k.sb("ident", [P, P])
        s_id = k.sem("ident")
        s_rows = ctx.enter_context(nc.semaphore("gathered"))
        q_dram = nc.dram_tensor("q_parts", (B, H, KROWS, S), BF16).ap()
        k_dram = nc.dram_tensor("k_parts", (B, H, 3 * DK, S), BF16).ap()
        v_dram = nc.dram_tensor("v_rows", (B, S, H * VW), F32).ap()
        m_dram = nc.dram_tensor("maxima", (2, MROWS, HG * S), BF16).ap()
        dram, soft = second_ffn_space(nc, ctx)
        with nc.Block() as block:
            @block.gpsimd
            def _(pool):
                pool.memset(ident[:], 0.0).then_inc(s_id, 1)
                pool.wait_ge(s_id, 1)
                pool.affine_select(out=ident[:], in_=ident[:], compare_op=ALU.not_equal, fill=1.0, base=0,
                                   pattern=[[-1, P]], channel_multiplier=1).then_inc(s_id, 1)
                pool.wait_ge(s_id, 2)
        embed(nc, res, ident, s_rows, a["ids"], a["E1"], a["tok_w2t"], a["b2"], a["pos"])
        with nc.sbuf_tensor("attn0", [P, NT, D], F32) as attn:
            project_qkv(nc, "qkv0", res, ident, a["w_qk0"], a["w_v0"], None, (a["cos"], a["sin"]), None, None,
                    q_dram, k_dram, v_dram, None)
            attend(nc, "att0", None, q_dram, k_dram, v_dram, m_dram, ident, None, attn)
            project_out(nc, "out0", res, attn, ident, a["w_o0"], None)
        ffn_sq(nc, a, res, ident)
        Kit.used.remove(s_id)
        clear_semaphores(nc)
        with nc.sbuf_tensor("attn1", [P, NT, D], F32) as attn, nc.sbuf_tensor("gates", [P, NT, H], F32) as gates:
            project_qkv(nc, "qkv1", res, ident, a["w_qk1"], None, a["bqk"], None, a["w_g1"], a["bgate"],
                    q_dram, k_dram, v_dram, gates)
            with ExitStack() as ctx2:
                split = split_experts(nc, ctx2, "prep", a["w_all"], dram["w_hi"], dram["w_lo"],
                                      (soft["raw"], soft["stored"]))
                attend(nc, "att1", WINDOWS, q_dram, k_dram, v_dram, m_dram, ident, gates, attn, split)
            project_out(nc, "out1", res, attn, ident, a["w_o1"], a["bproj"])
        ffn_swiglu(nc, a, res, ident, dram, soft)


def host_layout(np, x, L0_tok_E1, L0_tok_W2, L0_tok_b2, L0_tok_pos_emb, L0_attn_W_Q, L0_attn_W_K, L0_attn_W_V,
                L0_attn_W_O, L0_ffn_Ws1, L0_ffn_Ws2, L0_ffn_W1, L0_ffn_W2, L0_ffn_Wr, L1_attn_Wqk, L1_attn_bqk,
                L1_attn_Wgate, L1_attn_bgate, L1_attn_Wproj, L1_attn_bproj, L1_ffn_router_w, L1_ffn_experts_bias,
                L1_ffn_w1, L1_ffn_w3, L1_ffn_w2, L1_ffn_sw1, L1_ffn_sw3, L1_ffn_sw2):
    c = np.ascontiguousarray

    def rows(w):
        return c(w.reshape(-1, P, w.shape[-1]).transpose(1, 0, 2))

    def pieces(w1, w3, w2, sw1, sw3, sw2):
        w13 = np.stack([np.concatenate([w1, sw1]), np.concatenate([w3, sw3])], 1)
        w13 = w13.reshape(E1N + 1, 2, KD, P, F1).transpose(0, 3, 1, 2, 4).reshape(E1N + 1, P, -1)
        w2 = np.concatenate([w2, sw2]).reshape(E1N + 1, HB, P, D).transpose(0, 2, 1, 3).reshape(E1N + 1, P, -1)
        return c(np.concatenate([w13, w2], 2).reshape(E1N + 1, P, -1, CUT).transpose(0, 2, 1, 3).reshape(-1, P, CUT))

    theta = (1.0 / np.float32(10000.0) ** (np.arange(0, DK, 2, dtype=np.float32) / np.float32(DK))).astype(np.float32)
    ang = np.outer(np.arange(S, dtype=np.float32), theta).astype(np.float32)
    cos, sin = np.cos(ang), np.sin(ang)
    place = lambda t: c(t.reshape(TG, P, DK).transpose(1, 0, 2).astype(np.float32))
    return dict(
        ids=c(x.reshape(NT, P).T), E1=L0_tok_E1, tok_w2t=c(L0_tok_W2.T), b2=L0_tok_b2, pos=L0_tok_pos_emb,
        cos=place(np.concatenate([cos, cos], 1)), sin=place(np.concatenate([-sin, sin], 1)),
        w_qk0=rows(np.concatenate([L0_attn_W_Q.T, L0_attn_W_K.T], 1)), w_v0=rows(L0_attn_W_V.T),
        w_o0=rows(L0_attn_W_O.T),
        ws1=rows(L0_ffn_Ws1), ws2=rows(L0_ffn_Ws2),
        wr0=rows(L0_ffn_Wr), w1_0=c(L0_ffn_W1.reshape(E0, KD, P, F0).transpose(0, 2, 1, 3)), w2_0=L0_ffn_W2,
        w_qk1=rows(L1_attn_Wqk), bqk=L1_attn_bqk, w_g1=rows(L1_attn_Wgate), bgate=L1_attn_bgate,
        w_o1=rows(L1_attn_Wproj), bproj=L1_attn_bproj,
        wr1=rows(L1_ffn_router_w.T), br1=L1_ffn_experts_bias,
        w_all=pieces(L1_ffn_w1, L1_ffn_w3, L1_ffn_w2, L1_ffn_sw1, L1_ffn_sw3, L1_ffn_sw2),
    )


def kernel(**inputs):
    import numpy as np
    import concourse.bacc as bacc
    from concourse.bass_utils import run_bass_kernel_spmd

    arrays = {f"in_{name}": np.ascontiguousarray(x) for name, x in host_layout(np, **inputs).items()}
    nc = bacc.Bacc("TRN2", target_bir_lowering=False, num_devices=1)
    a = {name[3:]: nc.dram_tensor(name, x.shape, mybir.dt.from_np(x.dtype), kind="ExternalInput").ap()
         for name, x in arrays.items()}
    a["out"] = nc.dram_tensor("out_0", (B, S, D), F32, kind="ExternalOutput").ap()
    tower(nc, a)
    r = run_bass_kernel_spmd(nc, [arrays], core_ids=[0])
    return r.results[0]["out_0"]
```
